# Optimizing a Trainium2 kernel written in Bass

```python
import numpy as np
import jax
import jax.numpy as jnp

def _softmax(x, axis=-1):
    return jax.nn.softmax(x, axis=axis)

def _gelu(x):
    return jax.nn.gelu(x, approximate=True)

def _silu(x):
    return jax.nn.silu(x)

def _sigmoid(x):
    return jax.nn.sigmoid(x)

def _layernorm(x, axis=-1, eps=1e-05):
    m = jnp.mean(x, axis=axis, keepdims=True)
    v = jnp.var(x, axis=axis, keepdims=True)
    return (x - m) / jnp.sqrt(v + eps)

def _scatter_add(tgt, idx, src, axis=0):
    return tgt.at[idx].add(src)

def _segment_sum(src, seg, n):
    return jax.ops.segment_sum(src, seg, n)
kernel_name = 'mk_recurrent_d2_jaxref_r8_580015'

def setup_inputs(seed: int=0):
    np.random.seed(seed)
    _w = jnp.asarray

    def _L0_attn_setup():
        import jax, jax.numpy as jnp
        import numpy as np
        HEADS = 16
        NUM_MEM_KV = 16
        SPARSE_TOPK = 8
        key = jax.random.key(seed)
        ks = jax.random.split(key, 10)
        b, n, dim = (2, 256, 128)
        h, dh = (HEADS, 64)
        inner = h * dh
        s = 0.02
        return {'x': jax.random.normal(ks[0], (b, n, dim), jnp.float32), 'Wq': jax.random.normal(ks[1], (dim, inner), jnp.float32) * s, 'Wk': jax.random.normal(ks[2], (dim, inner), jnp.float32) * s, 'Wv': jax.random.normal(ks[3], (dim, inner), jnp.float32) * s, 'pre_proj': jax.random.normal(ks[4], (h, h), jnp.float32), 'post_proj': jax.random.normal(ks[5], (h, h), jnp.float32), 'mem_k': jax.random.normal(ks[6], (h, NUM_MEM_KV, dh), jnp.float32), 'mem_v': jax.random.normal(ks[7], (h, NUM_MEM_KV, dh), jnp.float32), 'Wo': jax.random.normal(ks[8], (inner, dim), jnp.float32) * s, 'bo': jnp.zeros((dim,), jnp.float32)}
    _L0_attn_in = _L0_attn_setup()

    def _L0_ffn_setup():
        import jax, jax.numpy as jnp
        import numpy as np
        DIM = 128
        HID = 256
        OUT = 128
        NE = 8
        TOPK = 2

        def _xavier(key, shape):
            fan_in, fan_out = (shape[-2], shape[-1])
            lim = jnp.sqrt(6.0 / (fan_in + fan_out))
            return jax.random.uniform(key, shape, jnp.float32, -lim, lim)
        key = jax.random.key(seed)
        ks = jax.random.split(key, 8)
        X = jax.random.normal(ks[0], (4, 128, DIM), jnp.float32)
        W1 = _xavier(ks[1], (NE, DIM, HID))
        W3 = _xavier(ks[2], (NE, DIM, HID))
        W2 = _xavier(ks[3], (NE, HID, OUT))
        b1 = jnp.zeros((NE, HID), jnp.float32)
        b3 = jnp.zeros((NE, HID), jnp.float32)
        b2 = jnp.zeros((NE, OUT), jnp.float32)
        Wg = _xavier(ks[4], (DIM, NE))
        bg = jnp.zeros((NE,), jnp.float32)
        Wf = _xavier(ks[5], (OUT, OUT))
        bf = jnp.zeros((OUT,), jnp.float32)
        return {'X': X, 'W1': W1, 'b1': b1, 'W3': W3, 'b3': b3, 'W2': W2, 'b2': b2, 'Wg': Wg, 'bg': bg, 'Wf': Wf, 'bf': bf}
    _L0_ffn_in = _L0_ffn_setup()

    def _L1_attn_setup():
        import jax, jax.numpy as jnp
        import numpy as np
        NUM_HEADS = 1
        LN_EPS = 1e-05
        key = jax.random.key(seed)
        ks = jax.random.split(key, 4)
        B, L, D = (8, 512, 128)
        x = jax.random.normal(ks[0], (B, L, D), dtype=jnp.float32)
        qkv_w = jax.random.normal(ks[1], (3 * D, D), dtype=jnp.float32) * np.float32(np.sqrt(1.0 / D))
        qkv_b = jnp.zeros((3 * D,), dtype=jnp.float32)
        proj_w = jax.random.normal(ks[2], (D, D), dtype=jnp.float32) * np.float32(np.sqrt(1.0 / D))
        proj_b = jnp.zeros((D,), dtype=jnp.float32)
        return {'x': x, 'norm_w': jnp.ones((D,), dtype=jnp.float32), 'norm_b': jnp.zeros((D,), dtype=jnp.float32), 'qkv_w': qkv_w, 'qkv_b': qkv_b, 'proj_w': proj_w, 'proj_b': proj_b}
    _L1_attn_in = _L1_attn_setup()

    def _L1_ffn_setup():
        import jax, jax.numpy as jnp
        import numpy as np
        K = 2
        CAP_FACTOR = 1.25
        key = jax.random.key(seed)
        ks = jax.random.split(key, 6)
        B, T, C, H, E = (8, 256, 128, 512, 8)
        return {'x': jax.random.normal(ks[0], (B, T, C), dtype=jnp.float32), 'Wr': jax.random.normal(ks[1], (C, E), dtype=jnp.float32) * 0.02, 'W1': jax.random.normal(ks[2], (E, C, H), dtype=jnp.float32) * 0.02, 'b1': jax.random.normal(ks[3], (E, H), dtype=jnp.float32) * 0.02, 'W2': jax.random.normal(ks[4], (E, H, C), dtype=jnp.float32) * 0.02, 'b2': jax.random.normal(ks[5], (E, C), dtype=jnp.float32) * 0.02}
    _L1_ffn_in = _L1_ffn_setup()
    _d = {'L0_attn_x': _L0_attn_in['x'], 'L0_attn_Wq': _L0_attn_in['Wq'], 'L0_attn_Wk': _L0_attn_in['Wk'], 'L0_attn_Wv': _L0_attn_in['Wv'], 'L0_attn_pre_proj': _L0_attn_in['pre_proj'], 'L0_attn_post_proj': _L0_attn_in['post_proj'], 'L0_attn_mem_k': _L0_attn_in['mem_k'], 'L0_attn_mem_v': _L0_attn_in['mem_v'], 'L0_attn_Wo': _L0_attn_in['Wo'], 'L0_attn_bo': _L0_attn_in['bo'], 'L0_ffn_W1': _L0_ffn_in['W1'], 'L0_ffn_b1': _L0_ffn_in['b1'], 'L0_ffn_W3': _L0_ffn_in['W3'], 'L0_ffn_b3': _L0_ffn_in['b3'], 'L0_ffn_W2': _L0_ffn_in['W2'], 'L0_ffn_b2': _L0_ffn_in['b2'], 'L0_ffn_Wg': _L0_ffn_in['Wg'], 'L0_ffn_bg': _L0_ffn_in['bg'], 'L0_ffn_Wf': _L0_ffn_in['Wf'], 'L0_ffn_bf': _L0_ffn_in['bf'], 'L1_attn_norm_w': _L1_attn_in['norm_w'], 'L1_attn_norm_b': _L1_attn_in['norm_b'], 'L1_attn_qkv_w': _L1_attn_in['qkv_w'], 'L1_attn_qkv_b': _L1_attn_in['qkv_b'], 'L1_attn_proj_w': _L1_attn_in['proj_w'], 'L1_attn_proj_b': _L1_attn_in['proj_b'], 'L1_ffn_Wr': _L1_ffn_in['Wr'], 'L1_ffn_W1': _L1_ffn_in['W1'], 'L1_ffn_b1': _L1_ffn_in['b1'], 'L1_ffn_W2': _L1_ffn_in['W2'], 'L1_ffn_b2': _L1_ffn_in['b2']}
    _x0 = _d['L0_attn_x']
    _d['L0_attn_x'] = jax.random.normal(jax.random.fold_in(jax.random.key(seed), 1), (8, 512, 128), dtype=_x0.dtype)
    del _x0
    return _d

def reference(L0_attn_x, L0_attn_Wq, L0_attn_Wk, L0_attn_Wv, L0_attn_pre_proj, L0_attn_post_proj, L0_attn_mem_k, L0_attn_mem_v, L0_attn_Wo, L0_attn_bo, L0_ffn_W1, L0_ffn_b1, L0_ffn_W3, L0_ffn_b3, L0_ffn_W2, L0_ffn_b2, L0_ffn_Wg, L0_ffn_bg, L0_ffn_Wf, L0_ffn_bf, L1_attn_norm_w, L1_attn_norm_b, L1_attn_qkv_w, L1_attn_qkv_b, L1_attn_proj_w, L1_attn_proj_b, L1_ffn_Wr, L1_ffn_W1, L1_ffn_b1, L1_ffn_W2, L1_ffn_b2):

    def _L0_attn_ref(x, Wq, Wk, Wv, pre_proj, post_proj, mem_k, mem_v, Wo, bo):
        import jax, jax.numpy as jnp
        import numpy as np
        HEADS = 16
        NUM_MEM_KV = 16
        SPARSE_TOPK = 8
        b, n, dim = x.shape
        h = HEADS
        dh = Wq.shape[1] // h
        nm = mem_k.shape[1]
        scale = dh ** (-0.5)

        def split_heads(t):
            return t.reshape(b, -1, h, dh).transpose(0, 2, 1, 3)
        q = split_heads(x @ Wq)
        k = split_heads(x @ Wk)
        v = split_heads(x @ Wv)
        k = jnp.concatenate([jnp.broadcast_to(mem_k[None], (b, h, nm, dh)), k], axis=2)
        v = jnp.concatenate([jnp.broadcast_to(mem_v[None], (b, h, nm, dh)), v], axis=2)
        dots = jnp.einsum('bhid,bhjd->bhij', q, k) * scale
        mask_value = -jnp.finfo(dots.dtype).max
        dots = jnp.einsum('bhij,hk->bkij', dots, pre_proj)
        j = nm + n
        causal = jnp.arange(n)[:, None] < jnp.arange(j)[None, :] - nm
        dots = jnp.where(causal[None, None], mask_value, dots)
        top = jax.lax.top_k(dots, SPARSE_TOPK)[0]
        thresh = top[..., -1:]
        dots = jnp.where(dots < thresh, mask_value, dots)
        attn = jax.nn.softmax(dots, axis=-1)
        attn = jnp.einsum('bhij,hk->bkij', attn, post_proj)
        out = jnp.einsum('bhij,bhjd->bhid', attn, v)
        out = out.transpose(0, 2, 1, 3).reshape(b, n, h * dh)
        return out @ Wo + bo

    def _L0_ffn_ref(X, W1, b1, W3, b3, W2, b2, Wg, bg, Wf, bf):
        import jax, jax.numpy as jnp
        import numpy as np
        DIM = 128
        HID = 256
        OUT = 128
        NE = 8
        TOPK = 2

        def _xavier(key, shape):
            fan_in, fan_out = (shape[-2], shape[-1])
            lim = jnp.sqrt(6.0 / (fan_in + fan_out))
            return jax.random.uniform(key, shape, jnp.float32, -lim, lim)
        gating = jax.nn.softmax(X @ Wg + bg, axis=-1)
        top_k_indices = jnp.argsort(gating, axis=-1)[..., -TOPK:]
        h1 = jnp.einsum('bsd,edh->bseh', X, W1) + b1
        h3 = jnp.einsum('bsd,edh->bseh', X, W3) + b3
        h = jax.nn.silu(h1 * h3)
        expert_outputs = jnp.einsum('bseh,eho->bseo', h, W2) + b2
        topk_out = jnp.take_along_axis(expert_outputs, top_k_indices[..., None], axis=2)
        topk_w = jnp.take_along_axis(gating, top_k_indices, axis=-1)
        mixed = jnp.sum(topk_w[..., None] * topk_out, axis=2)
        return mixed @ Wf + bf

    def _L1_attn_ref(x, norm_w, norm_b, qkv_w, qkv_b, proj_w, proj_b):
        import jax, jax.numpy as jnp
        import numpy as np
        NUM_HEADS = 1
        LN_EPS = 1e-05
        B, L, D = x.shape
        H = NUM_HEADS
        mu = jnp.mean(x, axis=-1, keepdims=True)
        var = jnp.mean(jnp.square(x - mu), axis=-1, keepdims=True)
        h = (x - mu) / jnp.sqrt(var + LN_EPS) * norm_w + norm_b
        qkv = h @ qkv_w.T + qkv_b
        qkv = qkv.reshape(B * H, L // H, 3, D)
        q, k, v = (qkv[..., 0, :], qkv[..., 1, :], qkv[..., 2, :])
        scale = np.float32(1.0 / np.sqrt(L // H))
        w = jax.nn.softmax(jnp.einsum('ncq,nck->nqk', q, k * scale), axis=2)
        a = jnp.einsum('nqk,nck->ncq', w, v)
        a = a.reshape(B, L, D)
        return a @ proj_w.T + proj_b + x

    def _L1_ffn_ref(x, Wr, W1, b1, W2, b2):
        import jax, jax.numpy as jnp
        import numpy as np
        K = 2
        CAP_FACTOR = 1.25
        B, T, C = x.shape
        E = Wr.shape[1]
        capacity = int(T / E * CAP_FACTOR)
        probs = jax.nn.softmax(x @ Wr, axis=-1)
        topk_probs, topk_experts = jax.lax.top_k(probs, K)
        S = T * K
        e_flat = topk_experts.reshape(B, S)
        p_flat = topk_probs.reshape(B, S)
        x_rep = jnp.repeat(x, K, axis=1)
        onehot = jax.nn.one_hot(e_flat, E, dtype=jnp.int32)
        pos_all = jnp.cumsum(onehot, axis=1) - onehot
        pos = jnp.take_along_axis(pos_all, e_flat[..., None], axis=-1)[..., 0]
        keep = pos < capacity
        pos_c = jnp.minimum(pos, capacity - 1)
        b_idx = jnp.broadcast_to(jnp.arange(B)[:, None], (B, S))
        buf = jnp.zeros((E, B, capacity, C), dtype=x.dtype)
        buf = buf.at[e_flat, b_idx, pos_c].add(x_rep * keep[..., None].astype(x.dtype))
        h = jax.nn.relu(jnp.einsum('ebnc,ech->ebnh', buf, W1) + b1[:, None, None, :])
        y = jnp.einsum('ebnh,ehc->ebnc', h, W2) + b2[:, None, None, :]
        y_tok = y[e_flat, b_idx, pos_c]
        y_tok = y_tok * keep[..., None].astype(x.dtype) * p_flat[..., None]
        out = y_tok.reshape(B, T, K, C).sum(axis=2)
        return out
    x = L0_attn_x
    xn = _layernorm(x, axis=-1)
    s = _L0_attn_ref(xn, L0_attn_Wq, L0_attn_Wk, L0_attn_Wv, L0_attn_pre_proj, L0_attn_post_proj, L0_attn_mem_k, L0_attn_mem_v, L0_attn_Wo, L0_attn_bo)
    g = _silu(_L0_ffn_ref(xn, L0_ffn_W1, L0_ffn_b1, L0_ffn_W3, L0_ffn_b3, L0_ffn_W2, L0_ffn_b2, L0_ffn_Wg, L0_ffn_bg, L0_ffn_Wf, L0_ffn_bf))
    x = x + s * g
    xn = _layernorm(x, axis=-1)
    s = _L1_attn_ref(xn, L1_attn_norm_w, L1_attn_norm_b, L1_attn_qkv_w, L1_attn_qkv_b, L1_attn_proj_w, L1_attn_proj_b)
    g = _silu(_L1_ffn_ref(xn, L1_ffn_Wr, L1_ffn_W1, L1_ffn_b1, L1_ffn_W2, L1_ffn_b2))
    x = x + s * g
    return x

_drawn_inputs = setup_inputs


def setup_inputs(seed=0):
    import zlib

    import numpy as np

    out = dict(_drawn_inputs(seed))
    spreads = {'L0_attn_bo': (0.0, 0.587),
     'L0_ffn_b1': (0.0, 0.522),
     'L0_ffn_b3': (0.0, 0.525),
     'L0_ffn_b2': (0.0, 0.315),
     'L0_ffn_bg': (0.0, 0.499),
     'L0_ffn_bf': (0.0, 0.1),
     'L1_attn_norm_w': (1.0, 0.6),
     'L1_attn_norm_b': (0.0, 0.8),
     'L1_attn_qkv_b': (0.0, 0.8),
     'L1_attn_proj_b': (0.0, 0.8)}
    factors = {'L0_attn_Wk': 2.963,
     'L0_attn_Wv': 3.98,
     'L1_attn_qkv_w': 8.0,
     'L1_attn_proj_w': 8.0,
     'L1_ffn_Wr': 8.0,
     'L1_ffn_W1': 8.0,
     'L1_ffn_b1': 8.0,
     'L1_ffn_W2': 7.603,
     'L1_ffn_b2': 8.0}
    for name, (base, spread) in spreads.items():
        noise = np.random.default_rng([zlib.crc32(name.encode()), seed]).standard_normal(out[name].shape)
        drawn = base * np.exp(spread * noise) if base else spread * noise
        out[name] = jnp.asarray(drawn.astype(out[name].dtype))
    for name, factor in factors.items():
        out[name] = (out[name] * factor).astype(out[name].dtype)
    return out
```

```python
from contextlib import ExitStack

import numpy as np

import concourse.bass as bass
from concourse import mybir

F32 = mybir.dt.float32
BF16 = mybir.dt.bfloat16
ALU = mybir.AluOpType
ACT = mybir.ActivationFunctionType
AX = mybir.AxisListType

P = 128
B, T, C = 8, 512, 128
NT = T // P
H, DH, NM = 16, 64, 16
HC = H * DH // P
NIT = H // 2
E0, HID0 = 8, 256
E1, HID1 = 8, 512
HM1 = HID1 // P
CAP = int(T / E1 * 1.25)
EPS = 1e-5
MASKED = -3.3895313892515355e38
KEYS = NM + T
UNITS = 2 * NT
MISC = 10
assert E0 == NIT and C == P


class Signal:

    def __init__(self, sem, per_row, preset=0):
        self.sem, self.per_row, self.preset = sem, per_row, preset

    def at(self, b, n):
        return b * self.per_row + (n + self.preset)


def build(nc, x, Wq, Wk, Wv, pre, post, mem_k, mem_v, Wo, bo, W1, b1, W3, b3, W2, b2, Wg, bg, Wf, bf,
          norm_w, norm_b, qkv_w, qkv_b, proj_w, proj_b, Wr, V1, c1, V2, c2, out):
    with ExitStack() as ctx:
        def sb(name, shape, dt=F32):
            return ctx.enter_context(nc.sbuf_tensor(name, shape, dt))

        def ps(name, shape):
            return ctx.enter_context(nc.psum_tensor(name, shape, F32))

        def sem(name):
            return ctx.enter_context(nc.semaphore(name))

        sc = ps("sc", [P, 4, 512])
        tr = ps("tr", [P, 512])
        sa = ps("sa", [P, 512])
        mb = ps("mb", [P, 2, 512])

        x_next = sb("x_next", [P, NT, C])
        mt_all = sb("mt_all", [P, NIT + 1, 2, C])
        n_all = sb("n_all", [P, NIT, 2, C])
        g_all = sb("g_all", [P, NIT + 1, 2, NM])
        r_all = sb("r_all", [P, 2, C])
        w13_all = sb("w13_all", [P, E0 + 1, 2, HID0])
        w2f = sb("w2f", [P, E0, 2, C])
        b1c = sb("b1c", [P, E0, 2])
        b3c = sb("b3c", [P, E0, 2])
        b2f = sb("b2f", [E0 + 1, C])
        wg = sb("wg", [P, E0])
        bg_b = sb("bg_b", [P, E0])
        bo_row = sb("bo_row", [1, 1, C])
        ones_row = sb("ones_row", [1, P])
        v1_all = sb("v1_all", [P, E1, HID1])
        v2_all = sb("v2_all", [P, E1, HM1, C])
        c1c = sb("c1c", [P, E1, HM1])
        c2_b = sb("c2_b", [CAP, E1, C])
        qkvT = sb("qkvT", [P, 3, C])
        qk_bias = sb("qk_bias", [P, 2, C])
        v_bias = sb("v_bias", [P, 1])
        projT = sb("projT", [P, C])
        pb_b = sb("pb_b", [P, C])
        wr = sb("wr", [P, E1])
        ident = sb("ident", [P, P])
        ident_h = sb("ident_h", [P, P], BF16)
        causal = sb("causal", [P, P], BF16)
        before = sb("before", [P, P], BF16)
        ones_h = sb("ones_h", [P, P], BF16)
        slot_no = sb("slot_no", [P, CAP])
        ties0 = sb("ties0", [P, E0, E0])
        ties1 = sb("ties1", [P, E1, E1])
        neghalf = sb("neghalf", [P, NT])

        arena = sb("arena", [P, 10240])
        wq_raw, wk_raw, wv_raw = (v1_all[:, 2 * i:2 * i + 2, :].rearrange("p a n -> p (a n)") for i in range(3))
        wo_sb = arena[:, 0:1024].rearrange("p (c n) -> p c n", c=HC)
        wqT = arena[:, 1024:2048].rearrange("p (c n) -> p c n", c=HC)
        wkT = arena[:, 2048:3072].rearrange("p (c n) -> p c n", c=HC)
        wvT = arena[:, 3072:4096].rearrange("p (c n) -> p c n", c=HC)
        scaled = arena[:, 4096:8192].rearrange("p (c k n) -> p c k n", c=HC, k=4)
        one_hot = arena[:, 0:2560].rearrange("p (t e s) -> p t e s", t=NT, e=E1)
        weighted = arena[:, 2560:5120].rearrange("p (t e s) -> p t e s", t=NT, e=E1)
        backT = arena[0:CAP, 5120:9216].rearrange("p (e t) -> p e t", e=E1)
        y_slots = arena[0:CAP, 9216:10240].rearrange("p (e c) -> p e c", e=E1)

        xb = sb("xb", [P, NT, C])
        stats = sb("stats", [P, NT, 6])
        mv = sb("mv", [P, NT, 2])
        veps = sb("veps", [P, NT])
        rstd = sb("rstd", [P, NT])
        xn = sb("xn", [P, NT, C])
        xnT = sb("xnT", [P, T])
        gates = sb("gates", [P, NT, E0 + 1])
        gatesT = sb("gatesT", [E0 + 1, T])
        lg = sb("lg", [P, NT, E0])
        pr = sb("pr", [P, NT, E0])
        red = sb("red", [P, NT])
        cmpa = sb("cmpa", [P, NT, E0, E0])
        cmpb = sb("cmpb", [P, NT, E0, E0])
        rank = sb("rank", [P, NT, E0])
        facc = sb("facc", [P, NT, C])
        mt_slot = sb("mt_slot", [P, 2, C])
        w13 = sb("w13", [P, 2, HID0])
        gv = sb("gv", [P, 2, KEYS])
        wv = sb("wv", [P, NT, 2, C])
        top8 = sb("top8", [P, 2, 8])
        nmax = sb("nmax", [P, 2])
        den = sb("den", [P, 2])
        rden = sb("rden", [P, 2])
        ex = sb("ex", [P, 2, KEYS])
        kept = sb("kept", [P, 2, KEYS])
        attn = sb("attn", [P, 2, T])
        attnT = sb("attnT", [P, 2, T])
        attn_mem = sb("attn_mem", [P, NT, H, NM])
        memT = sb("memT", [P, 2, T])
        h1 = sb("h1", [P, 2, T])
        hu = sb("hu", [P, 2, T])
        ht = sb("ht", [P, 2, T])
        hh = sb("hh", [P, 2, T])
        x1 = sb("x1", [P, NT, C])
        sg = hh[:, 0, :].rearrange("p (t c) -> p t c", t=NT)
        hn = xb
        hT = attnT[:, 0, :]
        qk = attn[:, :, :].rearrange("p a (t k c) -> p (a t) k c", t=2, k=2)
        vT = hu[:, 1, :]
        cw = sb("cw", [P, C])
        cwT = sb("cwT", [P, C])
        cmax = sb("cmax", [P, 1])
        csum = sb("csum", [P, 1])
        aT = attnT[:, 1, :]
        s1 = sb("s1", [P, NT, C])
        chosen = sb("chosen", [P, NT, E1], BF16)
        pos = sb("pos", [P, NT, E1])
        bufT = kept[:, :, :].rearrange("p a n -> p (a n)")[:, 0:E1 * CAP].rearrange("p (e s) -> p e s", e=E1)
        hid = ex[:, :, :].rearrange("p a n -> p (a n)")[:, 0:2 * HM1 * CAP].rearrange("p (a m s) -> p a m s", a=2, m=HM1)
        y_out = sb("y_out", [P, NT, C])

        loaded_a = sem("loaded_a")
        loaded_b = sem("loaded_b")
        consts = sem("consts")
        su_pe = sem("su_pe")
        su_act = sem("su_act")
        su_dve = sem("su_dve")
        x_loaded = Signal(sem("x_loaded"), 16)
        x_taken = Signal(sem("x_taken"), 1)
        def sig(name, per_row, preset=0):
            return Signal(sem(name), per_row, preset)

        mt_ready = sig("mt_ready", NIT, 1)
        w13_ready = sig("w13_ready", NIT, 1)
        g_ready = sig("g_ready", NIT, 1)
        misc_ready = sig("misc_ready", NIT * MISC)
        misc_free = [sig(f"misc_free{i}", NIT * MISC // 2, 1) for i in range(2)]
        sc_ready = sig("sc_ready", NIT * UNITS)
        top_done = sig("top_done", NIT * UNITS)
        nmax_ready = sig("nmax_ready", NIT * UNITS)
        exp_done = sig("exp_done", NIT * UNITS)
        kept_ready = sig("kept_ready", NIT * UNITS, 2)
        rden_ready = sig("rden_ready", NIT * UNITS)
        attn_ready = sig("attn_ready", NIT * UNITS, 2)
        tr_ready = sig("tr_ready", NIT * UNITS, 2)
        attnT_ready = sig("attnT_ready", NIT * UNITS, 1)
        av_done = sig("av_done", NIT * UNITS, 2)
        th_ready = sig("th_ready", NIT * 2)
        hh_ready = sig("hh_ready", NIT * 2)
        var_ready = sig("var_ready", 3)
        rstd_ready = sig("rstd_ready", 3)
        xn_ready = sig("xn_ready", 3)
        xnT_ps = sig("xnT_ps", 3)
        xnT_ready = sig("xnT_ready", 3)
        logit_ps = sig("logit_ps", 2)
        logit_ready = sig("logit_ready", 2)
        gexp_done = sig("gexp_done", 2)
        gates_ready = sig("gates_ready", 1)
        gatesT_ps = sig("gatesT_ps", 1)
        gatesT_ready = sig("gatesT_ready", 1)
        facc_ps = sig("facc_ps", 1)
        facc_ready = sig("facc_ready", 1)
        memT_ps = sig("memT_ps", 2)
        memT_ready = sig("memT_ready", 2)
        s0_ready = sig("s0_ready", 1)
        z_ready = sig("z_ready", 1)
        ez_ready = sig("ez_ready", 2)
        x1_ready = sig("x1_ready", 1)
        qk_ps = sig("qk_ps", 1)
        qk_ready = sig("qk_ready", 1)
        v_ps = sig("v_ps", 1)
        vT_ready = sig("vT_ready", 1)
        cw_ps = sig("cw_ps", 1)
        cmax_ready = sig("cmax_ready", 1)
        cexp_done = sig("cexp_done", 1)
        cw_ready = sig("cw_ready", 1)
        cwT_ps = sig("cwT_ps", 1)
        cwT_ready = sig("cwT_ready", 1)
        aT_ps = sig("aT_ps", 1)
        aT_ready = sig("aT_ready", 1)
        proj_ps = sig("proj_ps", 1)
        s1_ready = sig("s1_ready", 1)
        chosen_ready = sig("chosen_ready", 1)
        pos_ps = sig("pos_ps", 1)
        one_hot_ready = sig("one_hot_ready", 1)
        weighted_ready = sig("weighted_ready", 1)
        buf_ps = sig("buf_ps", 2)
        buf_ready = sig("buf_ready", 2)
        back_ps = sig("back_ps", E1)
        back_ready = sig("back_ready", E1)
        hid_ps = sig("hid_ps", E1)
        hid_act = sig("hid_act", E1)
        hid_dve = sig("hid_dve", E1)
        y_ps = sig("y_ps", 2)
        y_ready = sig("y_ready", 2)
        comb_ps = sig("comb_ps", 1)
        out_ready = sig("out_ready", 1)
        stored = Signal(sem("stored"), 16, 16)

        block = ctx.enter_context(nc.Block())

        def score_slot(u, t):
            n = NM + P * (t + 1)
            at = 0 if n <= 512 else 512 - NM - 256
            flat = sc[:, 2 * (u % 2):2 * (u % 2) + 2, :].rearrange("p a n -> p (a n)")
            return flat[:, at:at + n], n

        def bank(i):
            return sc[:, i, :]

        N_A, N_B = 10, 23

        @block.sync
        def _(sp):
            sp.dma_start(wq_raw, Wq).then_inc(loaded_a, 16)
            sp.dma_start(wk_raw, Wk).then_inc(loaded_a, 16)
            sp.dma_start(wv_raw, Wv).then_inc(loaded_a, 16)
            sp.dma_start(wo_sb, Wo.rearrange("(c p) n -> p c n", p=P)).then_inc(loaded_a, 16)
            for a in range(2):
                sp.dma_start(gv[0:NM, a, 0:512].rearrange("m (h d) -> m h d", d=DH),
                             mem_k[a * H // 2:(a + 1) * H // 2].rearrange("h m d -> m h d")).then_inc(loaded_a, 16)
            sp.dma_start(wv[0:NM, :, :, :].rearrange("m t k c -> m (t k c)").rearrange("m (h d) -> m h d", d=DH),
                         mem_v.rearrange("h m d -> m h d")).then_inc(loaded_a, 16)
            sp.dma_start(kept[0:H, 0, 0:H], pre).then_inc(loaded_a, 16)
            sp.dma_start(kept[0:H, 1, 0:H], post).then_inc(loaded_a, 16)
            sp.dma_start(hh[:, 0, 0:C], Wf).then_inc(loaded_a, 16)
            sp.dma_start(x_next[:, :, :], x[0].rearrange("(t p) c -> p t c", p=P)).then_inc(x_loaded.sem, 16)
            n = 0

            def load(dst, src):
                nonlocal n
                sp.dma_start(dst, src).then_inc(loaded_b, 16)
                n += 1
            load(attn_mem[:, :, :, :].rearrange("p t h m -> p (t h m)").rearrange("p (e m o) -> p e m o", e=4, m=2),
                 W2[0:4].rearrange("e (m p) o -> p e m o", p=P))
            load(memT[:, :, :].rearrange("p a n -> p (a n)").rearrange("p (e m o) -> p e m o", e=4, m=2),
                 W2[4:8].rearrange("e (m p) o -> p e m o", p=P))
            load(w13_all[:, 0:E0, 0, :], W1.rearrange("e c h -> c e h"))
            load(w13_all[:, 0:E0, 1, :], W3.rearrange("e c h -> c e h"))
            load(w13_all[:, E0, 0, :], W1[0])
            load(w13_all[:, E0, 1, :], W3[0])
            load(hu[0:E0, 0, 0:C], b2)
            load(b2f[E0:E0 + 1, :], bf.rearrange("(a n) -> a n", a=1))
            load(wg[:, :], Wg)
            load(bg_b[:, :], bg.rearrange("(a n) -> a n", a=1).partition_broadcast(P))
            load(bo_row[:, 0, :], bo.rearrange("(a n) -> a n", a=1))
            load(b1c[:, :, :], b1)
            load(b3c[:, :, :], b3)
            load(qk[:, 0:3, 0, :], qkv_w.rearrange("(a p) c -> p a c", p=P))
            load(qk[:, 3, 0, :], proj_w)
            load(cmax[:, :], norm_w.rearrange("(p a) -> p a", a=1))
            load(csum[:, :], norm_b.rearrange("(p a) -> p a", a=1))
            load(qk_bias[:, :, :].rearrange("p a c -> p (a c)"),
                 qkv_b[0:2 * C].rearrange("(a n) -> a n", a=1).partition_broadcast(P))
            load(v_bias[:, :], qkv_b[2 * C:3 * C].rearrange("(p a) -> p a", a=1))
            load(pb_b[:, :], proj_b.rearrange("(a n) -> a n", a=1).partition_broadcast(P))
            load(wr[:, :], Wr)
            sp.wait_ge(su_act, 6)
            load(v1_all[:, :, :], V1.rearrange("e c h -> c e h"))
            load(v2_all[:, :, :, :], V2.rearrange("e (m p) c -> p e m c", p=P))
            assert n == N_B
            sp.dma_start(c1c[:, :, :], c1).then_inc(loaded_b, 16)
            sp.dma_start(c2_b[:, :, :].rearrange("p e c -> p (e c)"),
                         c2.rearrange("e c -> (e c)").rearrange("(a n) -> a n", a=1).partition_broadcast(CAP)
                         ).then_inc(loaded_b, 16)
            def store(b, row):
                sp.wait_ge(out_ready.sem, out_ready.at(b, 1))
                sp.dma_start(row.rearrange("(t p) c -> p t c", p=P), y_out[:, :, :]).then_inc(stored.sem, 16)

            with sp.Fori(0, B - 1) as b:
                sp.wait_ge(x_taken.sem, x_taken.at(b, 1))
                sp.dma_start(x_next[:, :, :], x[bass.ds(b + 1, 1)].rearrange("o (t p) c -> p (o t) c", p=P)
                             ).then_inc(x_loaded.sem, 16)
                store(b, out[bass.ds(b, 1)].rearrange("o t c -> (o t) c"))
            store(B - 1, out[B - 1])
            sp.wait_ge(stored.sem, stored.at(B - 1, 16))

        N_B += 2

        @block.gpsimd
        def _(pool):
            pool.memset(ident[:, :], 0.0)
            pool.memset(ident_h[:, :], 0.0)
            pool.memset(causal[:, :], 0.0)
            pool.memset(before[:, :], 1.0)
            pool.memset(ones_h[:, :], 1.0)
            pool.memset(ties0[:, :, :], 1.0)
            pool.memset(ties1[:, :, :], 1.0)
            pool.memset(neghalf[:, :], -0.5)
            pool.memset(ones_row[:, :], 1.0)
            pool.memset(gates[:, :, :], 1.0)
            pool.memset(ex[0:H, 0, 0:512], 0.0)
            pool.memset(ex[0:H, 1, 0:512], 0.0)
            pool.iota(slot_no[:, :], pattern=[[1, CAP]], base=0, channel_multiplier=0,
                      allow_small_or_imprecise_dtypes=True)
            pool.drain()
            for m in (ident, ident_h):
                pool.affine_select(out=m[:, :], in_=m[:, :], compare_op=ALU.not_equal, fill=1.0,
                                   base=0, pattern=[[-1, P]], channel_multiplier=1)
            pool.affine_select(out=causal[:, :], in_=causal[:, :], compare_op=ALU.is_ge, fill=MASKED,
                               base=0, pattern=[[-1, P]], channel_multiplier=1)
            pool.affine_select(out=before[:, :], in_=before[:, :], compare_op=ALU.is_gt, fill=0.0,
                               base=0, pattern=[[1, P]], channel_multiplier=-1)
            pool.affine_select(out=ties0[:, :, :], in_=ties0[:, :, :], compare_op=ALU.is_gt, fill=0.0,
                               base=0, pattern=[[-1, E0], [1, E0]], channel_multiplier=0)
            pool.affine_select(out=ties1[:, :, :], in_=ties1[:, :, :], compare_op=ALU.is_gt, fill=0.0,
                               base=0, pattern=[[1, E1], [-1, E1]], channel_multiplier=0)
            for half in range(2):
                sel = ex[0:H, half, 0:512].rearrange("h (c two d) -> h c two d", c=4, two=2)
                pool.affine_select(out=sel, in_=sel, compare_op=ALU.not_equal, fill=1.0, base=-8 * half,
                                   pattern=[[-2, 4], [-1, 2], [0, DH]], channel_multiplier=1)
            pool.drain()
            pool.memset(neghalf[:, :], -0.5).then_inc(consts, 1)
            pool.wait_ge(su_dve, SU_DVE)
            pool.wait_ge(su_act, SU_ACT)
            pool.wait_ge(loaded_b, 16 * N_B)
            pool.tensor_copy(mt_slot[:, :, :], mt_all[:, 0, :, :]).then_inc(mt_ready.sem, 1)
            pool.tensor_copy(w13[:, :, :], w13_all[:, 0, :, :]).then_inc(w13_ready.sem, 1)
            pool.tensor_copy(gv[:, :, 0:NM], g_all[:, 0, :, :]).then_inc(g_ready.sem, 1)

            def root(b, n):
                pool.wait_ge(var_ready.sem, var_ready.at(b, n))
                pool.tensor_tensor(rstd[:, :], veps[:, :], neghalf[:, :], ALU.pow).then_inc(rstd_ready.sem, 1)

            with pool.Fori(0, B) as b:
                root(b, 1)
                with pool.Fori(0, NIT) as it:
                    for u in range(UNITS):
                        t = u % NT
                        n = it * UNITS + u + 1
                        pool.wait_ge(rden_ready.sem, rden_ready.at(b, n))
                        pool.wait_ge(tr_ready.sem, tr_ready.at(b, n - 2))
                        pool.nop(nofuse=True)
                        pool.tensor_scalar(attn[:, u % 2, 0:P * (t + 1)], kept[:, u % 2, NM:NM + P * (t + 1)],
                                           rden[:, u % 2:u % 2 + 1], 1.0, ALU.mult, ALU.mult
                                           ).then_inc(attn_ready.sem, 1)
                        if u == 3:
                            pool.wait_ge(misc_ready.sem, misc_ready.at(b, it * MISC + 4))
                            pool.tensor_copy(mt_slot[:, :, :], mt_all[:, bass.ds(it + 1, 1), :, :].rearrange(
                                "p o a c -> p (o a) c")).then_inc(mt_ready.sem, 1)
                        if u == 6:
                            pool.wait_ge(misc_ready.sem, misc_ready.at(b, it * MISC + 8))
                            pool.tensor_copy(w13[:, :, :], w13_all[:, bass.ds(it + 1, 1), :, :].rearrange(
                                "p o a c -> p (o a) c")).then_inc(w13_ready.sem, 1)
                    pool.wait_ge(sc_ready.sem, sc_ready.at(b, it * UNITS + UNITS))
                    pool.tensor_copy(gv[:, :, 0:NM], g_all[:, bass.ds(it + 1, 1), :, :].rearrange(
                        "p o a c -> p (o a) c")).then_inc(g_ready.sem, 1)
                root(b, 2)
                root(b, 3)
                pool.wait_ge(one_hot_ready.sem, one_hot_ready.at(b, 1))
                pool.tensor_tensor(weighted[:, :, :, :], one_hot[:, :, :, :],
                                   pr[:, :, :].unsqueeze(3).to_broadcast([P, NT, E1, CAP]), ALU.mult
                                   ).then_inc(weighted_ready.sem, 1)

        @block.scalar
        def _(act):
            step = [0]

            def setup_copy(dst, src, pe_stage, scale=None):
                act.wait_ge(su_pe, pe_stage)
                ins = act.activation(dst, src, ACT.Copy, scale=1.0 if scale is None else scale)
                step[0] += 1
                ins.then_inc(su_act, 1)

            stages = SetupStages()
            for w, dst in ((0, wqT), (1, wkT), (2, wvT)):
                for half in range(2):
                    setup_copy(dst[:, 4 * half:4 * half + 4, :],
                               bank(2 * (w % 2) + half).rearrange("p (c n) -> p c n", c=4), stages.turned(w, half))
            setup_copy(h1[:, 0, 0:HC * NM], mb[:, 0, 0:HC * NM], stages.memk)
            setup_copy(h1[:, 1, 0:HC * NM], mb[:, 1, 0:HC * NM], stages.memv)
            setup_copy(ht[0:H, 0, 0:H], tr[0:H, 0:H], stages.postT)
            setup_copy(ht[:, 1, 0:2 * HC * H], sa[:, 0:2 * HC * H], stages.cols)
            for q in range(4):
                setup_copy(mt_all[:, 2 * q:2 * q + 2, :, :].rearrange("p a k c -> p (a k c)"), bank(q % 2), stages.fold(q))
                setup_copy(g_all[:, 2 * q:2 * q + 2, :, :].rearrange("p a k m -> p (a k m)"),
                           bank(2 + q % 2)[:, 0:4 * NM], stages.fold(q))
            for q in range(4):
                setup_copy(n_all[:, 2 * q:2 * q + 2, :, :].rearrange("p a k c -> p (a k c)"), bank(q % 2),
                           stages.fold(4 + q))
            setup_copy(r_all[:, :, :].rearrange("p a c -> p (a c)"), bank(2)[:, 0:2 * C], stages.memr)
            for q in range(4):
                setup_copy(h1[:, q % 2, :], mb[:, q % 2, :], stages.w2turned(q))
                setup_copy(w2f[:, 2 * q:2 * q + 2, :, :].rearrange("p e m c -> p (e m c)"), bank(q % 2),
                           stages.w2folded(q), scale=0.5)
            setup_copy(xnT[:, 0:E0], tr[:, 0:E0], stages.b2turned)
            setup_copy(b2f[0:E0, :], bank(2)[0:E0, 0:C], stages.b2folded)
            setup_copy(hT, bank(3), stages.qkvturned)
            assert step[0] == SU_ACT

            def evacuate(b, it, n, dst, bias=None):
                act.wait_ge(misc_ready.sem, misc_ready.at(b, it * MISC + n + 1))
                if bias is None:
                    return act.activation(dst, mb[:, n % 2, :], ACT.Copy)
                return act.activation(dst, mb[:, n % 2, :], ACT.Identity, bias=bias)

            with act.Fori(0, B) as b:
                act.wait_ge(xnT_ps.sem, xnT_ps.at(b, 1))
                act.activation(xnT[:, :], bank(0), ACT.Copy).then_inc(xnT_ready.sem, 1)
                act.wait_ge(logit_ready.sem, logit_ready.at(b, 1))
                act.activation(pr[:, :, :], lg[:, :, :], ACT.Exp).then_inc(gexp_done.sem, 1)
                act.wait_ge(gatesT_ps.sem, gatesT_ps.at(b, 1))
                act.activation(gatesT[:, :], bank(2)[0:E0 + 1, :], ACT.Copy).then_inc(gatesT_ready.sem, 1)
                act.wait_ge(facc_ps.sem, facc_ps.at(b, 1))
                act.activation(facc[:, :, :].rearrange("p t c -> p (t c)"), bank(3), ACT.Copy
                               ).then_inc(facc_ready.sem, 1)
                with act.Fori(0, NIT) as it:
                    def value_keys(k, n):
                        evacuate(b, it, n, gv[:, k, NM:KEYS]).then_inc(misc_free[n % 2].sem, 1)

                    def hidden1(m, n):
                        evacuate(b, it, n, h1[:, m, :], b1c[:, bass.ds(it, 1), m]).then_inc(misc_free[n % 2].sem, 1)

                    def exps(u):
                        t, n = u % NT, it * UNITS + u + 1
                        src, w = score_slot(u, t)
                        act.wait_ge(nmax_ready.sem, nmax_ready.at(b, n))
                        act.activation(ex[:, u % 2, 0:w], src, ACT.Exp, bias=nmax[:, u % 2:u % 2 + 1]
                                       ).then_inc(exp_done.sem, 1)

                    def values(half, n):
                        if half == 0:
                            act.wait_ge(av_done.sem, av_done.at(b, it * UNITS))
                        evacuate(b, it, n, wv[:, 2 * half:2 * half + 2, :, :].rearrange("p t k c -> p (t k c)")
                                 ).then_inc(misc_free[n % 2].sem, 1)

                    def turned(u):
                        t, n = u % NT, it * UNITS + u + 1
                        act.wait_ge(rden_ready.sem, rden_ready.at(b, n))
                        act.activation(attn_mem[:, t, bass.ds(2 * it + u // NT, 1), :],
                                       kept[:, u % 2:u % 2 + 1, 0:NM], ACT.Copy, scale=rden[:, u % 2:u % 2 + 1])
                        act.wait_ge(tr_ready.sem, tr_ready.at(b, n))
                        act.wait_ge(av_done.sem, av_done.at(b, n - 2))
                        act.activation(attnT[:, u % 2, 0:P * (t + 1)], tr[:, 0:P * (t + 1)], ACT.Copy
                                       ).then_inc(attnT_ready.sem, 1)

                    def tanhs(m):
                        act.wait_ge(misc_free[m].sem, misc_free[m].at(b, it * (MISC // 2) + (2, 4)[m]))
                        act.activation(ht[:, m, :], hu[:, m, :], ACT.Tanh, scale=0.5).then_inc(th_ready.sem, 1)

                    value_keys(0, 0)
                    hidden1(0, 1)
                    exps(0)
                    exps(1)
                    value_keys(1, 3)
                    values(0, 4)
                    turned(0)
                    exps(2)
                    values(1, 5)
                    tanhs(0)
                    turned(1)
                    exps(3)
                    hidden1(1, 6)
                    turned(2)
                    exps(4)
                    turned(3)
                    exps(5)
                    tanhs(1)
                    turned(4)
                    exps(6)
                    turned(5)
                    exps(7)
                    turned(6)
                    turned(7)
                for g in range(2):
                    act.wait_ge(memT_ps.sem, memT_ps.at(b, g + 1))
                    act.activation(memT[:, g, :], bank(g), ACT.Copy).then_inc(memT_ready.sem, 1)
                act.wait_ge(z_ready.sem, z_ready.at(b, 1))
                act.activation(sg[:, :, :], facc[:, :, :], ACT.Exp, scale=-1.0).then_inc(ez_ready.sem, 1)
                act.wait_ge(xnT_ps.sem, xnT_ps.at(b, 2))
                act.activation(xnT[:, :], bank(0), ACT.Copy).then_inc(xnT_ready.sem, 1)
                act.wait_ge(logit_ready.sem, logit_ready.at(b, 2))
                act.activation(pr[:, :, :], lg[:, :, :], ACT.Exp).then_inc(gexp_done.sem, 1)
                act.wait_ge(xnT_ps.sem, xnT_ps.at(b, 3))
                act.activation(hT, bank(2), ACT.Copy).then_inc(xnT_ready.sem, 1)
                act.wait_ge(v_ps.sem, v_ps.at(b, 1))
                act.activation(vT, bank(3), ACT.Identity, bias=v_bias[:, 0:1]).then_inc(vT_ready.sem, 1)
                act.wait_ge(cmax_ready.sem, cmax_ready.at(b, 1))
                act.activation(cw[:, :], tr[:, 0:C], ACT.Exp, bias=cmax[:, 0:1], scale=float(1.0 / np.sqrt(T))
                               ).then_inc(cexp_done.sem, 1)
                act.wait_ge(cwT_ps.sem, cwT_ps.at(b, 1))
                act.activation(cwT[:, :], tr[:, 0:C], ACT.Copy).then_inc(cwT_ready.sem, 1)
                act.wait_ge(aT_ps.sem, aT_ps.at(b, 1))
                act.activation(aT, bank(2), ACT.Copy).then_inc(aT_ready.sem, 1)
                for half in range(2):
                    act.wait_ge(buf_ps.sem, buf_ps.at(b, half + 1))
                    act.activation(bufT[:, 4 * half:4 * half + 4, :].rearrange("p e s -> p (e s)"),
                                   bank(half)[:, 0:4 * CAP], ACT.Copy).then_inc(buf_ready.sem, 1)
                for e in range(E1):
                    act.wait_ge(hid_ps.sem, hid_ps.at(b, e + 1))
                    for m in range(HM1 // 2):
                        ins = act.activation(hid[:, e % 2, m, :], bank(e % 2)[:, m * CAP:(m + 1) * CAP], ACT.Relu,
                                             bias=c1c[:, e, m:m + 1])
                    ins.then_inc(hid_act.sem, 1)
                    act.wait_ge(back_ps.sem, back_ps.at(b, e + 1))
                    act.activation(backT[:, e, :], bank(2 + e % 2)[0:CAP, :], ACT.Copy).then_inc(back_ready.sem, 1)
                act.wait_ge(comb_ps.sem, comb_ps.at(b, 1))
                act.activation(sg[:, :, :].rearrange("p t c -> p (t c)"), sa[:, :], ACT.Exp, scale=-1.0
                               ).then_inc(ez_ready.sem, 1)

        @block.vector
        def _(dve):
            stages = SetupStages()
            pre_col = ht[:, 1, 0:HC * H].rearrange("p (c h) -> p c h", c=HC)
            post_col = ht[:, 1, HC * H:2 * HC * H].rearrange("p (c h) -> p c h", c=HC)
            dve.wait_ge(su_act, stages.act_cols)
            dve.wait_ge(loaded_a, 16 * N_A)
            for q in range(4):
                if q:
                    dve.wait_ge(su_pe, stages.fold(q - 1))
                for k in range(4):
                    col = pre_col[:, :, 4 * q + k:4 * q + k + 1].to_broadcast([P, HC, C])
                    ins = dve.scalar_tensor_tensor(out=scaled[:, :, k, :], in0=wqT, scalar=float(DH) ** -0.5,
                                                   in1=col, op0=ALU.mult, op1=ALU.mult)
                ins.then_inc(su_dve, 1)
            for q in range(4):
                dve.wait_ge(su_pe, stages.fold(3 + q))
                for k in range(4):
                    col = post_col[:, :, 4 * q + k:4 * q + k + 1].to_broadcast([P, HC, C])
                    ins = dve.tensor_tensor(scaled[:, :, k, :], wo_sb, col, ALU.mult)
                ins.then_inc(su_dve, 1)
            dve.wait_ge(su_pe, stages.fold(7))
            mem_scaled = scaled[:, :, :, :].rearrange("p c k n -> p c (k n)")[:, :, 0:H * NM].rearrange(
                "p c (h m) -> p c h m", h=H)
            memvT = h1[:, 1, 0:HC * NM].rearrange("p (c m) -> p c m", c=HC)
            for c in range(HC):
                ins = dve.tensor_tensor(mem_scaled[:, c, :, :], memvT[:, c, :].unsqueeze(1).to_broadcast([P, H, NM]),
                                        post_col[:, c, :].unsqueeze(2).to_broadcast([P, H, NM]), ALU.mult)
            ins.then_inc(su_dve, 1)
            dve.wait_ge(su_pe, stages.biases)
            dve.wait_ge(su_act, SU_ACT)
            dve.wait_ge(loaded_b, 16 * N_B)
            dve.tensor_tensor(qk_bias[:, :, :].rearrange("p a c -> p (a c)"), bank(0)[:, 0:2 * C],
                              qk_bias[:, :, :].rearrange("p a c -> p (a c)"), ALU.add)
            dve.tensor_tensor(v_bias[:, :], bank(1)[:, 0:1], v_bias[:, :], ALU.add)
            dve.tensor_scalar(qkvT[:, :, :].rearrange("p a c -> p (a c)"), hT[:, 0:3 * C], cmax[:, 0:1], None, ALU.mult)
            dve.tensor_copy(projT[:, :], hT[:, 3 * C:4 * C])
            dve.tensor_copy(mt_all[:, NIT, :, :], mt_all[:, 0, :, :])
            dve.tensor_copy(g_all[:, NIT, :, :], g_all[:, 0, :, :])
            dve.drain()
            for s in (misc_free[0], misc_free[1], kept_ready, attn_ready, tr_ready, attnT_ready, av_done,
                      stored):
                dve.memset(den[:, 0:1], 0.0).then_inc(s.sem, s.preset)
                dve.drain()
            dve.memset(den[:, 1:2], 0.0).then_inc(su_dve, 1)

            def norm(b, n, src, dst):
                for t in range(NT):
                    dve.bn_stats(stats[:, t, :], src[:, t, :])
                dve.drain()
                for t in range(NT):
                    dve.bn_aggr(mv[:, t, :], stats[:, t, :])
                dve.drain()
                dve.tensor_scalar(veps[:, :], mv[:, :, 1], EPS, None, ALU.add).then_inc(var_ready.sem, 1)
                dve.wait_ge(rstd_ready.sem, rstd_ready.at(b, n))
                for t in range(NT):
                    ins = dve.tensor_scalar(dst[:, t, :], src[:, t, :], mv[:, t, 0:1], rstd[:, t:t + 1],
                                            ALU.subtract, ALU.mult)
                ins.then_inc(xn_ready.sem, 1)

            def softmax_top2(b, n, logits, bias, ties):
                dve.wait_ge(logit_ps.sem, logit_ps.at(b, n))
                if bias is None:
                    dve.tensor_copy(lg[:, :, :], logits)
                else:
                    dve.tensor_tensor(lg[:, :, :], logits, bias[:, :].unsqueeze(1).to_broadcast([P, NT, E0]), ALU.add)
                dve.drain()
                dve.tensor_reduce(red[:, :], lg[:, :, :], AX.X, ALU.max)
                dve.drain()
                dve.tensor_tensor(lg[:, :, :], lg[:, :, :], red[:, :].unsqueeze(2).to_broadcast([P, NT, E0]),
                                  ALU.subtract).then_inc(logit_ready.sem, 1)
                dve.wait_ge(gexp_done.sem, gexp_done.at(b, n))
                dve.tensor_reduce(red[:, :], pr[:, :, :], AX.X, ALU.add)
                dve.drain()
                dve.reciprocal(red[:, :], red[:, :])
                dve.drain()
                dve.tensor_tensor(pr[:, :, :], pr[:, :, :], red[:, :].unsqueeze(2).to_broadcast([P, NT, E0]), ALU.mult)
                dve.drain()
                other = pr[:, :, :].unsqueeze(2).to_broadcast([P, NT, E0, E0])
                own = pr[:, :, :].unsqueeze(3).to_broadcast([P, NT, E0, E0])
                dve.tensor_tensor(cmpa[:, :, :, :], other, own, ALU.is_gt)
                dve.tensor_tensor(cmpb[:, :, :, :], other, own, ALU.is_equal)
                dve.drain()
                dve.tensor_tensor(cmpb[:, :, :, :], cmpb[:, :, :, :],
                                  ties[:, :, :].unsqueeze(1).to_broadcast([P, NT, E0, E0]), ALU.mult)
                dve.drain()
                dve.tensor_tensor(cmpa[:, :, :, :], cmpa[:, :, :, :], cmpb[:, :, :, :], ALU.add)
                dve.drain()
                dve.tensor_reduce(rank[:, :, :], cmpa[:, :, :, :], AX.X, ALU.add)
                dve.drain()
                dve.tensor_scalar(rank[:, :, :], rank[:, :, :], 1.5, None, ALU.is_lt)
                dve.drain()

            def gated(b, n, z, s, base, dst):
                dve.wait_ge(ez_ready.sem, ez_ready.at(b, n))
                dve.tensor_scalar(sg[:, :, :], sg[:, :, :], 1.0, None, ALU.add)
                dve.drain()
                dve.reciprocal(sg[:, :, :], sg[:, :, :])
                dve.drain()
                dve.tensor_tensor(sg[:, :, :], sg[:, :, :], z, ALU.mult)
                dve.drain()
                dve.tensor_tensor(sg[:, :, :], sg[:, :, :], s, ALU.mult)
                dve.drain()
                return dve.tensor_tensor(dst, sg[:, :, :], base, ALU.add)

            with dve.Fori(0, B) as b:
                dve.wait_ge(x_loaded.sem, x_loaded.at(b, 16))
                dve.tensor_copy(xb[:, :, :], x_next[:, :, :]).then_inc(x_taken.sem, 1)
                dve.drain()
                norm(b, 1, xb, xn)
                softmax_top2(b, 1, bank(1)[:, 0:NT * E0].rearrange("p (t e) -> p t e", t=NT), bg_b, ties0)
                dve.tensor_tensor(gates[:, :, 0:E0], pr[:, :, :], rank[:, :, :], ALU.mult).then_inc(gates_ready.sem, 1)
                dve.wait_ge(facc_ready.sem, facc_ready.at(b, 1))
                dve.nop(nofuse=True)
                with dve.Fori(0, NIT) as it:
                    def top(u):
                        t, n = u % NT, it * UNITS + u + 1
                        src, w = score_slot(u, t)
                        dve.wait_ge(sc_ready.sem, sc_ready.at(b, n))
                        dve.nop(nofuse=True)
                        dve.max(top8[:, u % 2, :], src).then_inc(top_done.sem, 1)
                        dve.wait_ge(top_done.sem, top_done.at(b, n))
                        dve.tensor_scalar(nmax[:, u % 2:u % 2 + 1], top8[:, u % 2, 0:1], -1.0, None, ALU.mult
                                          ).then_inc(nmax_ready.sem, 1)

                    def keep(u):
                        t, n = u % NT, it * UNITS + u + 1
                        src, w = score_slot(u, t)
                        dve.wait_ge(exp_done.sem, exp_done.at(b, n))
                        dve.wait_ge(attn_ready.sem, attn_ready.at(b, n - 2))
                        dve.scalar_tensor_tensor(out=kept[:, u % 2, 0:w], in0=src, scalar=top8[:, u % 2, 7:8],
                                                 in1=ex[:, u % 2, 0:w], op0=ALU.is_ge, op1=ALU.mult,
                                                 accum_out=den[:, u % 2:u % 2 + 1]).then_inc(kept_ready.sem, 1)
                        dve.wait_ge(kept_ready.sem, kept_ready.at(b, n))
                        dve.reciprocal(rden[:, u % 2:u % 2 + 1], den[:, u % 2:u % 2 + 1]).then_inc(rden_ready.sem, 1)

                    def hidden3(m, n):
                        dve.wait_ge(misc_ready.sem, misc_ready.at(b, it * MISC + n + 1))
                        h1n = 1 if m == 0 else 6
                        dve.wait_ge(misc_free[h1n % 2].sem, misc_free[h1n % 2].at(b, it * (MISC // 2) + h1n // 2 + 1))
                        dve.scalar_tensor_tensor(out=hu[:, m, :], in0=mb[:, n % 2, :], scalar=b3c[:, bass.ds(it, 1), m],
                                                 in1=h1[:, m, :], op0=ALU.add, op1=ALU.mult
                                                 ).then_inc(misc_free[n % 2].sem, 1)

                    def silu(m):
                        dve.wait_ge(th_ready.sem, th_ready.at(b, it * 2 + m + 1))
                        dve.scalar_tensor_tensor(out=hh[:, m, :], in0=ht[:, m, :], scalar=1.0, in1=hu[:, m, :],
                                                 op0=ALU.add, op1=ALU.mult).then_inc(hh_ready.sem, 1)

                    def experts_out(half, n):
                        dve.wait_ge(misc_ready.sem, misc_ready.at(b, it * MISC + n + 1))
                        for j in range(2):
                            t = 2 * half + j
                            ins = dve.scalar_tensor_tensor(
                                out=facc[:, t, :], in0=mb[:, n % 2, j * C:(j + 1) * C], scalar=gates[:, t, bass.ds(it, 1)],
                                in1=facc[:, t, :], op0=ALU.mult, op1=ALU.add)
                        ins.then_inc(misc_free[n % 2].sem, 1)

                    top(0)
                    hidden3(0, 2)
                    top(1)
                    keep(0)
                    top(2)
                    keep(1)
                    silu(0)
                    top(3)
                    keep(2)
                    top(4)
                    keep(3)
                    hidden3(1, 7)
                    top(5)
                    keep(4)
                    silu(1)
                    top(6)
                    keep(5)
                    top(7)
                    keep(6)
                    keep(7)
                    experts_out(0, 8)
                    experts_out(1, 9)
                dve.drain()
                dve.memset(den[:, 0:1], 0.0).then_inc(z_ready.sem, 1)
                dve.wait_ge(s0_ready.sem, s0_ready.at(b, 1))
                gated(b, 1, facc[:, :, :], sa[:, :].rearrange("p (t c) -> p t c", t=NT), xb[:, :, :], x1[:, :, :]
                      ).then_inc(x1_ready.sem, 1)
                dve.drain()
                norm(b, 2, x1, xn)
                dve.drain()
                norm(b, 3, xn, hn)
                softmax_top2(b, 2, bank(1)[:, 0:NT * E1].rearrange("p (t e) -> p t e", t=NT), None, ties1)
                dve.tensor_copy(chosen[:, :, :], rank[:, :, :]).then_inc(chosen_ready.sem, 1)
                dve.tensor_tensor(s1[:, :, :], xn[:, :, :], pb_b[:, :].unsqueeze(1).to_broadcast([P, NT, C]), ALU.add)
                dve.wait_ge(qk_ps.sem, qk_ps.at(b, 1))
                for j in range(2):
                    ins = dve.tensor_tensor(
                        qk[:, 2 * j:2 * j + 2, :, :].rearrange("p t a c -> p t (a c)"),
                        mb[:, j, :].rearrange("p (t n) -> p t n", t=2),
                        qk_bias[:, :, :].rearrange("p a c -> p (a c)").unsqueeze(1).to_broadcast([P, 2, 2 * C]), ALU.add)
                ins.then_inc(qk_ready.sem, 1)
                dve.wait_ge(cw_ps.sem, cw_ps.at(b, 1))
                dve.tensor_reduce(cmax[:, :], tr[:, 0:C], AX.X, ALU.max)
                dve.drain()
                dve.tensor_scalar(cmax[:, :], cmax[:, :], float(-1.0 / np.sqrt(T)), None, ALU.mult
                                  ).then_inc(cmax_ready.sem, 1)
                dve.wait_ge(cexp_done.sem, cexp_done.at(b, 1))
                dve.tensor_reduce(csum[:, :], cw[:, :], AX.X, ALU.add)
                dve.drain()
                dve.reciprocal(csum[:, :], csum[:, :])
                dve.drain()
                dve.tensor_scalar(cw[:, :], cw[:, :], csum[:, 0:1], None, ALU.mult).then_inc(cw_ready.sem, 1)
                dve.wait_ge(pos_ps.sem, pos_ps.at(b, 1))
                dve.scalar_tensor_tensor(out=pos[:, :, :], in0=bank(1)[:, 64:64 + NT * E1].rearrange("p (t e) -> p t e", t=NT),
                                         scalar=1.0, in1=rank[:, :, :], op0=ALU.add, op1=ALU.mult)
                dve.drain()
                dve.tensor_scalar(pos[:, :, :], pos[:, :, :], -1.0, None, ALU.add)
                dve.drain()
                for t in range(NT):
                    ins = dve.tensor_tensor(one_hot[:, t, :, :], slot_no[:, :].unsqueeze(1).to_broadcast([P, E1, CAP]),
                                            pos[:, t, :].unsqueeze(2).to_broadcast([P, E1, CAP]), ALU.is_equal)
                ins.then_inc(one_hot_ready.sem, 1)
                dve.wait_ge(proj_ps.sem, proj_ps.at(b, 1))
                dve.tensor_tensor(s1[:, :, :].rearrange("p t c -> p (t c)"), bank(3),
                                  s1[:, :, :].rearrange("p t c -> p (t c)"), ALU.add).then_inc(s1_ready.sem, 1)
                for e in range(E1):
                    dve.wait_ge(hid_act.sem, hid_act.at(b, e + 1))
                    for m in range(HM1 // 2, HM1):
                        ins = dve.tensor_scalar(hid[:, e % 2, m, :], bank(e % 2)[:, m * CAP:(m + 1) * CAP],
                                                c1c[:, e, m:m + 1], 0.0, ALU.add, ALU.max)
                    ins.then_inc(hid_dve.sem, 1)
                    if e % 4 == 3:
                        half = e // 4
                        dve.wait_ge(y_ps.sem, y_ps.at(b, half + 1))
                        dve.tensor_tensor(y_slots[:, 4 * half:4 * half + 4, :].rearrange("p e c -> p (e c)"),
                                          mb[0:CAP, half, :],
                                          c2_b[:, 4 * half:4 * half + 4, :].rearrange("p e c -> p (e c)"), ALU.add
                                          ).then_inc(y_ready.sem, 1)
                dve.wait_ge(stored.sem, stored.at(b, 0))
                gated(b, 2, sa[:, :].rearrange("p (t c) -> p t c", t=NT), s1[:, :, :], x1[:, :, :], y_out[:, :, :]
                      ).then_inc(out_ready.sem, 1)

        @block.tensor
        def _(pe):
            stages = SetupStages()
            pe.wait_ge(consts, 1)
            pe.wait_ge(loaded_a, 16 * N_A)
            count = [0]

            def done(ins, expected):
                count[0] += 1
                assert count[0] == expected, (count[0], expected)
                ins.then_inc(su_pe, 1)

            for w, raw in ((0, wq_raw), (1, wk_raw), (2, wv_raw)):
                if w == 2:
                    pe.wait_ge(su_act, 2)
                for half in range(2):
                    for j in range(4):
                        c = 4 * half + j
                        ins = pe.transpose(bank(2 * (w % 2) + half)[:, j * P:(j + 1) * P], raw[:, c * P:(c + 1) * P],
                                           ident[:, :])
                    done(ins, stages.turned(w, half))
            mk = gv[0:NM, :, 0:512]
            mv_flat = wv[0:NM, :, :, :].rearrange("m t k c -> m (t k c)")
            for c in range(HC):
                ins = pe.transpose(mb[:, 0, c * NM:(c + 1) * NM], mk[:, c // 4, (c % 4) * P:(c % 4 + 1) * P],
                                   ident[0:NM, 0:NM])
            done(ins, stages.memk)
            for c in range(HC):
                ins = pe.transpose(mb[:, 1, c * NM:(c + 1) * NM], mv_flat[:, c * P:(c + 1) * P], ident[0:NM, 0:NM])
            done(ins, stages.memv)
            done(pe.transpose(tr[0:H, 0:H], kept[0:H, 1, 0:H], ident[0:H, 0:H]), stages.postT)
            pe.wait_ge(su_act, stages.act_postT)
            for c in range(HC):
                sel = ex[0:H, c // 4, (c % 4) * P:(c % 4 + 1) * P]
                pe.matmul(sa[:, c * H:(c + 1) * H], sel, kept[0:H, 0, 0:H], start=True, stop=True)
                ins = pe.matmul(sa[:, (HC + c) * H:(HC + c + 1) * H], sel, ht[0:H, 0, 0:H], start=True, stop=True)
            done(ins, stages.cols)
            pe.wait_ge(su_act, stages.act_cols)
            for q in range(4):
                pe.wait_ge(su_dve, q + 1)
                if q >= 2:
                    pe.wait_ge(su_act, stages.act_fold(q - 2))
                for c in range(HC):
                    ins = pe.matmul(bank(q % 2), wkT[:, c, :], scaled[:, c, :, :].rearrange("p k n -> p (k n)"),
                                    start=(c == 0), stop=(c == HC - 1))
                for k in range(4):
                    for c in range(HC):
                        ins = pe.matmul(bank(2 + q % 2)[:, k * NM:(k + 1) * NM], scaled[:, c, k, :],
                                        h1[:, 0, c * NM:(c + 1) * NM], start=(c == 0), stop=(c == HC - 1))
                done(ins, stages.fold(q))
            for q in range(4):
                pe.wait_ge(su_dve, 4 + q + 1)
                pe.wait_ge(su_act, stages.act_fold(2 + q))
                for c in range(HC):
                    ins = pe.matmul(bank(q % 2), wvT[:, c, :], scaled[:, c, :, :].rearrange("p k n -> p (k n)"),
                                    start=(c == 0), stop=(c == HC - 1))
                done(ins, stages.fold(4 + q))
            pe.wait_ge(su_dve, 9)
            mem_scaled = scaled[:, :, :, :].rearrange("p c k n -> p c (k n)")
            for g in range(2):
                for c in range(HC):
                    ins = pe.matmul(bank(2)[:, g * C:(g + 1) * C], mem_scaled[:, c, g * P:(g + 1) * P], wo_sb[:, c, :],
                                    start=(c == 0), stop=(c == HC - 1))
            done(ins, stages.memr)
            pe.wait_ge(loaded_b, 16 * N_B)
            pe.wait_ge(su_act, stages.act_memr)
            for q in range(4):
                w2raw = (attn_mem[:, :, :, :].rearrange("p t h m -> p (t h m)") if q < 2
                         else memT[:, :, :].rearrange("p a n -> p (a n)"))
                if q >= 2:
                    pe.wait_ge(su_act, stages.act_w2(q - 2))
                for j in range(4):
                    at = ((q % 2) * 4 + j) * C
                    ins = pe.transpose(mb[:, q % 2, j * P:(j + 1) * P], w2raw[:, at:at + C], ident[:, :])
                done(ins, stages.w2turned(q))
                pe.wait_ge(su_act, stages.act_w2(q) - 1)
                for j in range(4):
                    ins = pe.matmul(bank(q % 2)[:, j * C:(j + 1) * C], h1[:, q % 2, j * P:(j + 1) * P], hh[:, 0, 0:C],
                                    start=True, stop=True)
                done(ins, stages.w2folded(q))
            done(pe.transpose(tr[:, 0:E0], hu[0:E0, 0, 0:C], ident[0:E0, 0:E0]), stages.b2turned)
            pe.wait_ge(su_act, stages.act_b2turned)
            done(pe.matmul(bank(2)[0:E0, 0:C], xnT[:, 0:E0], hh[:, 0, 0:C], start=True, stop=True), stages.b2folded)
            for a in range(4):
                ins = pe.transpose(bank(3)[:, a * P:(a + 1) * P], qk[:, a, 0, :], ident[:, :])
            done(ins, stages.qkvturned)
            pe.wait_ge(su_act, SU_ACT)
            pe.matmul(bank(0)[:, 0:2 * C], csum[:, 0:1].to_broadcast([P, P]), hT[:, 0:2 * C], start=True, stop=True)
            done(pe.matmul(bank(1)[:, 0:1], hT[:, 2 * C:3 * C], csum[:, 0:1], start=True, stop=True), stages.biases)
            pe.wait_ge(su_dve, SU_DVE)

            def turn(dst_bank, src):
                for t in range(NT):
                    ins = pe.transpose(dst_bank[:, t * P:(t + 1) * P], src[:, t, :], ident[:, :])
                return ins

            with pe.Fori(0, B) as b:
                pe.wait_ge(xn_ready.sem, xn_ready.at(b, 1))
                turn(bank(0), xn).then_inc(xnT_ps.sem, 1)
                pe.wait_ge(xnT_ready.sem, xnT_ready.at(b, 1))
                for t in range(NT):
                    ins = pe.matmul(bank(1)[:, t * E0:(t + 1) * E0], xnT[:, t * P:(t + 1) * P], wg[:, :],
                                    start=True, stop=True)
                ins.then_inc(logit_ps.sem, 1)
                pe.wait_ge(gates_ready.sem, gates_ready.at(b, 1))
                for t in range(NT):
                    ins = pe.transpose(bank(2)[0:E0 + 1, t * P:(t + 1) * P], gates[:, t, :], ident[:, :])
                ins.then_inc(gatesT_ps.sem, 1)
                pe.wait_ge(gatesT_ready.sem, gatesT_ready.at(b, 1))
                for t in range(NT):
                    ins = pe.matmul(bank(3)[:, t * C:(t + 1) * C], gatesT[:, t * P:(t + 1) * P], b2f[:, :],
                                    start=True, stop=True)
                ins.then_inc(facc_ps.sem, 1)
                pe.matmul(sa[:, :], ones_row[:, :], bo_row[:, :, :].to_broadcast([1, NT, C]),
                          start=True, stop=False, skip_group_check=True)
                pe.wait_ge(facc_ready.sem, facc_ready.at(b, 1))
                pe.nop(nofuse=True)
                with pe.Fori(0, NIT) as it:
                    def misc(n, pieces):
                        pe.wait_ge(misc_free[n % 2].sem, misc_free[n % 2].at(b, it * (MISC // 2) + n // 2))
                        for at, width, lhsT, rhs, start, stop in pieces:
                            ins = pe.matmul(mb[:, n % 2, at:at + width], lhsT, rhs, start=start, stop=stop)
                        ins.then_inc(misc_ready.sem, 1)

                    def value_keys(k, n):
                        misc(n, [(0, T, mt_slot[:, k, :], xnT[:, :], True, True)])

                    def values(half, n):
                        misc(n, [(j * 2 * C, 2 * C, xnT[:, (2 * half + j) * P:(2 * half + j + 1) * P],
                                  n_all[:, bass.ds(it, 1), :, :].rearrange("p o k c -> p (o k c)"), True, True)
                                 for j in range(2)])

                    def hidden(side, m, n):
                        misc(n, [(0, T, w13[:, side, m * P:(m + 1) * P], xnT[:, :], True, True)])

                    def experts_out(half, n):
                        misc(n, [(j * C, C, hh[:, m, (2 * half + j) * P:(2 * half + j + 1) * P],
                                  w2f[:, bass.ds(it, 1), m, :].rearrange("p o c -> p (o c)"), m == 0, m == 1)
                                 for j in range(2) for m in range(2)])

                    def scores(u):
                        t, n = u % NT, it * UNITS + u + 1
                        dst, w = score_slot(u, t)
                        k = u // NT
                        pe.wait_ge(kept_ready.sem, kept_ready.at(b, n - 2))
                        cut = w if w <= 512 else w - 256
                        for lo, hi in ((0, cut), (cut, w)):
                            if lo == hi:
                                continue
                            pe.matmul(dst[:, lo:hi], xnT[:, t * P:(t + 1) * P], gv[:, k, lo:hi],
                                      start=True, stop=(hi < w), skip_group_check=True)
                        pe.matmul(dst[:, w - P:w], ident_h[:, :], causal[:, :], start=False, stop=True,
                                  skip_group_check=True).then_inc(sc_ready.sem, 1)

                    def turned(u):
                        t, n = u % NT, it * UNITS + u + 1
                        pe.wait_ge(attn_ready.sem, attn_ready.at(b, n))
                        pe.wait_ge(attnT_ready.sem, attnT_ready.at(b, n - 1))
                        for j in range(t + 1):
                            ins = pe.transpose(tr[:, j * P:(j + 1) * P], attn[:, u % 2, j * P:(j + 1) * P], ident[:, :])
                        ins.then_inc(tr_ready.sem, 1)

                    def attend(u):
                        t, n = u % NT, it * UNITS + u + 1
                        pe.wait_ge(attnT_ready.sem, attnT_ready.at(b, n))
                        for j in range(t + 1):
                            ins = pe.matmul(sa[:, t * C:(t + 1) * C], attnT[:, u % 2, j * P:(j + 1) * P],
                                            wv[:, j, u // NT, :], start=False, stop=False, skip_group_check=True)
                        ins.then_inc(av_done.sem, 1)

                    pe.wait_ge(mt_ready.sem, mt_ready.at(b, it))
                    value_keys(0, 0)
                    pe.wait_ge(w13_ready.sem, w13_ready.at(b, it))
                    hidden(0, 0, 1)
                    pe.wait_ge(g_ready.sem, g_ready.at(b, it))
                    pe.wait_ge(misc_free[0].sem, misc_free[0].at(b, it * (MISC // 2) + 1))
                    scores(0)
                    hidden(1, 0, 2)
                    scores(1)
                    value_keys(1, 3)
                    values(0, 4)
                    turned(0)
                    scores(2)
                    values(1, 5)
                    pe.wait_ge(misc_free[0].sem, misc_free[0].at(b, it * (MISC // 2) + 3))
                    pe.wait_ge(misc_free[1].sem, misc_free[1].at(b, it * (MISC // 2) + 3))
                    attend(0)
                    turned(1)
                    scores(3)
                    hidden(0, 1, 6)
                    attend(1)
                    turned(2)
                    scores(4)
                    hidden(1, 1, 7)
                    attend(2)
                    turned(3)
                    scores(5)
                    attend(3)
                    turned(4)
                    scores(6)
                    attend(4)
                    turned(5)
                    scores(7)
                    attend(5)
                    turned(6)
                    pe.wait_ge(hh_ready.sem, hh_ready.at(b, it * 2 + 2))
                    experts_out(0, 8)
                    attend(6)
                    turned(7)
                    experts_out(1, 9)
                    attend(7)
                for g in range(2):
                    if g == 0:
                        pe.wait_ge(attnT_ready.sem, attnT_ready.at(b, NIT * UNITS))
                    for t in range(NT):
                        ins = pe.transpose(bank(g)[:, t * P:(t + 1) * P],
                                           attn_mem[:, t, 8 * g:8 * g + 8, :].rearrange("p h m -> p (h m)"), ident[:, :])
                    ins.then_inc(memT_ps.sem, 1)
                for g in range(2):
                    pe.wait_ge(memT_ready.sem, memT_ready.at(b, g + 1))
                    for t in range(NT):
                        ins = pe.matmul(sa[:, t * C:(t + 1) * C], memT[:, g, t * P:(t + 1) * P], r_all[:, g, :],
                                        start=False, stop=(g == 1), skip_group_check=True)
                ins.then_inc(s0_ready.sem, 1)
                pe.wait_ge(xn_ready.sem, xn_ready.at(b, 2))
                turn(bank(0), xn).then_inc(xnT_ps.sem, 1)
                pe.wait_ge(xnT_ready.sem, xnT_ready.at(b, 2))
                for t in range(NT):
                    ins = pe.matmul(bank(1)[:, t * E1:(t + 1) * E1], xnT[:, t * P:(t + 1) * P], wr[:, :],
                                    start=True, stop=True)
                ins.then_inc(logit_ps.sem, 1)
                pe.wait_ge(xn_ready.sem, xn_ready.at(b, 3))
                turn(bank(2), hn).then_inc(xnT_ps.sem, 1)
                pe.wait_ge(xnT_ready.sem, xnT_ready.at(b, 3))
                for t in range(NT):
                    ins = pe.matmul(mb[:, t // 2, (t % 2) * 2 * C:(t % 2 + 1) * 2 * C], hT[:, t * P:(t + 1) * P],
                                    qkvT[:, 0:2, :].rearrange("p a c -> p (a c)"), start=True, stop=True)
                ins.then_inc(qk_ps.sem, 1)
                pe.matmul(bank(3), qkvT[:, 2, :], hT, start=True, stop=True).then_inc(v_ps.sem, 1)
                pe.wait_ge(qk_ready.sem, qk_ready.at(b, 1))
                for t in range(NT):
                    ins = pe.matmul(tr[:, 0:C], qk[:, t, 0, :], qk[:, t, 1, :], start=(t == 0), stop=(t == NT - 1))
                ins.then_inc(cw_ps.sem, 1)
                pe.wait_ge(chosen_ready.sem, chosen_ready.at(b, 1))
                for t in range(NT):
                    for s in range(t + 1):
                        ins = pe.matmul(bank(1)[:, 64 + t * E1:64 + (t + 1) * E1], before[:, :] if s == t else ones_h[:, :],
                                        chosen[:, s, :], start=(s == 0), stop=(s == t))
                ins.then_inc(pos_ps.sem, 1)
                pe.wait_ge(cw_ready.sem, cw_ready.at(b, 1))
                pe.transpose(tr[:, 0:C], cw[:, :], ident[:, :]).then_inc(cwT_ps.sem, 1)
                pe.wait_ge(cwT_ready.sem, cwT_ready.at(b, 1))
                pe.wait_ge(vT_ready.sem, vT_ready.at(b, 1))
                pe.matmul(bank(2), cwT[:, :], vT, start=True, stop=True).then_inc(aT_ps.sem, 1)
                pe.wait_ge(one_hot_ready.sem, one_hot_ready.at(b, 1))
                for half in range(2):
                    for t in range(NT):
                        ins = pe.matmul(bank(half)[:, 0:4 * CAP], xn[:, t, :],
                                        one_hot[:, t, 4 * half:4 * half + 4, :].rearrange("p e s -> p (e s)"),
                                        start=(t == 0), stop=(t == NT - 1))
                    ins.then_inc(buf_ps.sem, 1)
                pe.wait_ge(aT_ready.sem, aT_ready.at(b, 1))
                for t in range(NT):
                    ins = pe.matmul(bank(3)[:, t * C:(t + 1) * C], aT[:, t * P:(t + 1) * P], projT[:, :],
                                    start=True, stop=True)
                ins.then_inc(proj_ps.sem, 1)

                def expert_up(e):
                    if e < 2:
                        pe.wait_ge(buf_ready.sem, buf_ready.at(b, 2))
                    else:
                        pe.wait_ge(hid_dve.sem, hid_dve.at(b, e - 1))
                    for m in range(HM1):
                        ins = pe.matmul(bank(e % 2)[:, m * CAP:(m + 1) * CAP], v1_all[:, e, m * P:(m + 1) * P],
                                        bufT[:, e, :], start=True, stop=True)
                    ins.then_inc(hid_ps.sem, 1)

                def back(e):
                    if e == 0:
                        pe.wait_ge(weighted_ready.sem, weighted_ready.at(b, 1))
                        pe.wait_ge(s1_ready.sem, s1_ready.at(b, 1))
                    if e >= 2:
                        pe.wait_ge(back_ready.sem, back_ready.at(b, e - 1))
                    for t in range(NT):
                        ins = pe.transpose(bank(2 + e % 2)[0:CAP, t * P:(t + 1) * P], weighted[:, t, e, :], ident[:, :])
                    ins.then_inc(back_ps.sem, 1)

                def expert_down(e):
                    pe.wait_ge(hid_dve.sem, hid_dve.at(b, e + 1))
                    for m in range(HM1):
                        ins = pe.matmul(mb[0:CAP, e // 4, (e % 4) * C:(e % 4 + 1) * C], hid[:, e % 2, m, :],
                                        v2_all[:, e, m, :], start=(m == 0), stop=(m == HM1 - 1))
                    if e % 4 == 3:
                        ins.then_inc(y_ps.sem, 1)

                expert_up(0)
                back(0)
                for e in range(1, E1):
                    expert_up(e)
                    back(e)
                    expert_down(e - 1)
                expert_down(E1 - 1)
                pe.wait_ge(back_ready.sem, back_ready.at(b, E1))
                pe.wait_ge(y_ready.sem, y_ready.at(b, 2))
                for t in range(NT):
                    for e in range(E1):
                        ins = pe.matmul(sa[:, t * C:(t + 1) * C], backT[:, e, t * P:(t + 1) * P], y_slots[:, e, :],
                                        start=(e == 0), stop=(e == E1 - 1))
                ins.then_inc(comb_ps.sem, 1)


class SetupStages:

    memk, memv, postT, cols = 7, 8, 9, 10
    act_postT, act_cols = 9, 10
    memr = 19
    b2turned, b2folded, qkvturned, biases = 28, 29, 30, 31
    act_memr = 23
    act_b2turned = 32

    def turned(self, w, half):
        return 2 * w + half + 1

    def fold(self, q):
        return 11 + q

    def act_fold(self, q):
        return 10 + 2 * (q + 1) if q < 4 else 18 + (q - 3)

    def w2turned(self, q):
        return 20 + 2 * q

    def w2folded(self, q):
        return 21 + 2 * q

    def act_w2(self, q):
        return 23 + 2 * (q + 1)


SU_ACT = 34
SU_DVE = 10

_INS = ["L0_attn_x", "L0_attn_Wq", "L0_attn_Wk", "L0_attn_Wv", "L0_attn_pre_proj", "L0_attn_post_proj",
        "L0_attn_mem_k", "L0_attn_mem_v", "L0_attn_Wo", "L0_attn_bo", "L0_ffn_W1", "L0_ffn_b1", "L0_ffn_W3",
        "L0_ffn_b3", "L0_ffn_W2", "L0_ffn_b2", "L0_ffn_Wg", "L0_ffn_bg", "L0_ffn_Wf", "L0_ffn_bf",
        "L1_attn_norm_w", "L1_attn_norm_b", "L1_attn_qkv_w", "L1_attn_qkv_b", "L1_attn_proj_w",
        "L1_attn_proj_b", "L1_ffn_Wr", "L1_ffn_W1", "L1_ffn_b1", "L1_ffn_W2", "L1_ffn_b2"]

_BY_PARTITION = ("L0_ffn_b1", "L0_ffn_b3", "L1_ffn_b1")


def kernel(**inputs):
    import concourse.bacc as bacc
    from concourse.bass_utils import run_bass_kernel_spmd

    nc = bacc.Bacc("TRN2", target_bir_lowering=False, num_devices=1)
    arrays, args = {}, []
    for name in _INS:
        a = np.asarray(inputs[name])
        if name in _BY_PARTITION:
            a = a.reshape(a.shape[0], -1, P).transpose(2, 0, 1)
        a = np.ascontiguousarray(a)
        arrays[name] = a
        args.append(nc.dram_tensor(name, a.shape, mybir.dt.from_np(a.dtype), kind="ExternalInput").ap())
    args.append(nc.dram_tensor("out", (B, T, C), F32, kind="ExternalOutput").ap())
    build(nc, *args)
    r = run_bass_kernel_spmd(nc, [arrays], core_ids=[0])
    return r.results[0]["out"]
```

```python
from contextlib import ExitStack

import numpy as np

import concourse.bass as bass
from concourse import mybir

F32 = mybir.dt.float32
F32R = mybir.dt.float32r
BF16 = mybir.dt.bfloat16
ALU = mybir.AluOpType
ACT = mybir.ActivationFunctionType
AX = mybir.AxisListType

P = 128
B, T, C = 8, 512, 128
NT = T // P
H, DH, NM = 16, 64, 16
HC = H * DH // P
NIT = H // 2
E0, HID0 = 8, 256
E1, HID1 = 8, 512
HM1 = HID1 // P
CAP = int(T / E1 * 1.25)
EPS = 1e-5
MASKED = -3.3895313892515355e38
KEYS = NM + T
UNITS = 2 * NT
MISCS = ("keys1", "values0", "h1_0", "h3_0", "values1", "h1_1", "h3_1", "keys0", "out0", "out1")
MISC = len(MISCS)
PARTS = ((0, 0), (0, 1), (1, 0))
START_AT = (1, 2, 3, 5, 6)
PE_START_AT = (1, 2, 5, 6)
assert E0 == NIT and C == P


class Signal:

    def __init__(self, sem, per_row, preset=0):
        self.sem, self.per_row, self.preset = sem, per_row, preset

    def at(self, b, n):
        return b * self.per_row + (n + self.preset)


def build(nc, x, Wq, Wk, Wv, pre, post, mem_k, mem_v, Wo, bo, W1, b1, W3, b3, W2, b2, Wg, bg, Wf, bf,
          norm_w, norm_b, qkv_w, qkv_b, proj_w, proj_b, Wr, V1, c1, V2, c2, out):
    with ExitStack() as ctx:
        def sb(name, shape, dt=F32):
            return ctx.enter_context(nc.sbuf_tensor(name, shape, dt))

        def ps(name, shape):
            return ctx.enter_context(nc.psum_tensor(name, shape, F32))

        def sem(name):
            return ctx.enter_context(nc.semaphore(name))

        sc = ps("sc", [P, 4, 512])
        tr = ps("tr", [P, 512])
        sa = ps("sa", [P, 512])
        mb = ps("mb", [P, 2, 512])

        x_next = sb("x_next", [P, NT, C])
        mt_all = sb("mt_all", [P, NIT + 1, 2, C])
        n_all = sb("n_all", [P, NIT, 2, C])
        g_all = sb("g_all", [P, NIT + 1, 2, NM])
        r_all = sb("r_all", [P, 2, C])
        w13_all = sb("w13_all", [P, E0 + 1, 2, HID0])
        w2f = sb("w2f", [P, E0, 2, C])
        b1c = sb("b1c", [P, E0, 2])
        b3c = sb("b3c", [P, E0, 2])
        b2f = sb("b2f", [E0 + 1, C])
        wg = sb("wg", [P, E0])
        bg_b = sb("bg_b", [P, E0])
        bo_row = sb("bo_row", [1, 1, C])
        ones_row = sb("ones_row", [1, P])
        v1_all = sb("v1_all", [P, E1, HID1])
        v2_all = sb("v2_all", [P, E1, HM1, C])
        c1c = sb("c1c", [P, E1, HM1])
        c2_b = sb("c2_b", [CAP, E1, C])
        qkvT = sb("qkvT", [P, 3, C])
        qk_bias = sb("qk_bias", [P, 2, C])
        v_bias = sb("v_bias", [P, 1])
        projT = sb("projT", [P, C])
        pb_b = sb("pb_b", [P, C])
        wr = sb("wr", [P, E1])
        ident = sb("ident", [P, P])
        ident_h = sb("ident_h", [P, P], BF16)
        causal = sb("causal", [P, P], BF16)
        before = sb("before", [P, P], BF16)
        ones_h = sb("ones_h", [P, P], BF16)
        slot_no = sb("slot_no", [P, CAP])
        ties0 = sb("ties0", [P, E0, E0])
        ties1 = sb("ties1", [P, E1, E1])
        neghalf = sb("neghalf", [P, NT])

        arena = sb("arena", [P, 8192])
        wq_raw, wk_raw, wv_raw = (v1_all[:, 2 * i:2 * i + 2, :].rearrange("p a n -> p (a n)") for i in range(3))
        wo_sb = arena[:, 0:1024].rearrange("p (c n) -> p c n", c=HC)
        wqT = arena[:, 1024:2048].rearrange("p (c n) -> p c n", c=HC)
        wkT = arena[:, 2048:3072].rearrange("p (c n) -> p c n", c=HC)
        wvT = arena[:, 3072:4096].rearrange("p (c n) -> p c n", c=HC)
        scaled = arena[:, 4096:8192].rearrange("p (c k n) -> p c k n", c=HC, k=4)
        one_hot = arena[:, 0:2560].rearrange("p (t e s) -> p t e s", t=NT, e=E1)
        weighted = arena[:, 2560:5120].rearrange("p (t e s) -> p t e s", t=NT, e=E1)
        y_slots = arena[0:CAP, 5120:6144].rearrange("p (e c) -> p e c", e=E1)

        xb = sb("xb", [P, NT, C])
        stats = sb("stats", [P, NT, 6])
        mv = sb("mv", [P, NT, 2])
        veps = sb("veps", [P, NT])
        rstd = sb("rstd", [P, NT])
        xn = sb("xn", [P, NT, C])
        xnT = sb("xnT", [P, T])
        gates = sb("gates", [P, NT, E0 + 1])
        gatesT = sb("gatesT", [E0 + 1, T])
        lg = sb("lg", [P, NT, E0])
        pr = sb("pr", [P, NT, E0])
        red = sb("red", [P, NT])
        cmpa = sb("cmpa", [P, NT, E0, E0])
        cmpb = sb("cmpb", [P, NT, E0, E0])
        rank = sb("rank", [P, NT, E0])
        facc = sb("facc", [P, NT, C])
        x_hl = sb("x_hl", [P, 2, T], F32R)
        m_hl = sb("m_hl", [P, 2, 2, C], F32R)
        w_hl = sb("w_hl", [P, 2, 2, HID0], F32R)
        k_hl = sb("k_hl", [P, 2, 2, KEYS], F32R)
        wv = sb("wv", [P, NT, 2, C])
        top8 = sb("top8", [P, 2, 8])
        nmax = sb("nmax", [P, 2])
        den = sb("den", [P, 2])
        rden = sb("rden", [P, 2])
        ex = sb("ex", [P, 2, KEYS])
        kept = sb("kept", [P, 2, KEYS])
        attn = sb("attn", [P, 2, T])
        attnT = sb("attnT", [P, 2, T])
        attn_mem = sb("attn_mem", [P, NT, H, NM])
        memT = sb("memT", [P, 2, T])
        h1 = sb("h1", [P, 2, T])
        hu = sb("hu", [P, 2, T])
        ht = sb("ht", [P, 2, T])
        hh = sb("hh", [P, 2, T])
        x1 = sb("x1", [P, NT, C])
        sg = hh[:, 0, :].rearrange("p (t c) -> p t c", t=NT)
        hn = xb
        hT = attnT[:, 0, :]
        qk = attn[:, :, :].rearrange("p a (t k c) -> p (a t) k c", t=2, k=2)
        vT = hu[:, 1, :]
        backT = [a[0:CAP, i, :] for a, i in ((h1, 0), (h1, 1), (ht, 0), (ht, 1), (hu, 0), (hu, 1), (hh, 1), (attn, 0))]
        cw = sb("cw", [P, C])
        cwT = sb("cwT", [P, C])
        cmax = sb("cmax", [P, 1])
        csum = sb("csum", [P, 1])
        aT = attnT[:, 1, :]
        s1 = sb("s1", [P, NT, C])
        chosen = sb("chosen", [P, NT, E1], BF16)
        pos = sb("pos", [P, NT, E1])
        bufT = kept[:, :, :].rearrange("p a n -> p (a n)")[:, 0:E1 * CAP].rearrange("p (e s) -> p e s", e=E1)
        hid = ex[:, :, :].rearrange("p a n -> p (a n)")[:, 0:2 * HM1 * CAP].rearrange("p (a m s) -> p a m s", a=2, m=HM1)
        y_out = sb("y_out", [P, NT, C])

        loaded_a = sem("loaded_a")
        loaded_b = sem("loaded_b")
        consts = sem("consts")
        su_pe = sem("su_pe")
        su_act = sem("su_act")
        su_dve = sem("su_dve")
        x_loaded = Signal(sem("x_loaded"), 16)
        x_taken = Signal(sem("x_taken"), 1)
        def sig(name, per_row, preset=0):
            return Signal(sem(name), per_row, preset)

        mt_ready = [sig("mt0_ready", NIT, 1), sig("mt1_ready", NIT, 1)]
        w13_ready = sig("w13_ready", NIT * 4, 4)
        g_ready = [sig("g0_ready", NIT, 1), sig("g1_ready", NIT)]
        key0_ps = sig("key0_ps", 1)
        key0_high = sig("key0_high", 1)
        key0_ready = sig("key0_ready", 1)
        key_high = sig("key_high", NIT * 2)
        xhl_ready = sig("xhl_ready", 1)
        misc_ready = sig("misc_ready", NIT * MISC)
        misc_free = [sig(f"misc_free{i}", NIT * MISC // 2, 1) for i in range(2)]
        sc_ready = sig("sc_ready", NIT * UNITS)
        top_done = sig("top_done", NIT * UNITS)
        nmax_ready = sig("nmax_ready", NIT * UNITS)
        exp_done = sig("exp_done", NIT * UNITS)
        kept_ready = sig("kept_ready", NIT * UNITS, 2)
        rden_ready = sig("rden_ready", NIT * UNITS)
        attn_ready = sig("attn_ready", NIT * UNITS, 2)
        tr_ready = sig("tr_ready", NIT * UNITS, 2)
        attnT_ready = sig("attnT_ready", NIT * UNITS, 1)
        av_done = sig("av_done", NIT * UNITS, 2)
        th_ready = sig("th_ready", NIT * 2)
        hh_ready = sig("hh_ready", NIT * 2)
        mem_kept = sig("mem_kept", NIT * UNITS, 2)
        var_ready = sig("var_ready", 3)
        rstd_ready = sig("rstd_ready", 3)
        xn_ready = sig("xn_ready", 3)
        xnT_ps = sig("xnT_ps", 3)
        xnT_ready = sig("xnT_ready", 3)
        logit_ps = sig("logit_ps", 2)
        logit_ready = sig("logit_ready", 2)
        gexp_done = sig("gexp_done", 2)
        gates_ready = sig("gates_ready", 1)
        gatesT_ps = sig("gatesT_ps", 1)
        gatesT_ready = sig("gatesT_ready", 1)
        facc_ps = sig("facc_ps", 1)
        facc_ready = sig("facc_ready", 1)
        memT_ps = sig("memT_ps", 2)
        memT_ready = sig("memT_ready", 2)
        s0_ready = sig("s0_ready", 1)
        gate_tanh = sig("gate_tanh", 3)
        x1_ready = sig("x1_ready", 1)
        qk_ps = sig("qk_ps", 1)
        qk_ready = sig("qk_ready", 1)
        v_ps = sig("v_ps", 1)
        vT_ready = sig("vT_ready", 1)
        cw_ps = sig("cw_ps", 1)
        cmax_ready = sig("cmax_ready", 1)
        cexp_done = sig("cexp_done", 1)
        cw_ready = sig("cw_ready", 1)
        cwT_ps = sig("cwT_ps", 1)
        cwT_ready = sig("cwT_ready", 1)
        aT_ps = sig("aT_ps", 1)
        aT_ready = sig("aT_ready", 1)
        proj_ps = sig("proj_ps", 1)
        s1_ready = sig("s1_ready", 1)
        chosen_ready = sig("chosen_ready", 1)
        pos_ps = sig("pos_ps", 1)
        one_hot_ready = sig("one_hot_ready", NT)
        weighted_ready = sig("weighted_ready", 1)
        buf_ps = sig("buf_ps", 2)
        buf_ready = sig("buf_ready", 2)
        back_ps = sig("back_ps", E1)
        back_ready = sig("back_ready", E1)
        hid_ps = sig("hid_ps", E1)
        hid_ready = sig("hid_ready", E1)
        y_ps = sig("y_ps", 2)
        y_ready = sig("y_ready", 2)
        comb_ps = sig("comb_ps", 2)
        out_ready = sig("out_ready", 1, 1)
        stored = Signal(sem("stored"), 16, 16)

        block = ctx.enter_context(nc.Block())

        def score_slot(u, t):
            n = NM + P * (t + 1)
            at = 0 if n <= 512 else 512 - NM - 256
            flat = sc[:, 2 * (u % 2):2 * (u % 2) + 2, :].rearrange("p a n -> p (a n)")
            return flat[:, at:at + n], n

        def bank(i):
            return sc[:, i, :]

        def misc_done(b, it, name):
            return misc_ready.sem, misc_ready.at(b, it * MISC + MISCS.index(name) + 1)

        def misc_left(b, it, name):
            n = MISCS.index(name)
            return misc_free[n % 2].sem, misc_free[n % 2].at(b, it * (MISC // 2) + n // 2 + 1)

        N_A, N_B = 10, 23

        @block.sync
        def _(sp):
            sp.dma_start(wq_raw, Wq).then_inc(loaded_a, 16)
            sp.dma_start(wk_raw, Wk).then_inc(loaded_a, 16)
            sp.dma_start(wv_raw, Wv).then_inc(loaded_a, 16)
            sp.dma_start(wo_sb, Wo.rearrange("(c p) n -> p c n", p=P)).then_inc(loaded_a, 16)
            for a in range(2):
                sp.dma_start((x1, s1)[a][0:NM, :, :].rearrange("m t c -> m (t c)").rearrange("m (h d) -> m h d", d=DH),
                             mem_k[a * H // 2:(a + 1) * H // 2].rearrange("h m d -> m h d")).then_inc(loaded_a, 16)
            sp.dma_start(wv[0:NM, :, :, :].rearrange("m t k c -> m (t k c)").rearrange("m (h d) -> m h d", d=DH),
                         mem_v.rearrange("h m d -> m h d")).then_inc(loaded_a, 16)
            sp.dma_start(kept[0:H, 0, 0:H], pre).then_inc(loaded_a, 16)
            sp.dma_start(kept[0:H, 1, 0:H], post).then_inc(loaded_a, 16)
            sp.dma_start(hh[:, 0, 0:C], Wf).then_inc(loaded_a, 16)
            sp.dma_start(x_next[:, :, :], x[0].rearrange("(t p) c -> p t c", p=P)).then_inc(x_loaded.sem, 16)
            n = 0

            def load(dst, src):
                nonlocal n
                sp.dma_start(dst, src).then_inc(loaded_b, 16)
                n += 1
            load(attn_mem[:, :, :, :].rearrange("p t h m -> p (t h m)").rearrange("p (e m o) -> p e m o", e=4, m=2),
                 W2[0:4].rearrange("e (m p) o -> p e m o", p=P))
            load(memT[:, :, :].rearrange("p a n -> p (a n)").rearrange("p (e m o) -> p e m o", e=4, m=2),
                 W2[4:8].rearrange("e (m p) o -> p e m o", p=P))
            load(w13_all[:, 0:E0, 0, :], W1.rearrange("e c h -> c e h"))
            load(w13_all[:, 0:E0, 1, :], W3.rearrange("e c h -> c e h"))
            load(w13_all[:, E0, 0, :], W1[0])
            load(w13_all[:, E0, 1, :], W3[0])
            load(hu[0:E0, 0, 0:C], b2)
            load(b2f[E0:E0 + 1, :], bf.rearrange("(a n) -> a n", a=1))
            load(wg[:, :], Wg)
            load(bg_b[:, :], bg.rearrange("(a n) -> a n", a=1).partition_broadcast(P))
            load(bo_row[:, 0, :], bo.rearrange("(a n) -> a n", a=1))
            load(b1c[:, :, :], b1)
            load(b3c[:, :, :], b3)
            load(qk[:, 0:3, 0, :], qkv_w.rearrange("(a p) c -> p a c", p=P))
            load(qk[:, 3, 0, :], proj_w)
            load(cmax[:, :], norm_w.rearrange("(p a) -> p a", a=1))
            load(csum[:, :], norm_b.rearrange("(p a) -> p a", a=1))
            load(qk_bias[:, :, :].rearrange("p a c -> p (a c)"),
                 qkv_b[0:2 * C].rearrange("(a n) -> a n", a=1).partition_broadcast(P))
            load(v_bias[:, :], qkv_b[2 * C:3 * C].rearrange("(p a) -> p a", a=1))
            load(pb_b[:, :], proj_b.rearrange("(a n) -> a n", a=1).partition_broadcast(P))
            load(wr[:, :], Wr)
            sp.wait_ge(su_act, 6)
            load(v1_all[:, :, :], V1.rearrange("e c h -> c e h"))
            load(v2_all[:, :, :, :], V2.rearrange("e (m p) c -> p e m c", p=P))
            assert n == N_B
            sp.dma_start(c1c[:, :, :], c1).then_inc(loaded_b, 16)
            sp.dma_start(c2_b[:, :, :].rearrange("p e c -> p (e c)"),
                         c2.rearrange("e c -> (e c)").rearrange("(a n) -> a n", a=1).partition_broadcast(CAP)
                         ).then_inc(loaded_b, 16)
            def store(b, row):
                sp.wait_ge(out_ready.sem, out_ready.at(b, 1))
                sp.dma_start(row.rearrange("(t p) c -> p t c", p=P), y_out[:, :, :]).then_inc(stored.sem, 16)

            with sp.Fori(0, B - 1) as b:
                sp.wait_ge(x_taken.sem, x_taken.at(b, 1))
                sp.dma_start(x_next[:, :, :], x[bass.ds(b + 1, 1)].rearrange("o (t p) c -> p (o t) c", p=P)
                             ).then_inc(x_loaded.sem, 16)
                store(b, out[bass.ds(b, 1)].rearrange("o t c -> (o t) c"))
            sp.wait_ge(x_taken.sem, x_taken.at(B - 1, 1))
            sp.dma_start(x_next[:, :, :], x[0].rearrange("(t p) c -> p t c", p=P)).then_inc(x_loaded.sem, 16)
            store(B - 1, out[B - 1])
            sp.wait_ge(stored.sem, stored.at(B - 1, 16))

        N_B += 2

        @block.gpsimd
        def _(pool):
            pool.memset(ident[:, :], 0.0)
            pool.memset(ident_h[:, :], 0.0)
            pool.memset(causal[:, :], 0.0)
            pool.memset(before[:, :], 1.0)
            pool.memset(ones_h[:, :], 1.0)
            pool.memset(ties0[:, :, :], 1.0)
            pool.memset(ties1[:, :, :], 1.0)
            pool.memset(neghalf[:, :], -0.5)
            pool.memset(ones_row[:, :], 1.0)
            pool.memset(gates[:, :, :], 1.0)
            pool.memset(ex[0:H, 0, 0:512], 0.0)
            pool.memset(ex[0:H, 1, 0:512], 0.0)
            pool.iota(slot_no[:, :], pattern=[[1, CAP]], base=0, channel_multiplier=0,
                      allow_small_or_imprecise_dtypes=True)
            pool.drain()
            for m in (ident, ident_h):
                pool.affine_select(out=m[:, :], in_=m[:, :], compare_op=ALU.not_equal, fill=1.0,
                                   base=0, pattern=[[-1, P]], channel_multiplier=1)
            pool.affine_select(out=causal[:, :], in_=causal[:, :], compare_op=ALU.is_ge, fill=MASKED,
                               base=0, pattern=[[-1, P]], channel_multiplier=1)
            pool.affine_select(out=before[:, :], in_=before[:, :], compare_op=ALU.is_gt, fill=0.0,
                               base=0, pattern=[[1, P]], channel_multiplier=-1)
            pool.affine_select(out=ties0[:, :, :], in_=ties0[:, :, :], compare_op=ALU.is_gt, fill=0.0,
                               base=0, pattern=[[-1, E0], [1, E0]], channel_multiplier=0)
            pool.affine_select(out=ties1[:, :, :], in_=ties1[:, :, :], compare_op=ALU.is_gt, fill=0.0,
                               base=0, pattern=[[1, E1], [-1, E1]], channel_multiplier=0)
            for half in range(2):
                sel = ex[0:H, half, 0:512].rearrange("h (c two d) -> h c two d", c=4, two=2)
                pool.affine_select(out=sel, in_=sel, compare_op=ALU.not_equal, fill=1.0, base=-8 * half,
                                   pattern=[[-2, 4], [-1, 2], [0, DH]], channel_multiplier=1)
            pool.drain()
            pool.memset(neghalf[:, :], -0.5).then_inc(consts, 1)
            pool.wait_ge(su_dve, SU_DVE)
            pool.wait_ge(su_act, SU_ACT)
            pool.wait_ge(loaded_b, 16 * N_B)

            def split(dst, src):
                pool.tensor_copy(dst[0], src)
                pool.drain()
                return pool.tensor_tensor(dst[1], src, dst[0], ALU.subtract)

            for k in range(2):
                split([m_hl[:, i, k, :] for i in range(2)], mt_all[:, 0, k, :]).then_inc(mt_ready[k].sem, 1)
            split([w_hl[:, i, :, :] for i in range(2)], w13_all[:, 0, :, :]).then_inc(w13_ready.sem, 4)
            split([k_hl[:, i, 0, 0:NM] for i in range(2)], g_all[:, 0, 0, :]).then_inc(g_ready[0].sem, 1)

            def root(b, n):
                pool.wait_ge(var_ready.sem, var_ready.at(b, n))
                pool.tensor_tensor(rstd[:, :], veps[:, :], neghalf[:, :], ALU.pow).then_inc(rstd_ready.sem, 1)

            root(0, 1)
            with pool.Fori(0, B) as b:

                def normalise(it, u):
                    t, n = u % NT, it * UNITS + u + 1
                    pool.wait_ge(rden_ready.sem, rden_ready.at(b, n))
                    pool.wait_ge(tr_ready.sem, tr_ready.at(b, n - 2))
                    pool.nop(nofuse=True)
                    pool.tensor_scalar(attn[:, u % 2, 0:P * (t + 1)], kept[:, u % 2, NM:NM + P * (t + 1)],
                                       rden[:, u % 2:u % 2 + 1], 1.0, ALU.mult, ALU.mult
                                       ).then_inc(attn_ready.sem, 1)

                def next_m(it, k):
                    pool.nop(nofuse=True)
                    split([m_hl[:, i, k:k + 1, :] for i in range(2)], mt_all[:, bass.ds(it + 1, 1), k, :]
                          ).then_inc(mt_ready[k].sem, 1)

                def next_w13(it, side, m):
                    pool.wait_ge(*misc_done(b, it, ("h1_", "h3_")[side] + str(m)))
                    pool.nop(nofuse=True)
                    split([w_hl[:, i, side:side + 1, m * P:(m + 1) * P] for i in range(2)],
                          w13_all[:, bass.ds(it + 1, 1), side, m * P:(m + 1) * P]).then_inc(w13_ready.sem, 1)

                def step(it, first=False):
                    if first:
                        pool.wait_ge(key0_ps.sem, key0_ps.at(b, 1))
                    else:
                        pool.wait_ge(*misc_done(b, it - 1, "keys0"))
                    next_m(it, 0)
                    if not first:
                        pool.wait_ge(sc_ready.sem, sc_ready.at(b, it * UNITS))
                    pool.nop(nofuse=True)
                    split([k_hl[:, i, 1:2, 0:NM] for i in range(2)], g_all[:, bass.ds(it, 1), 1, :]
                          ).then_inc(g_ready[1].sem, 1)
                    normalise(it, 0)
                    pool.wait_ge(*misc_done(b, it, "keys1"))
                    next_m(it, 1)
                    normalise(it, 1)
                    next_w13(it, 0, 0)
                    normalise(it, 2)
                    next_w13(it, 1, 0)
                    normalise(it, 3)
                    split([k_hl[:, i, 0:1, 0:NM] for i in range(2)], g_all[:, bass.ds(it + 1, 1), 0, :]
                          ).then_inc(g_ready[0].sem, 1)
                    normalise(it, 4)
                    next_w13(it, 0, 1)
                    normalise(it, 5)
                    next_w13(it, 1, 1)
                    normalise(it, 6)
                    normalise(it, 7)

                step(0, first=True)
                with pool.Fori(1, NIT) as it:
                    step(it)
                root(b, 2)
                root(b, 3)
                for t in range(NT):
                    pool.wait_ge(one_hot_ready.sem, one_hot_ready.at(b, t + 1))
                    ins = pool.tensor_tensor(weighted[:, t, :, :], one_hot[:, t, :, :],
                                             pr[:, t, :].unsqueeze(2).to_broadcast([P, E1, CAP]), ALU.mult)
                ins.then_inc(weighted_ready.sem, 1)
                root(b + 1, 1)

        @block.scalar
        def _(act):
            step = [0]

            def setup_copy(dst, src, pe_stage, scale=None):
                act.wait_ge(su_pe, pe_stage)
                ins = act.activation(dst, src, ACT.Copy, scale=1.0 if scale is None else scale)
                step[0] += 1
                ins.then_inc(su_act, 1)

            stages = SetupStages()
            for w, dst in ((0, wqT), (1, wkT), (2, wvT)):
                for half in range(2):
                    setup_copy(dst[:, 4 * half:4 * half + 4, :],
                               bank(2 * (w % 2) + half).rearrange("p (c n) -> p c n", c=4), stages.turned(w, half))
            setup_copy(h1[:, 0, 0:HC * NM], mb[:, 0, 0:HC * NM], stages.memk)
            setup_copy(h1[:, 1, 0:HC * NM], mb[:, 1, 0:HC * NM], stages.memv)
            setup_copy(ht[0:H, 0, 0:H], tr[0:H, 0:H], stages.postT)
            setup_copy(ht[:, 1, 0:2 * HC * H], sa[:, 0:2 * HC * H], stages.cols)
            for q in range(4):
                setup_copy(mt_all[:, 2 * q:2 * q + 2, :, :].rearrange("p a k c -> p (a k c)"), bank(q % 2), stages.fold(q))
                setup_copy(g_all[:, 2 * q:2 * q + 2, :, :].rearrange("p a k m -> p (a k m)"),
                           bank(2 + q % 2)[:, 0:4 * NM], stages.fold(q))
            for q in range(4):
                setup_copy(n_all[:, 2 * q:2 * q + 2, :, :].rearrange("p a k c -> p (a k c)"), bank(q % 2),
                           stages.fold(4 + q))
            setup_copy(r_all[:, :, :].rearrange("p a c -> p (a c)"), bank(2)[:, 0:2 * C], stages.memr)
            for q in range(4):
                setup_copy(h1[:, q % 2, :], mb[:, q % 2, :], stages.w2turned(q))
                setup_copy(w2f[:, 2 * q:2 * q + 2, :, :].rearrange("p e m c -> p (e m c)"), bank(q % 2),
                           stages.w2folded(q), scale=0.5)
            setup_copy(xnT[:, 0:E0], tr[:, 0:E0], stages.b2turned)
            setup_copy(b2f[0:E0, :], bank(2)[0:E0, 0:C], stages.b2folded)
            setup_copy(hT, bank(3), stages.qkvturned)
            assert step[0] == SU_ACT

            def evacuate(b, it, name, dst, bias=None):
                act.wait_ge(*misc_done(b, it, name))
                n = MISCS.index(name) % 2
                if bias is None:
                    ins = act.activation(dst, mb[:, n, :], ACT.Copy)
                else:
                    ins = act.activation(dst, mb[:, n, :], ACT.Identity, bias=bias)
                return ins

            def row_start(b):
                act.wait_ge(xnT_ps.sem, xnT_ps.at(b, 1))
                act.activation(xnT[:, :], tr[:, :], ACT.Copy).then_inc(xnT_ready.sem, 1)
                yield
                act.wait_ge(key0_ps.sem, key0_ps.at(b, 1))
                act.activation(k_hl[:, 0, 0, NM:KEYS], sa[:, :], ACT.Copy).then_inc(key0_high.sem, 1)
                yield
                act.wait_ge(logit_ready.sem, logit_ready.at(b, 1))
                act.activation(pr[:, :, :], lg[:, :, :], ACT.Exp).then_inc(gexp_done.sem, 1)
                yield
                act.wait_ge(gatesT_ps.sem, gatesT_ps.at(b, 1))
                act.activation(gatesT[:, :], tr[0:E0 + 1, :], ACT.Copy).then_inc(gatesT_ready.sem, 1)
                yield
                act.wait_ge(facc_ps.sem, facc_ps.at(b, 1))
                act.activation(facc[:, :, :].rearrange("p t c -> p (t c)"), tr[:, :], ACT.Copy
                               ).then_inc(facc_ready.sem, 1)
                yield

            for _part in row_start(0):
                pass
            with act.Fori(0, B) as b:
                def value_keys(it, k):
                    evacuate(b, it, f"keys{k}", k_hl[:, 0, k, NM:KEYS]).then_inc(key_high.sem, 1)

                def hidden1(it, m):
                    evacuate(b, it, f"h1_{m}", h1[:, m, :], b1c[:, bass.ds(it, 1), m]
                             ).then_inc(misc_free[MISCS.index(f"h1_{m}") % 2].sem, 1)

                def exps(it, u):
                    t, n = u % NT, it * UNITS + u + 1
                    src, w = score_slot(u, t)
                    act.wait_ge(nmax_ready.sem, nmax_ready.at(b, n))
                    act.activation(ex[:, u % 2, 0:w], src, ACT.Exp, bias=nmax[:, u % 2:u % 2 + 1]
                                   ).then_inc(exp_done.sem, 1)

                def values(it, k, first):
                    if not (first and k == 0):
                        act.wait_ge(av_done.sem, av_done.at(b, it * UNITS + (k - 1) * NT))
                    evacuate(b, it, f"values{k}", wv[:, :, k, :]
                             ).then_inc(misc_free[MISCS.index(f"values{k}") % 2].sem, 1)

                def turned(it, u):
                    t, n = u % NT, it * UNITS + u + 1
                    act.wait_ge(rden_ready.sem, rden_ready.at(b, n))
                    act.activation(attn_mem[:, t, bass.ds(2 * it + u // NT, 1), :],
                                   kept[:, u % 2:u % 2 + 1, 0:NM], ACT.Copy, scale=rden[:, u % 2:u % 2 + 1]
                                   ).then_inc(mem_kept.sem, 1)
                    act.wait_ge(tr_ready.sem, tr_ready.at(b, n))
                    act.wait_ge(av_done.sem, av_done.at(b, n - 2))
                    act.activation(attnT[:, u % 2, 0:P * (t + 1)], tr[:, 0:P * (t + 1)], ACT.Copy
                                   ).then_inc(attnT_ready.sem, 1)

                def tanhs(it, m):
                    act.wait_ge(*misc_left(b, it, f"h3_{m}"))
                    act.activation(ht[:, m, :], hu[:, m, :], ACT.Tanh, scale=0.5).then_inc(th_ready.sem, 1)

                def step(it, first=False):
                    if not first:
                        turned(it, -2)
                    value_keys(it, 1)
                    exps(it, 0)
                    values(it, 0, first)
                    if not first:
                        turned(it, -1)
                    exps(it, 1)
                    hidden1(it, 0)
                    turned(it, 0)
                    exps(it, 2)
                    turned(it, 1)
                    exps(it, 3)
                    tanhs(it, 0)
                    values(it, 1, first)
                    turned(it, 2)
                    exps(it, 4)
                    hidden1(it, 1)
                    turned(it, 3)
                    exps(it, 5)
                    tanhs(it, 1)
                    value_keys(it, 0)
                    turned(it, 4)
                    exps(it, 6)
                    turned(it, 5)
                    exps(it, 7)

                step(0, first=True)
                with act.Fori(1, NIT) as it:
                    step(it)
                turned(NIT, -2)
                turned(NIT, -1)
                act.wait_ge(*misc_left(b, NIT - 1, "out1"))
                act.activation(sg[:, :, :], facc[:, :, :], ACT.Tanh, scale=0.5).then_inc(gate_tanh.sem, 1)
                for g in range(2):
                    act.wait_ge(memT_ps.sem, memT_ps.at(b, g + 1))
                    act.activation(memT[:, g, :], bank(g), ACT.Copy).then_inc(memT_ready.sem, 1)
                act.wait_ge(xnT_ps.sem, xnT_ps.at(b, 2))
                act.activation(xnT[:, :], bank(0), ACT.Copy).then_inc(xnT_ready.sem, 1)
                act.wait_ge(logit_ready.sem, logit_ready.at(b, 2))
                act.activation(pr[:, :, :], lg[:, :, :], ACT.Exp).then_inc(gexp_done.sem, 1)
                act.wait_ge(xnT_ps.sem, xnT_ps.at(b, 3))
                act.activation(hT, bank(2), ACT.Copy).then_inc(xnT_ready.sem, 1)
                act.wait_ge(v_ps.sem, v_ps.at(b, 1))
                act.activation(vT, bank(3), ACT.Identity, bias=v_bias[:, 0:1]).then_inc(vT_ready.sem, 1)
                act.wait_ge(cmax_ready.sem, cmax_ready.at(b, 1))
                act.activation(cw[:, :], tr[:, 0:C], ACT.Exp, bias=cmax[:, 0:1], scale=float(1.0 / np.sqrt(T))
                               ).then_inc(cexp_done.sem, 1)
                act.wait_ge(cwT_ps.sem, cwT_ps.at(b, 1))
                act.activation(cwT[:, :], tr[:, 0:C], ACT.Copy).then_inc(cwT_ready.sem, 1)
                act.wait_ge(aT_ps.sem, aT_ps.at(b, 1))
                act.activation(aT, bank(2), ACT.Copy).then_inc(aT_ready.sem, 1)
                for half in range(2):
                    act.wait_ge(buf_ps.sem, buf_ps.at(b, half + 1))
                    act.activation(bufT[:, 4 * half:4 * half + 4, :].rearrange("p e s -> p (e s)"),
                                   bank(half)[:, 0:4 * CAP], ACT.Copy).then_inc(buf_ready.sem, 1)
                start = row_start(b + 1)
                for e in range(E1):
                    act.wait_ge(hid_ps.sem, hid_ps.at(b, e + 1))
                    for m in range(HM1):
                        ins = act.activation(hid[:, e % 2, m, :], bank(e % 2)[:, m * CAP:(m + 1) * CAP], ACT.Relu,
                                             bias=c1c[:, e, m:m + 1])
                    ins.then_inc(hid_ready.sem, 1)
                    act.wait_ge(back_ps.sem, back_ps.at(b, e + 1))
                    act.activation(backT[e], bank(2 + e % 2)[0:CAP, :], ACT.Copy).then_inc(back_ready.sem, 1)
                    if e in START_AT:
                        next(start)
                for half, z in enumerate((sa[:, 0:2 * C], bank(0)[:, 0:2 * C])):
                    act.wait_ge(comb_ps.sem, comb_ps.at(b, half + 1))
                    act.activation(sg[:, 2 * half:2 * half + 2, :].rearrange("p t c -> p (t c)"), z, ACT.Tanh, scale=0.5
                                   ).then_inc(gate_tanh.sem, 1)

        @block.vector
        def _(dve):
            stages = SetupStages()
            pre_col = ht[:, 1, 0:HC * H].rearrange("p (c h) -> p c h", c=HC)
            post_col = ht[:, 1, HC * H:2 * HC * H].rearrange("p (c h) -> p c h", c=HC)
            dve.wait_ge(su_act, stages.act_cols)
            dve.wait_ge(loaded_a, 16 * N_A)
            for q in range(4):
                if q:
                    dve.wait_ge(su_pe, stages.fold(q - 1))
                for k in range(4):
                    col = pre_col[:, :, 4 * q + k:4 * q + k + 1].to_broadcast([P, HC, C])
                    ins = dve.scalar_tensor_tensor(out=scaled[:, :, k, :], in0=wqT, scalar=float(DH) ** -0.5,
                                                   in1=col, op0=ALU.mult, op1=ALU.mult)
                ins.then_inc(su_dve, 1)
            for q in range(4):
                dve.wait_ge(su_pe, stages.fold(3 + q))
                for k in range(4):
                    col = post_col[:, :, 4 * q + k:4 * q + k + 1].to_broadcast([P, HC, C])
                    ins = dve.tensor_tensor(scaled[:, :, k, :], wo_sb, col, ALU.mult)
                ins.then_inc(su_dve, 1)
            dve.wait_ge(su_pe, stages.fold(7))
            mem_scaled = scaled[:, :, :, :].rearrange("p c k n -> p c (k n)")[:, :, 0:H * NM].rearrange(
                "p c (h m) -> p c h m", h=H)
            memvT = h1[:, 1, 0:HC * NM].rearrange("p (c m) -> p c m", c=HC)
            for c in range(HC):
                ins = dve.tensor_tensor(mem_scaled[:, c, :, :], memvT[:, c, :].unsqueeze(1).to_broadcast([P, H, NM]),
                                        post_col[:, c, :].unsqueeze(2).to_broadcast([P, H, NM]), ALU.mult)
            ins.then_inc(su_dve, 1)
            dve.wait_ge(su_pe, stages.biases)
            dve.wait_ge(su_act, SU_ACT)
            dve.wait_ge(loaded_b, 16 * N_B)
            dve.tensor_tensor(qk_bias[:, :, :].rearrange("p a c -> p (a c)"), bank(0)[:, 0:2 * C],
                              qk_bias[:, :, :].rearrange("p a c -> p (a c)"), ALU.add)
            dve.tensor_tensor(v_bias[:, :], bank(1)[:, 0:1], v_bias[:, :], ALU.add)
            dve.tensor_scalar(qkvT[:, :, :].rearrange("p a c -> p (a c)"), hT[:, 0:3 * C], cmax[:, 0:1], None, ALU.mult)
            dve.tensor_copy(projT[:, :], hT[:, 3 * C:4 * C])
            dve.tensor_copy(mt_all[:, NIT, :, :], mt_all[:, 0, :, :])
            dve.tensor_copy(g_all[:, NIT, :, :], g_all[:, 0, :, :])
            dve.drain()
            for s in (misc_free[0], misc_free[1], kept_ready, attn_ready, tr_ready, attnT_ready, av_done,
                      mem_kept, out_ready, stored):
                dve.memset(den[:, 0:1], 0.0).then_inc(s.sem, s.preset)
                dve.drain()
            dve.memset(den[:, 1:2], 0.0).then_inc(su_dve, 1)

            def variance(src):
                for t in range(NT):
                    dve.bn_stats(stats[:, t, :], src[:, t, :])
                dve.drain()
                for t in range(NT):
                    dve.bn_aggr(mv[:, t, :], stats[:, t, :])
                dve.drain()
                dve.tensor_scalar(veps[:, :], mv[:, :, 1], EPS, None, ALU.add).then_inc(var_ready.sem, 1)

            def normed(b, n, src, dst):
                dve.wait_ge(rstd_ready.sem, rstd_ready.at(b, n))
                for t in range(NT):
                    ins = dve.tensor_scalar(dst[:, t, :], src[:, t, :], mv[:, t, 0:1], rstd[:, t:t + 1],
                                            ALU.subtract, ALU.mult)
                ins.then_inc(xn_ready.sem, 1)

            def softmax_top2(b, n, logits, bias, ties):
                dve.wait_ge(logit_ps.sem, logit_ps.at(b, n))
                if bias is None:
                    dve.tensor_copy(lg[:, :, :], logits)
                else:
                    dve.tensor_tensor(lg[:, :, :], logits, bias[:, :].unsqueeze(1).to_broadcast([P, NT, E0]), ALU.add)
                dve.drain()
                dve.tensor_reduce(red[:, :], lg[:, :, :], AX.X, ALU.max)
                dve.drain()
                dve.tensor_tensor(lg[:, :, :], lg[:, :, :], red[:, :].unsqueeze(2).to_broadcast([P, NT, E0]),
                                  ALU.subtract).then_inc(logit_ready.sem, 1)
                dve.wait_ge(gexp_done.sem, gexp_done.at(b, n))
                dve.tensor_reduce(red[:, :], pr[:, :, :], AX.X, ALU.add)
                dve.drain()
                dve.reciprocal(red[:, :], red[:, :])
                dve.drain()
                dve.tensor_tensor(pr[:, :, :], pr[:, :, :], red[:, :].unsqueeze(2).to_broadcast([P, NT, E0]), ALU.mult)
                dve.drain()
                other = pr[:, :, :].unsqueeze(2).to_broadcast([P, NT, E0, E0])
                own = pr[:, :, :].unsqueeze(3).to_broadcast([P, NT, E0, E0])
                dve.tensor_tensor(cmpa[:, :, :, :], other, own, ALU.is_gt)
                dve.tensor_tensor(cmpb[:, :, :, :], other, own, ALU.is_equal)
                dve.drain()
                dve.tensor_tensor(cmpb[:, :, :, :], cmpb[:, :, :, :],
                                  ties[:, :, :].unsqueeze(1).to_broadcast([P, NT, E0, E0]), ALU.mult)
                dve.drain()
                dve.tensor_tensor(cmpa[:, :, :, :], cmpa[:, :, :, :], cmpb[:, :, :, :], ALU.add)
                dve.drain()
                dve.tensor_reduce(rank[:, :, :], cmpa[:, :, :, :], AX.X, ALU.add)
                dve.drain()
                dve.tensor_scalar(rank[:, :, :], rank[:, :, :], 1.5, None, ALU.is_lt)
                dve.drain()

            def gate(g, z):
                dve.scalar_tensor_tensor(out=g, in0=g, scalar=1.0, in1=z, op0=ALU.add, op1=ALU.mult)
                dve.drain()

            def gated(g, s, base, dst):
                dve.scalar_tensor_tensor(out=g, in0=g, scalar=0.5, in1=s, op0=ALU.mult, op1=ALU.mult)
                dve.drain()
                return dve.tensor_tensor(dst, g, base, ALU.add)

            def row_variance(b):
                dve.wait_ge(x_loaded.sem, x_loaded.at(b, 16))
                dve.tensor_copy(xb[:, :, :], x_next[:, :, :]).then_inc(x_taken.sem, 1)
                dve.drain()
                variance(xb)

            def row_gates(b):
                dve.wait_ge(xnT_ready.sem, xnT_ready.at(b, 1))
                dve.tensor_copy(x_hl[:, 0, :], xnT[:, :])
                dve.drain()
                dve.tensor_tensor(x_hl[:, 1, :], xnT[:, :], x_hl[:, 0, :], ALU.subtract).then_inc(xhl_ready.sem, 1)
                softmax_top2(b, 1, tr[:, 0:NT * E0].rearrange("p (t e) -> p t e", t=NT), bg_b, ties0)
                dve.tensor_tensor(gates[:, :, 0:E0], pr[:, :, :], rank[:, :, :], ALU.mult).then_inc(gates_ready.sem, 1)
                dve.wait_ge(key0_high.sem, key0_high.at(b, 1))
                dve.tensor_tensor(k_hl[:, 1, 0, NM:KEYS], sa[:, :], k_hl[:, 0, 0, NM:KEYS], ALU.subtract
                                  ).then_inc(key0_ready.sem, 1)

            row_variance(0)
            normed(0, 1, xb, xn)
            row_gates(0)
            with dve.Fori(0, B) as b:
                dve.wait_ge(facc_ready.sem, facc_ready.at(b, 1))
                dve.nop(nofuse=True)

                def top(it, u):
                    t, n = u % NT, it * UNITS + u + 1
                    src, w = score_slot(u, t)
                    dve.wait_ge(sc_ready.sem, sc_ready.at(b, n))
                    dve.nop(nofuse=True)
                    dve.max(top8[:, u % 2, :], src).then_inc(top_done.sem, 1)
                    dve.wait_ge(top_done.sem, top_done.at(b, n))
                    dve.tensor_scalar(nmax[:, u % 2:u % 2 + 1], top8[:, u % 2, 0:1], -1.0, None, ALU.mult
                                      ).then_inc(nmax_ready.sem, 1)

                def keep(it, u):
                    t, n = u % NT, it * UNITS + u + 1
                    src, w = score_slot(u, t)
                    dve.wait_ge(exp_done.sem, exp_done.at(b, n))
                    dve.wait_ge(attn_ready.sem, attn_ready.at(b, n - 2))
                    dve.wait_ge(mem_kept.sem, mem_kept.at(b, n - 2))
                    dve.scalar_tensor_tensor(out=kept[:, u % 2, 0:w], in0=src, scalar=top8[:, u % 2, 7:8],
                                             in1=ex[:, u % 2, 0:w], op0=ALU.is_ge, op1=ALU.mult,
                                             accum_out=den[:, u % 2:u % 2 + 1]).then_inc(kept_ready.sem, 1)
                    dve.wait_ge(kept_ready.sem, kept_ready.at(b, n))
                    dve.reciprocal(rden[:, u % 2:u % 2 + 1], den[:, u % 2:u % 2 + 1]).then_inc(rden_ready.sem, 1)

                def keys_low(it, k):
                    n = MISCS.index(f"keys{k}") % 2
                    dve.wait_ge(key_high.sem, key_high.at(b, it * 2 + 2 - k))
                    dve.nop(nofuse=True)
                    dve.tensor_tensor(k_hl[:, 1, k, NM:KEYS], mb[:, n, :], k_hl[:, 0, k, NM:KEYS], ALU.subtract
                                      ).then_inc(misc_free[n].sem, 1)

                def hidden3(it, m):
                    dve.wait_ge(*misc_done(b, it, f"h3_{m}"))
                    dve.wait_ge(*misc_left(b, it, f"h1_{m}"))
                    n = MISCS.index(f"h3_{m}") % 2
                    dve.scalar_tensor_tensor(out=hu[:, m, :], in0=mb[:, n, :], scalar=b3c[:, bass.ds(it, 1), m],
                                             in1=h1[:, m, :], op0=ALU.add, op1=ALU.mult
                                             ).then_inc(misc_free[n].sem, 1)

                def silu(it, m):
                    dve.wait_ge(th_ready.sem, th_ready.at(b, it * 2 + m + 1))
                    dve.scalar_tensor_tensor(out=hh[:, m, :], in0=ht[:, m, :], scalar=1.0, in1=hu[:, m, :],
                                             op0=ALU.add, op1=ALU.mult).then_inc(hh_ready.sem, 1)

                def experts_out(it, half):
                    dve.wait_ge(*misc_done(b, it, f"out{half}"))
                    n = MISCS.index(f"out{half}") % 2
                    for j in range(2):
                        t = 2 * half + j
                        ins = dve.scalar_tensor_tensor(
                            out=facc[:, t, :], in0=mb[:, n, j * C:(j + 1) * C], scalar=gates[:, t, bass.ds(it, 1)],
                            in1=facc[:, t, :], op0=ALU.mult, op1=ALU.add)
                    ins.then_inc(misc_free[n].sem, 1)

                def step(it):
                    top(it, 0)
                    keys_low(it, 1)
                    keep(it, 0)
                    top(it, 1)
                    keep(it, 1)
                    top(it, 2)
                    hidden3(it, 0)
                    keep(it, 2)
                    top(it, 3)
                    keep(it, 3)
                    top(it, 4)
                    silu(it, 0)
                    keep(it, 4)
                    top(it, 5)
                    hidden3(it, 1)
                    keep(it, 5)
                    silu(it, 1)
                    top(it, 6)
                    keys_low(it, 0)
                    keep(it, 6)
                    top(it, 7)
                    experts_out(it, 0)
                    experts_out(it, 1)
                    keep(it, 7)

                with dve.Fori(0, NIT) as it:
                    step(it)
                dve.wait_ge(gate_tanh.sem, gate_tanh.at(b, 1))
                gate(sg[:, :, :], facc[:, :, :])
                dve.wait_ge(s0_ready.sem, s0_ready.at(b, 1))
                gated(sg[:, :, :], sa[:, :].rearrange("p (t c) -> p t c", t=NT), xb[:, :, :], x1[:, :, :]
                      ).then_inc(x1_ready.sem, 1)
                dve.drain()
                variance(x1)
                normed(b, 2, x1, xn)
                dve.drain()
                variance(xn)
                normed(b, 3, xn, hn)
                softmax_top2(b, 2, bank(1)[:, 0:NT * E1].rearrange("p (t e) -> p t e", t=NT), None, ties1)
                dve.tensor_copy(chosen[:, :, :], rank[:, :, :]).then_inc(chosen_ready.sem, 1)
                dve.tensor_tensor(s1[:, :, :], xn[:, :, :], pb_b[:, :].unsqueeze(1).to_broadcast([P, NT, C]), ALU.add)
                dve.wait_ge(qk_ps.sem, qk_ps.at(b, 1))
                for j in range(2):
                    ins = dve.tensor_tensor(
                        qk[:, 2 * j:2 * j + 2, :, :].rearrange("p t a c -> p t (a c)"),
                        mb[:, j, :].rearrange("p (t n) -> p t n", t=2),
                        qk_bias[:, :, :].rearrange("p a c -> p (a c)").unsqueeze(1).to_broadcast([P, 2, 2 * C]), ALU.add)
                ins.then_inc(qk_ready.sem, 1)
                dve.wait_ge(pos_ps.sem, pos_ps.at(b, 1))
                dve.scalar_tensor_tensor(out=pos[:, :, :], in0=bank(1)[:, 64:64 + NT * E1].rearrange("p (t e) -> p t e", t=NT),
                                         scalar=1.0, in1=rank[:, :, :], op0=ALU.add, op1=ALU.mult)
                dve.drain()
                dve.tensor_scalar(pos[:, :, :], pos[:, :, :], -1.0, None, ALU.add)
                dve.drain()

                def one_hots(t):
                    dve.tensor_tensor(one_hot[:, t, :, :], slot_no[:, :].unsqueeze(1).to_broadcast([P, E1, CAP]),
                                      pos[:, t, :].unsqueeze(2).to_broadcast([P, E1, CAP]), ALU.is_equal
                                      ).then_inc(one_hot_ready.sem, 1)

                one_hots(0)
                dve.wait_ge(cw_ps.sem, cw_ps.at(b, 1))
                dve.tensor_reduce(cmax[:, :], tr[:, 0:C], AX.X, ALU.max)
                dve.drain()
                dve.tensor_scalar(cmax[:, :], cmax[:, :], float(-1.0 / np.sqrt(T)), None, ALU.mult
                                  ).then_inc(cmax_ready.sem, 1)
                one_hots(1)
                dve.wait_ge(cexp_done.sem, cexp_done.at(b, 1))
                dve.tensor_reduce(csum[:, :], cw[:, :], AX.X, ALU.add)
                dve.drain()
                dve.reciprocal(csum[:, :], csum[:, :])
                dve.drain()
                dve.tensor_scalar(cw[:, :], cw[:, :], csum[:, 0:1], None, ALU.mult).then_inc(cw_ready.sem, 1)
                one_hots(2)
                one_hots(3)
                row_variance(b + 1)
                dve.wait_ge(proj_ps.sem, proj_ps.at(b, 1))
                dve.tensor_tensor(s1[:, :, :].rearrange("p t c -> p (t c)"), bank(3),
                                  s1[:, :, :].rearrange("p t c -> p (t c)"), ALU.add).then_inc(s1_ready.sem, 1)
                dve.wait_ge(buf_ps.sem, buf_ps.at(b, 2))
                normed(b + 1, 1, xb, xn)
                dve.wait_ge(weighted_ready.sem, weighted_ready.at(b, 1))
                row_gates(b + 1)
                for half in range(2):
                    dve.wait_ge(y_ps.sem, y_ps.at(b, half + 1))
                    dve.tensor_tensor(y_slots[:, 4 * half:4 * half + 4, :].rearrange("p e c -> p (e c)"),
                                      mb[0:CAP, half, :],
                                      c2_b[:, 4 * half:4 * half + 4, :].rearrange("p e c -> p (e c)"), ALU.add
                                      ).then_inc(y_ready.sem, 1)
                dve.wait_ge(stored.sem, stored.at(b, 0))
                dve.nop(nofuse=True)
                for half, z in enumerate((sa[:, 0:2 * C], bank(0)[:, 0:2 * C])):
                    two = slice(2 * half, 2 * half + 2)
                    dve.wait_ge(gate_tanh.sem, gate_tanh.at(b, 2 + half))
                    gate(sg[:, two, :], z.rearrange("p (t c) -> p t c", t=2))
                    ins = gated(sg[:, two, :], s1[:, two, :], x1[:, two, :], y_out[:, two, :])
                ins.then_inc(out_ready.sem, 1)

        @block.tensor
        def _(pe):
            stages = SetupStages()
            pe.wait_ge(consts, 1)
            pe.wait_ge(loaded_a, 16 * N_A)
            count = [0]

            def done(ins, expected):
                count[0] += 1
                assert count[0] == expected, (count[0], expected)
                ins.then_inc(su_pe, 1)

            for w, raw in ((0, wq_raw), (1, wk_raw), (2, wv_raw)):
                if w == 2:
                    pe.wait_ge(su_act, 2)
                for half in range(2):
                    for j in range(4):
                        c = 4 * half + j
                        ins = pe.transpose(bank(2 * (w % 2) + half)[:, j * P:(j + 1) * P], raw[:, c * P:(c + 1) * P],
                                           ident[:, :])
                    done(ins, stages.turned(w, half))
            mk = [a[0:NM, :, :].rearrange("m t c -> m (t c)") for a in (x1, s1)]
            mv_flat = wv[0:NM, :, :, :].rearrange("m t k c -> m (t k c)")
            for c in range(HC):
                ins = pe.transpose(mb[:, 0, c * NM:(c + 1) * NM], mk[c // 4][:, (c % 4) * P:(c % 4 + 1) * P],
                                   ident[0:NM, 0:NM])
            done(ins, stages.memk)
            for c in range(HC):
                ins = pe.transpose(mb[:, 1, c * NM:(c + 1) * NM], mv_flat[:, c * P:(c + 1) * P], ident[0:NM, 0:NM])
            done(ins, stages.memv)
            done(pe.transpose(tr[0:H, 0:H], kept[0:H, 1, 0:H], ident[0:H, 0:H]), stages.postT)
            pe.wait_ge(su_act, stages.act_postT)
            for c in range(HC):
                sel = ex[0:H, c // 4, (c % 4) * P:(c % 4 + 1) * P]
                pe.matmul(sa[:, c * H:(c + 1) * H], sel, kept[0:H, 0, 0:H], start=True, stop=True)
                ins = pe.matmul(sa[:, (HC + c) * H:(HC + c + 1) * H], sel, ht[0:H, 0, 0:H], start=True, stop=True)
            done(ins, stages.cols)
            pe.wait_ge(su_act, stages.act_cols)
            for q in range(4):
                pe.wait_ge(su_dve, q + 1)
                if q >= 2:
                    pe.wait_ge(su_act, stages.act_fold(q - 2))
                for c in range(HC):
                    ins = pe.matmul(bank(q % 2), wkT[:, c, :], scaled[:, c, :, :].rearrange("p k n -> p (k n)"),
                                    start=(c == 0), stop=(c == HC - 1))
                for k in range(4):
                    for c in range(HC):
                        ins = pe.matmul(bank(2 + q % 2)[:, k * NM:(k + 1) * NM], scaled[:, c, k, :],
                                        h1[:, 0, c * NM:(c + 1) * NM], start=(c == 0), stop=(c == HC - 1))
                done(ins, stages.fold(q))
            for q in range(4):
                pe.wait_ge(su_dve, 4 + q + 1)
                pe.wait_ge(su_act, stages.act_fold(2 + q))
                for c in range(HC):
                    ins = pe.matmul(bank(q % 2), wvT[:, c, :], scaled[:, c, :, :].rearrange("p k n -> p (k n)"),
                                    start=(c == 0), stop=(c == HC - 1))
                done(ins, stages.fold(4 + q))
            pe.wait_ge(su_dve, 9)
            mem_scaled = scaled[:, :, :, :].rearrange("p c k n -> p c (k n)")
            for g in range(2):
                for c in range(HC):
                    ins = pe.matmul(bank(2)[:, g * C:(g + 1) * C], mem_scaled[:, c, g * P:(g + 1) * P], wo_sb[:, c, :],
                                    start=(c == 0), stop=(c == HC - 1))
            done(ins, stages.memr)
            pe.wait_ge(loaded_b, 16 * N_B)
            pe.wait_ge(su_act, stages.act_memr)
            for q in range(4):
                w2raw = (attn_mem[:, :, :, :].rearrange("p t h m -> p (t h m)") if q < 2
                         else memT[:, :, :].rearrange("p a n -> p (a n)"))
                if q >= 2:
                    pe.wait_ge(su_act, stages.act_w2(q - 2))
                for j in range(4):
                    at = ((q % 2) * 4 + j) * C
                    ins = pe.transpose(mb[:, q % 2, j * P:(j + 1) * P], w2raw[:, at:at + C], ident[:, :])
                done(ins, stages.w2turned(q))
                pe.wait_ge(su_act, stages.act_w2(q) - 1)
                for j in range(4):
                    ins = pe.matmul(bank(q % 2)[:, j * C:(j + 1) * C], h1[:, q % 2, j * P:(j + 1) * P], hh[:, 0, 0:C],
                                    start=True, stop=True)
                done(ins, stages.w2folded(q))
            done(pe.transpose(tr[:, 0:E0], hu[0:E0, 0, 0:C], ident[0:E0, 0:E0]), stages.b2turned)
            pe.wait_ge(su_act, stages.act_b2turned)
            done(pe.matmul(bank(2)[0:E0, 0:C], xnT[:, 0:E0], hh[:, 0, 0:C], start=True, stop=True), stages.b2folded)
            for a in range(4):
                ins = pe.transpose(bank(3)[:, a * P:(a + 1) * P], qk[:, a, 0, :], ident[:, :])
            done(ins, stages.qkvturned)
            pe.wait_ge(su_act, SU_ACT)
            pe.matmul(bank(0)[:, 0:2 * C], csum[:, 0:1].to_broadcast([P, P]), hT[:, 0:2 * C], start=True, stop=True)
            done(pe.matmul(bank(1)[:, 0:1], hT[:, 2 * C:3 * C], csum[:, 0:1], start=True, stop=True), stages.biases)
            pe.wait_ge(su_dve, SU_DVE)

            def turn(dst_bank, src):
                for t in range(NT):
                    ins = pe.transpose(dst_bank[:, t * P:(t + 1) * P], src[:, t, :], ident[:, :])
                return ins

            def row_start(b):
                pe.wait_ge(xn_ready.sem, xn_ready.at(b, 1))
                turn(tr, xn).then_inc(xnT_ps.sem, 1)
                yield
                pe.wait_ge(xnT_ready.sem, xnT_ready.at(b, 1))
                for t in range(NT):
                    ins = pe.matmul(tr[:, t * E0:(t + 1) * E0], xnT[:, t * P:(t + 1) * P], wg[:, :],
                                    start=True, stop=True)
                ins.then_inc(logit_ps.sem, 1)
                pe.wait_ge(mt_ready[0].sem, mt_ready[0].at(b, 0))
                pe.wait_ge(xhl_ready.sem, xhl_ready.at(b, 1))
                for i, (w, m) in enumerate(PARTS):
                    ins = pe.matmul(sa[:, :], m_hl[:, w, 0, :], x_hl[:, m, :], start=(i == 0), stop=(i == 2))
                ins.then_inc(key0_ps.sem, 1)
                yield
                pe.wait_ge(gates_ready.sem, gates_ready.at(b, 1))
                for t in range(NT):
                    ins = pe.transpose(tr[0:E0 + 1, t * P:(t + 1) * P], gates[:, t, :], ident[:, :])
                ins.then_inc(gatesT_ps.sem, 1)
                yield
                pe.wait_ge(gatesT_ready.sem, gatesT_ready.at(b, 1))
                for t in range(NT):
                    ins = pe.matmul(tr[:, t * C:(t + 1) * C], gatesT[:, t * P:(t + 1) * P], b2f[:, :],
                                    start=True, stop=True)
                ins.then_inc(facc_ps.sem, 1)
                yield

            for _part in row_start(0):
                pass
            with pe.Fori(0, B) as b:
                pe.wait_ge(key0_ready.sem, key0_ready.at(b, 1))
                pe.wait_ge(facc_ready.sem, facc_ready.at(b, 1))
                pe.wait_ge(out_ready.sem, out_ready.at(b, 0))
                pe.nop(nofuse=True)
                pe.matmul(sa[:, :], ones_row[:, :], bo_row[:, :, :].to_broadcast([1, NT, C]),
                          start=True, stop=False, skip_group_check=True)

                def misc(it, name, pieces):
                    n = MISCS.index(name)
                    pe.wait_ge(misc_free[n % 2].sem, misc_free[n % 2].at(b, it * (MISC // 2) + n // 2))
                    for at, width, lhsT, rhs, start, stop in pieces:
                        ins = pe.matmul(mb[:, n % 2, at:at + width], lhsT, rhs, start=start, stop=stop)
                    ins.then_inc(misc_ready.sem, 1)

                def value_keys(it, k):
                    misc(it, f"keys{k}", [(0, T, m_hl[:, w, k, :], x_hl[:, m, :], i == 0, i == 2)
                                          for i, (w, m) in enumerate(PARTS)])

                def values(it, k):
                    misc(it, f"values{k}", [(t * C, C, xnT[:, t * P:(t + 1) * P],
                                             n_all[:, bass.ds(it, 1), k, :].rearrange("p o c -> p (o c)"), True, True)
                                            for t in range(NT)])

                def hidden(it, side, m):
                    pe.wait_ge(w13_ready.sem, w13_ready.at(b, 4 * it + 2 * m + side - 3))
                    misc(it, ("h1_", "h3_")[side] + str(m),
                         [(0, T, w_hl[:, w, side, m * P:(m + 1) * P], x_hl[:, r, :], i == 0, i == 2)
                          for i, (w, r) in enumerate(PARTS)])

                def experts_out(it, half):
                    misc(it, f"out{half}",
                         [(j * C, C, hh[:, m, (2 * half + j) * P:(2 * half + j + 1) * P],
                           w2f[:, bass.ds(it, 1), m, :].rearrange("p o c -> p (o c)"), m == 0, m == 1)
                          for j in range(2) for m in range(2)])

                def scores(it, u):
                    t, n = u % NT, it * UNITS + u + 1
                    dst, w = score_slot(u, t)
                    k = u // NT
                    pe.wait_ge(kept_ready.sem, kept_ready.at(b, n - 2))
                    cut = w if w <= 512 else w - 256
                    for lo, hi in ((0, cut), (cut, w)):
                        if lo == hi:
                            continue
                        for i, (a, m) in enumerate(PARTS):
                            pe.matmul(dst[:, lo:hi], x_hl[:, a, t * P:(t + 1) * P], k_hl[:, m, k, lo:hi],
                                      start=(i == 0), stop=(i == 2 and hi < w), skip_group_check=True)
                    pe.matmul(dst[:, w - P:w], ident_h[:, :], causal[:, :], start=False, stop=True,
                              skip_group_check=True).then_inc(sc_ready.sem, 1)

                def turned(it, u):
                    t, n = u % NT, it * UNITS + u + 1
                    pe.wait_ge(attn_ready.sem, attn_ready.at(b, n))
                    pe.wait_ge(attnT_ready.sem, attnT_ready.at(b, n - 1))
                    for j in range(t + 1):
                        ins = pe.transpose(tr[:, j * P:(j + 1) * P], attn[:, u % 2, j * P:(j + 1) * P], ident[:, :])
                    ins.then_inc(tr_ready.sem, 1)

                def attend(it, u):
                    t, n = u % NT, it * UNITS + u + 1
                    pe.wait_ge(attnT_ready.sem, attnT_ready.at(b, n))
                    for j in range(t + 1):
                        ins = pe.matmul(sa[:, t * C:(t + 1) * C], attnT[:, u % 2, j * P:(j + 1) * P],
                                        wv[:, j, u // NT % 2, :], start=False, stop=False, skip_group_check=True)
                    ins.then_inc(av_done.sem, 1)

                def step(it, first=False):
                    pe.wait_ge(g_ready[0].sem, g_ready[0].at(b, it))
                    if not first:
                        pe.wait_ge(*misc_left(b, it - 1, "keys0"))
                    scores(it, 0)
                    if not first:
                        turned(it, -2)
                    pe.wait_ge(mt_ready[1].sem, mt_ready[1].at(b, it))
                    value_keys(it, 1)
                    if not first:
                        attend(it, -3)
                    values(it, 0)
                    scores(it, 1)
                    if not first:
                        turned(it, -1)
                    hidden(it, 0, 0)
                    if not first:
                        attend(it, -2)
                    scores(it, 2)
                    turned(it, 0)
                    hidden(it, 1, 0)
                    if not first:
                        attend(it, -1)
                    scores(it, 3)
                    turned(it, 1)
                    values(it, 1)
                    pe.wait_ge(*misc_left(b, it, "values0"))
                    attend(it, 0)
                    pe.wait_ge(g_ready[1].sem, g_ready[1].at(b, it + 1))
                    pe.wait_ge(*misc_left(b, it, "keys1"))
                    scores(it, 4)
                    turned(it, 2)
                    hidden(it, 0, 1)
                    attend(it, 1)
                    hidden(it, 1, 1)
                    scores(it, 5)
                    turned(it, 3)
                    pe.wait_ge(mt_ready[0].sem, mt_ready[0].at(b, it + 1))
                    value_keys(it, 0)
                    attend(it, 2)
                    scores(it, 6)
                    turned(it, 4)
                    attend(it, 3)
                    pe.wait_ge(hh_ready.sem, hh_ready.at(b, it * 2 + 2))
                    experts_out(it, 0)
                    scores(it, 7)
                    turned(it, 5)
                    experts_out(it, 1)
                    pe.wait_ge(*misc_left(b, it, "values1"))
                    attend(it, 4)

                step(0, first=True)
                with pe.Fori(1, NIT) as it:
                    step(it)
                attend(NIT, -3)
                turned(NIT, -2)
                attend(NIT, -2)
                turned(NIT, -1)
                attend(NIT, -1)
                for g in range(2):
                    if g == 0:
                        pe.wait_ge(attnT_ready.sem, attnT_ready.at(b, NIT * UNITS))
                    for t in range(NT):
                        ins = pe.transpose(bank(g)[:, t * P:(t + 1) * P],
                                           attn_mem[:, t, 8 * g:8 * g + 8, :].rearrange("p h m -> p (h m)"), ident[:, :])
                    ins.then_inc(memT_ps.sem, 1)
                for g in range(2):
                    pe.wait_ge(memT_ready.sem, memT_ready.at(b, g + 1))
                    for t in range(NT):
                        ins = pe.matmul(sa[:, t * C:(t + 1) * C], memT[:, g, t * P:(t + 1) * P], r_all[:, g, :],
                                        start=False, stop=(g == 1), skip_group_check=True)
                ins.then_inc(s0_ready.sem, 1)
                pe.wait_ge(xn_ready.sem, xn_ready.at(b, 2))
                turn(bank(0), xn).then_inc(xnT_ps.sem, 1)
                pe.wait_ge(xnT_ready.sem, xnT_ready.at(b, 2))
                for t in range(NT):
                    ins = pe.matmul(bank(1)[:, t * E1:(t + 1) * E1], xnT[:, t * P:(t + 1) * P], wr[:, :],
                                    start=True, stop=True)
                ins.then_inc(logit_ps.sem, 1)
                pe.wait_ge(xn_ready.sem, xn_ready.at(b, 3))
                turn(bank(2), hn).then_inc(xnT_ps.sem, 1)
                pe.wait_ge(xnT_ready.sem, xnT_ready.at(b, 3))
                for t in range(NT):
                    ins = pe.matmul(mb[:, t // 2, (t % 2) * 2 * C:(t % 2 + 1) * 2 * C], hT[:, t * P:(t + 1) * P],
                                    qkvT[:, 0:2, :].rearrange("p a c -> p (a c)"), start=True, stop=True)
                ins.then_inc(qk_ps.sem, 1)
                pe.wait_ge(chosen_ready.sem, chosen_ready.at(b, 1))
                for t in range(NT):
                    for s in range(t + 1):
                        ins = pe.matmul(bank(1)[:, 64 + t * E1:64 + (t + 1) * E1], before[:, :] if s == t else ones_h[:, :],
                                        chosen[:, s, :], start=(s == 0), stop=(s == t))
                ins.then_inc(pos_ps.sem, 1)
                pe.matmul(bank(3), qkvT[:, 2, :], hT, start=True, stop=True).then_inc(v_ps.sem, 1)
                pe.wait_ge(qk_ready.sem, qk_ready.at(b, 1))
                for t in range(NT):
                    ins = pe.matmul(tr[:, 0:C], qk[:, t, 0, :], qk[:, t, 1, :], start=(t == 0), stop=(t == NT - 1))
                ins.then_inc(cw_ps.sem, 1)

                def gather(t):
                    pe.wait_ge(one_hot_ready.sem, one_hot_ready.at(b, t + 1))
                    for half in range(2):
                        ins = pe.matmul(bank(half)[:, 0:4 * CAP], xn[:, t, :],
                                        one_hot[:, t, 4 * half:4 * half + 4, :].rearrange("p e s -> p (e s)"),
                                        start=(t == 0), stop=(t == NT - 1))
                        if t == NT - 1:
                            ins.then_inc(buf_ps.sem, 1)

                gather(0)
                pe.wait_ge(cw_ready.sem, cw_ready.at(b, 1))
                pe.transpose(tr[:, 0:C], cw[:, :], ident[:, :]).then_inc(cwT_ps.sem, 1)
                gather(1)
                pe.wait_ge(cwT_ready.sem, cwT_ready.at(b, 1))
                pe.wait_ge(vT_ready.sem, vT_ready.at(b, 1))
                pe.matmul(bank(2), cwT[:, :], vT, start=True, stop=True).then_inc(aT_ps.sem, 1)
                gather(2)
                gather(3)
                pe.wait_ge(aT_ready.sem, aT_ready.at(b, 1))
                for t in range(NT):
                    ins = pe.matmul(bank(3)[:, t * C:(t + 1) * C], aT[:, t * P:(t + 1) * P], projT[:, :],
                                    start=True, stop=True)
                ins.then_inc(proj_ps.sem, 1)

                def expert_up(e):
                    if e < 2:
                        pe.wait_ge(buf_ready.sem, buf_ready.at(b, 2))
                    else:
                        pe.wait_ge(hid_ready.sem, hid_ready.at(b, e - 1))
                    for m in range(HM1):
                        ins = pe.matmul(bank(e % 2)[:, m * CAP:(m + 1) * CAP], v1_all[:, e, m * P:(m + 1) * P],
                                        bufT[:, e, :], start=True, stop=True)
                    ins.then_inc(hid_ps.sem, 1)

                def back(e):
                    if e == 0:
                        pe.wait_ge(weighted_ready.sem, weighted_ready.at(b, 1))
                        pe.wait_ge(s1_ready.sem, s1_ready.at(b, 1))
                    if e >= 2:
                        pe.wait_ge(back_ready.sem, back_ready.at(b, e - 1))
                    for t in range(NT):
                        ins = pe.transpose(bank(2 + e % 2)[0:CAP, t * P:(t + 1) * P], weighted[:, t, e, :], ident[:, :])
                    ins.then_inc(back_ps.sem, 1)

                def expert_down(e):
                    pe.wait_ge(hid_ready.sem, hid_ready.at(b, e + 1))
                    for m in range(HM1):
                        ins = pe.matmul(mb[0:CAP, e // 4, (e % 4) * C:(e % 4 + 1) * C], hid[:, e % 2, m, :],
                                        v2_all[:, e, m, :], start=(m == 0), stop=(m == HM1 - 1))
                    if e % 4 == 3:
                        ins.then_inc(y_ps.sem, 1)

                start = row_start(b + 1)
                expert_up(0)
                back(0)
                for e in range(1, E1):
                    expert_up(e)
                    back(e)
                    expert_down(e - 1)
                    if e in PE_START_AT:
                        next(start)
                expert_down(E1 - 1)
                pe.wait_ge(key0_ready.sem, key0_ready.at(b + 1, 1))
                pe.wait_ge(back_ready.sem, back_ready.at(b, E1))
                pe.wait_ge(y_ready.sem, y_ready.at(b, 2))
                for t in range(NT):
                    for e in range(E1):
                        ins = pe.matmul((sa, bank(0))[t // 2][:, t % 2 * C:(t % 2 + 1) * C],
                                        backT[e][:, t * P:(t + 1) * P], y_slots[:, e, :],
                                        start=(e == 0), stop=(e == E1 - 1))
                    if t % 2:
                        ins.then_inc(comb_ps.sem, 1)


class SetupStages:

    memk, memv, postT, cols = 7, 8, 9, 10
    act_postT, act_cols = 9, 10
    memr = 19
    b2turned, b2folded, qkvturned, biases = 28, 29, 30, 31
    act_memr = 23
    act_b2turned = 32

    def turned(self, w, half):
        return 2 * w + half + 1

    def fold(self, q):
        return 11 + q

    def act_fold(self, q):
        return 10 + 2 * (q + 1) if q < 4 else 18 + (q - 3)

    def w2turned(self, q):
        return 20 + 2 * q

    def w2folded(self, q):
        return 21 + 2 * q

    def act_w2(self, q):
        return 23 + 2 * (q + 1)


SU_ACT = 34
SU_DVE = 10

_INS = ["L0_attn_x", "L0_attn_Wq", "L0_attn_Wk", "L0_attn_Wv", "L0_attn_pre_proj", "L0_attn_post_proj",
        "L0_attn_mem_k", "L0_attn_mem_v", "L0_attn_Wo", "L0_attn_bo", "L0_ffn_W1", "L0_ffn_b1", "L0_ffn_W3",
        "L0_ffn_b3", "L0_ffn_W2", "L0_ffn_b2", "L0_ffn_Wg", "L0_ffn_bg", "L0_ffn_Wf", "L0_ffn_bf",
        "L1_attn_norm_w", "L1_attn_norm_b", "L1_attn_qkv_w", "L1_attn_qkv_b", "L1_attn_proj_w",
        "L1_attn_proj_b", "L1_ffn_Wr", "L1_ffn_W1", "L1_ffn_b1", "L1_ffn_W2", "L1_ffn_b2"]

_BY_PARTITION = ("L0_ffn_b1", "L0_ffn_b3", "L1_ffn_b1")


def kernel(**inputs):
    import concourse.bacc as bacc
    from concourse.bass_utils import run_bass_kernel_spmd

    nc = bacc.Bacc("TRN2", target_bir_lowering=False, num_devices=1)
    arrays, args = {}, []
    for name in _INS:
        a = np.asarray(inputs[name])
        if name in _BY_PARTITION:
            a = a.reshape(a.shape[0], -1, P).transpose(2, 0, 1)
        a = np.ascontiguousarray(a)
        arrays[name] = a
        args.append(nc.dram_tensor(name, a.shape, mybir.dt.from_np(a.dtype), kind="ExternalInput").ap())
    args.append(nc.dram_tensor("out", (B, T, C), F32, kind="ExternalOutput").ap())
    build(nc, *args)
    r = run_bass_kernel_spmd(nc, [arrays], core_ids=[0])
    return r.results[0]["out"]
```

```python
from contextlib import ExitStack

import numpy as np

import concourse.bass as bass
from concourse import mybir

F32 = mybir.dt.float32
F32R = mybir.dt.float32r
BF16 = mybir.dt.bfloat16
ALU = mybir.AluOpType
ACT = mybir.ActivationFunctionType
AX = mybir.AxisListType

P = 128
B, T, C = 8, 512, 128
NT = T // P
H, DH, NM = 16, 64, 16
HC = H * DH // P
NIT = H // 2
E0, HID0 = 8, 256
E1, HID1 = 8, 512
HM1 = HID1 // P
CAP = int(T / E1 * 1.25)
EPS = 1e-5
MASKED = -3.3895313892515355e38
KEYS = NM + T
UNITS = 2 * NT
MISCS = ("keys1", "values0", "h1_0", "h3_0", "values1", "h1_1", "h3_1", "keys0", "out0", "out1")
MISC = len(MISCS)
PARTS = ((0, 0), (0, 1), (1, 0))
START_AT = (1, 2, 3, 5, 6)
PE_START_AT = (1, 2, 5, 6)
assert E0 == NIT and C == P


class Signal:

    def __init__(self, sem, per_row, preset=0):
        self.sem, self.per_row, self.preset = sem, per_row, preset

    def at(self, b, n):
        return b * self.per_row + (n + self.preset)


def build(nc, x, Wq, Wk, Wv, pre, post, mem_k, mem_v, Wo, bo, W1, b1, W3, b3, W2, b2, Wg, bg, Wf, bf,
          norm_w, norm_b, qkv_w, qkv_b, proj_w, proj_b, Wr, V1, c1, V2, c2, out):
    with ExitStack() as ctx:
        def sb(name, shape, dt=F32):
            return ctx.enter_context(nc.sbuf_tensor(name, shape, dt))

        def ps(name, shape):
            return ctx.enter_context(nc.psum_tensor(name, shape, F32))

        def sem(name):
            return ctx.enter_context(nc.semaphore(name))

        sc = ps("sc", [P, 4, 512])
        tr = ps("tr", [P, 512])
        sa = ps("sa", [P, 512])
        mb = ps("mb", [P, 2, 512])

        x_next = sb("x_next", [P, NT, C])
        mt_all = sb("mt_all", [P, NIT + 1, 2, C])
        n_all = sb("n_all", [P, NIT, 2, C])
        g_all = sb("g_all", [P, NIT + 1, 2, NM])
        r_all = sb("r_all", [P, 2, C])
        w13_all = sb("w13_all", [P, E0 + 1, 2, HID0])
        w2f = sb("w2f", [P, E0, 2, C])
        b1c = sb("b1c", [P, E0, 2])
        b3c = sb("b3c", [P, E0, 2])
        b2f = sb("b2f", [E0 + 1, C])
        wg = sb("wg", [P, E0])
        bg_b = sb("bg_b", [P, E0])
        bo_row = sb("bo_row", [1, 1, C])
        ones_row = sb("ones_row", [1, P])
        v1_all = sb("v1_all", [P, E1, HID1])
        v2_all = sb("v2_all", [P, E1, HM1, C])
        c1c = sb("c1c", [P, E1, HM1])
        c2_b = sb("c2_b", [CAP, E1, C])
        qkvT = sb("qkvT", [P, 3, C])
        qk_bias = sb("qk_bias", [P, 2, C])
        v_bias = sb("v_bias", [P, 1])
        projT = sb("projT", [P, C])
        pb_b = sb("pb_b", [P, C])
        wr = sb("wr", [P, E1])
        ident = sb("ident", [P, P])
        ident_h = sb("ident_h", [P, P], BF16)
        causal = sb("causal", [P, P], BF16)
        before = sb("before", [P, P], BF16)
        ones_h = sb("ones_h", [P, P], BF16)
        slot_no = sb("slot_no", [P, CAP])
        ties0 = sb("ties0", [P, E0, E0])
        ties1 = sb("ties1", [P, E1, E1])
        neghalf = sb("neghalf", [P, NT])

        arena = sb("arena", [P, 8192])
        wo_sb = arena[:, 0:1024].rearrange("p (c n) -> p c n", c=HC)
        wqT = arena[:, 1024:2048].rearrange("p (c n) -> p c n", c=HC)
        wkT = arena[:, 2048:3072].rearrange("p (c n) -> p c n", c=HC)
        wvT = arena[:, 3072:4096].rearrange("p (c n) -> p c n", c=HC)
        scaled = arena[:, 4096:8192].rearrange("p (c k n) -> p c k n", c=HC, k=4)
        one_hot = arena[:, 0:2560].rearrange("p (t e s) -> p t e s", t=NT, e=E1)
        weighted = arena[:, 2560:5120].rearrange("p (t e s) -> p t e s", t=NT, e=E1)
        y_slots = arena[0:CAP, 5120:6144].rearrange("p (e c) -> p e c", e=E1)

        xb = sb("xb", [P, NT, C])
        stats = sb("stats", [P, NT, 6])
        mv = sb("mv", [P, NT, 2])
        veps = sb("veps", [P, NT])
        rstd = sb("rstd", [P, NT])
        xn = sb("xn", [P, NT, C])
        xnT = sb("xnT", [P, T])
        gates = sb("gates", [P, NT, E0 + 1])
        gatesT = sb("gatesT", [E0 + 1, T])
        lg = sb("lg", [P, NT, E0])
        pr = sb("pr", [P, NT, E0])
        red = sb("red", [P, NT])
        cmpa = sb("cmpa", [P, NT, E0, E0])
        cmpb = sb("cmpb", [P, NT, E0, E0])
        rank = sb("rank", [P, NT, E0])
        facc = sb("facc", [P, NT, C])
        x_hl = sb("x_hl", [P, 2, T], F32R)
        m_hl = sb("m_hl", [P, 2, 2, C], F32R)
        w_hl = sb("w_hl", [P, 2, 2, HID0], F32R)
        k_hl = sb("k_hl", [P, 2, 2, KEYS], F32R)
        wv = sb("wv", [P, NT, 2, C])
        top8 = sb("top8", [P, 2, 8])
        nmax = sb("nmax", [P, 2])
        den = sb("den", [P, 2])
        rden = sb("rden", [P, 2])
        ex = sb("ex", [P, 2, KEYS])
        kept = sb("kept", [P, 2, KEYS])
        attn = sb("attn", [P, 2, T])
        attnT = sb("attnT", [P, 2, T])
        attn_mem = sb("attn_mem", [P, NT, H, NM])
        memT = sb("memT", [P, 2, T])
        h1 = sb("h1", [P, 2, T])
        hu = sb("hu", [P, 2, T])
        ht = sb("ht", [P, 2, T])
        hh = sb("hh", [P, 2, T])
        x1 = sb("x1", [P, NT, C])
        sg = hh[:, 0, :].rearrange("p (t c) -> p t c", t=NT)
        hn = xb
        hT = attnT[:, 0, :]
        qk = attn[:, :, :].rearrange("p a (t k c) -> p (a t) k c", t=2, k=2)
        vT = hu[:, 1, :]
        backT = [a[0:CAP, i, :] for a, i in ((h1, 0), (h1, 1), (ht, 0), (ht, 1), (hu, 0), (hu, 1), (hh, 1), (attn, 0))]
        cw = sb("cw", [P, C])
        cwT = sb("cwT", [P, C])
        cmax = sb("cmax", [P, 1])
        csum = sb("csum", [P, 1])
        aT = attnT[:, 1, :]
        s1 = sb("s1", [P, NT, C])
        chosen = sb("chosen", [P, NT, E1], BF16)
        pos = sb("pos", [P, NT, E1])
        bufT = kept[:, :, :].rearrange("p a n -> p (a n)")[:, 0:E1 * CAP].rearrange("p (e s) -> p e s", e=E1)
        hid = ex[:, :, :].rearrange("p a n -> p (a n)")[:, 0:2 * HM1 * CAP].rearrange("p (a m s) -> p a m s", a=2, m=HM1)
        y_out = sb("y_out", [P, NT, C])

        mem_k_diag = h1[:, :, :].rearrange("p a n -> p (a n)").rearrange("p (g j n) -> p g j n", g=2, j=4)
        mem_kT = ht[:, 0, 0:HC * NM].rearrange("p (g j m) -> p g j m", g=2, j=4)
        mem_vT = ht[:, 0, HC * NM:2 * HC * NM].rearrange("p (c m) -> p c m", c=HC)
        pre_col = ht[:, 1, 0:HC * H].rearrange("p (c h) -> p c h", c=HC)
        post_col = ht[:, 1, HC * H:2 * HC * H].rearrange("p (c h) -> p c h", c=HC)
        pre_row = hu[:, 0, 0:2 * H].rearrange("p (g k) -> p g k", g=2)
        same_slot = hu[:, 0, 2 * H:2 * H + NM]
        pre_mix = hu[:, 1, :].rearrange("p (g k m) -> p g k m", g=2, k=H)
        mem_qk = hh[:, 1, 0:2 * C]
        wf = hh[:, 0, 0:C]
        mem_scaled = [a[:, :, :].rearrange("p a n -> p (a n)")[:, 0:4 * H * NM].rearrange("p (c n) -> p c n", c=4)
                      for a in (ex, kept)]
        w2T = [a.rearrange("p (e m h) -> p e m h", e=4, m=2) for a in
               (attn_mem[:, :, :, :].rearrange("p t h m -> p (t h m)"), memT[:, :, :].rearrange("p a n -> p (a n)"))]
        b2T = x1[:, 0, 0:E0]
        norm_w_col, norm_b_col = cmax, csum

        loaded_m = sem("loaded_m")
        loaded_n = sem("loaded_n")
        loaded_s = sem("loaded_s")
        loaded_b = sem("loaded_b")
        loaded_v = sem("loaded_v")
        consts = sem("consts")
        chunk_ready = sem("chunk_ready")
        chunk_read = Signal(sem("chunk_read"), 0, HC)
        fold_copied = Signal(sem("fold_copied"), 0, 2)
        diag_ready = sem("diag_ready")
        mix_ready = sem("mix_ready")
        mem_scaled_ready = sem("mem_scaled_ready")
        su_pe = sem("su_pe")
        su_act = sem("su_act")
        su_done = sem("su_done")
        x_loaded = Signal(sem("x_loaded"), 16)
        x_taken = Signal(sem("x_taken"), 1)
        def sig(name, per_row, preset=0):
            return Signal(sem(name), per_row, preset)

        mt_ready = [sig("mt0_ready", NIT, 1), sig("mt1_ready", NIT, 1)]
        w13_ready = sig("w13_ready", NIT * 4, 4)
        g_ready = [sig("g0_ready", NIT, 1), sig("g1_ready", NIT)]
        key0_ps = sig("key0_ps", 1)
        key0_high = sig("key0_high", 1)
        key0_ready = sig("key0_ready", 1)
        key_high = sig("key_high", NIT * 2)
        xhl_ready = sig("xhl_ready", 1)
        misc_ready = sig("misc_ready", NIT * MISC)
        misc_free = [sig(f"misc_free{i}", NIT * MISC // 2, 1) for i in range(2)]
        sc_ready = sig("sc_ready", NIT * UNITS)
        top_done = sig("top_done", NIT * UNITS)
        nmax_ready = sig("nmax_ready", NIT * UNITS)
        exp_done = sig("exp_done", NIT * UNITS)
        kept_ready = sig("kept_ready", NIT * UNITS, 2)
        rden_ready = sig("rden_ready", NIT * UNITS)
        attn_ready = sig("attn_ready", NIT * UNITS, 2)
        tr_ready = sig("tr_ready", NIT * UNITS, 2)
        attnT_ready = sig("attnT_ready", NIT * UNITS, 1)
        av_done = sig("av_done", NIT * UNITS, 2)
        th_ready = sig("th_ready", NIT * 2)
        hh_ready = sig("hh_ready", NIT * 2)
        mem_kept = sig("mem_kept", NIT * UNITS, 2)
        var_ready = sig("var_ready", 3)
        rstd_ready = sig("rstd_ready", 3)
        xn_ready = sig("xn_ready", 3)
        xnT_ps = sig("xnT_ps", 3)
        xnT_ready = sig("xnT_ready", 3)
        logit_ps = sig("logit_ps", 2)
        logit_ready = sig("logit_ready", 2)
        gexp_done = sig("gexp_done", 2)
        gates_ready = sig("gates_ready", 1)
        gatesT_ps = sig("gatesT_ps", 1)
        gatesT_ready = sig("gatesT_ready", 1)
        facc_ps = sig("facc_ps", 1)
        facc_ready = sig("facc_ready", 1)
        memT_ps = sig("memT_ps", 2)
        memT_ready = sig("memT_ready", 2)
        s0_ready = sig("s0_ready", 1)
        gate_tanh = sig("gate_tanh", 3)
        x1_ready = sig("x1_ready", 1)
        qk_ps = sig("qk_ps", 1)
        qk_ready = sig("qk_ready", 1)
        v_ps = sig("v_ps", 1)
        vT_ready = sig("vT_ready", 1)
        cw_ps = sig("cw_ps", 1)
        cmax_ready = sig("cmax_ready", 1)
        cexp_done = sig("cexp_done", 1)
        cw_ready = sig("cw_ready", 1)
        cwT_ps = sig("cwT_ps", 1)
        cwT_ready = sig("cwT_ready", 1)
        aT_ps = sig("aT_ps", 1)
        aT_ready = sig("aT_ready", 1)
        proj_ps = sig("proj_ps", 1)
        s1_ready = sig("s1_ready", 1)
        chosen_ready = sig("chosen_ready", 1)
        pos_ps = sig("pos_ps", 1)
        one_hot_ready = sig("one_hot_ready", NT)
        weighted_ready = sig("weighted_ready", 1)
        buf_ps = sig("buf_ps", 2)
        buf_ready = sig("buf_ready", 2)
        back_ps = sig("back_ps", E1)
        back_ready = sig("back_ready", E1)
        hid_ps = sig("hid_ps", E1)
        hid_ready = sig("hid_ready", E1)
        y_ps = sig("y_ps", 2)
        y_ready = sig("y_ready", 2)
        comb_ps = sig("comb_ps", 2)
        gate_read = sig("gate_read", 2, 2)
        out_ready = sig("out_ready", 1)
        stored = Signal(sem("stored"), 16, 16)

        block = ctx.enter_context(nc.Block())

        def score_slot(u, t):
            n = NM + P * (t + 1)
            at = 0 if n <= 512 else 512 - NM - 256
            flat = sc[:, 2 * (u % 2):2 * (u % 2) + 2, :].rearrange("p a n -> p (a n)")
            return flat[:, at:at + n], n

        def bank(i):
            return sc[:, i, :]

        def misc_done(b, it, name):
            return misc_ready.sem, misc_ready.at(b, it * MISC + MISCS.index(name) + 1)

        def misc_left(b, it, name):
            n = MISCS.index(name)
            return misc_free[n % 2].sem, misc_free[n % 2].at(b, it * (MISC // 2) + n // 2 + 1)

        G_COPIED, R_COPIED, SU_COPIES, SU_BIASES = 2, 3, 8, 9

        N_M, N_N, N_S, N_B, N_V = 4, 14, 18, 4, 4

        @block.sync
        def _(sp):
            def row(a):
                return a.rearrange("(a n) -> a n", a=1)

            def column(a):
                return a.rearrange("(p a) -> p a", a=1)

            def heads_by_half(a, half):
                return a.rearrange("(c two) k -> two c k", two=2)[half:half + 1].to_broadcast([DH, HC, H])

            for dst, src in ((pre_col, pre), (wqT, Wq), (wkT, Wk)):
                if dst is pre_col:
                    for half in range(2):
                        sp.dma_start(pre_col[half * DH:(half + 1) * DH], heads_by_half(src, half)).then_inc(loaded_m, 16)
                else:
                    sp.dma_start(dst, src).then_inc(loaded_m, 16)
            sp.dma_start(ht[:, 0, 0:HC * NM].rearrange("p (c m) -> p c m", c=HC), mem_k).then_inc(loaded_n, 16)
            for h in range(P // NM):
                sp.dma_start(pre_row[h * NM:(h + 1) * NM], pre.rearrange("(g h) k -> h g k", g=2)[h:h + 1].to_broadcast(
                    [NM, 2, H])).then_inc(loaded_n, 16)
            for half in range(2):
                sp.dma_start(post_col[half * DH:(half + 1) * DH], heads_by_half(post, half)).then_inc(loaded_n, 16)
            sp.dma_start(wvT, Wv).then_inc(loaded_n, 16)
            sp.dma_start(wo_sb, Wo.rearrange("(c p) n -> p c n", p=P)).then_inc(loaded_n, 16)
            sp.dma_start(mem_vT, mem_v).then_inc(loaded_n, 16)
            sp.dma_start(x_next[:, :, :], x[0].rearrange("(t p) c -> p t c", p=P)).then_inc(x_loaded.sem, 16)
            small = [(wf, Wf), (b2T, b2), (b2f[E0:E0 + 1, :], row(bf)), (wg[:, :], Wg),
                     (bg_b[:, :], row(bg).partition_broadcast(P)), (bo_row[:, 0, :], row(bo)), (b1c[:, :, :], b1),
                     (b3c[:, :, :], b3), (hT[:, 0:3 * C], qkv_w), (projT[:, :], proj_w),
                     (norm_w_col[:, :], column(norm_w)), (norm_b_col[:, :], column(norm_b)),
                     (qk_bias[:, :, :].rearrange("p a c -> p (a c)"), row(qkv_b[0:2 * C]).partition_broadcast(P)),
                     (v_bias[:, :], column(qkv_b[2 * C:3 * C])), (pb_b[:, :], row(proj_b).partition_broadcast(P)),
                     (wr[:, :], Wr)]
            small += [(w2T[i].rearrange("p e m h -> p e (m h)"), W2[:, 4 * i:4 * i + 4, :]) for i in range(2)]
            assert len(small) == N_S
            for dst, src in small:
                sp.dma_start(dst, src).then_inc(loaded_s, 16)
            for i, w in enumerate((W1, W3)):
                sp.dma_start(w13_all[:, 0:E0, i, :], w.rearrange("e c h -> c e h")).then_inc(loaded_b, 16)
                sp.dma_start(w13_all[:, E0, i, :], w[0]).then_inc(loaded_b, 16)
            sp.dma_start(v1_all[:, :, :], V1.rearrange("e c h -> c e h")).then_inc(loaded_v, 16)
            sp.dma_start(v2_all[:, :, :, :], V2.rearrange("e (m p) c -> p e m c", p=P)).then_inc(loaded_v, 16)
            sp.dma_start(c1c[:, :, :], c1).then_inc(loaded_v, 16)
            sp.dma_start(c2_b[:, :, :].rearrange("p e c -> p (e c)"),
                         c2.rearrange("e c -> (e c)").rearrange("(a n) -> a n", a=1).partition_broadcast(CAP)
                         ).then_inc(loaded_v, 16)

            def store(b, row):
                sp.wait_ge(out_ready.sem, out_ready.at(b, 1))
                sp.dma_start(row.rearrange("(t p) c -> p t c", p=P), y_out[:, :, :]).then_inc(stored.sem, 16)

            with sp.Fori(0, B - 1) as b:
                sp.wait_ge(x_taken.sem, x_taken.at(b, 1))
                sp.dma_start(x_next[:, :, :], x[bass.ds(b + 1, 1)].rearrange("o (t p) c -> p (o t) c", p=P)
                             ).then_inc(x_loaded.sem, 16)
                store(b, out[bass.ds(b, 1)].rearrange("o t c -> (o t) c"))
            sp.wait_ge(x_taken.sem, x_taken.at(B - 1, 1))
            sp.dma_start(x_next[:, :, :], x[0].rearrange("(t p) c -> p t c", p=P)).then_inc(x_loaded.sem, 16)
            store(B - 1, out[B - 1])
            sp.wait_ge(stored.sem, stored.at(B - 1, 16))

        @block.gpsimd
        def _(pool):
            pool.memset(ident[:, :], 0.0)
            pool.memset(ident_h[:, :], 0.0)
            pool.memset(causal[:, :], 0.0)
            pool.memset(before[:, :], 1.0)
            pool.memset(ones_h[:, :], 1.0)
            pool.memset(ties0[:, :, :], 1.0)
            pool.memset(ties1[:, :, :], 1.0)
            pool.memset(neghalf[:, :], -0.5)
            pool.memset(ones_row[:, :], 1.0)
            pool.memset(gates[:, :, :], 1.0)
            pool.memset(h1[:, :, :], 0.0)
            pool.iota(slot_no[:, :], pattern=[[1, CAP]], base=0, channel_multiplier=0,
                      allow_small_or_imprecise_dtypes=True)
            pool.drain()
            for m in (ident, ident_h):
                pool.affine_select(out=m[:, :], in_=m[:, :], compare_op=ALU.not_equal, fill=1.0,
                                   base=0, pattern=[[-1, P]], channel_multiplier=1)
            pool.affine_select(out=causal[:, :], in_=causal[:, :], compare_op=ALU.is_ge, fill=MASKED,
                               base=0, pattern=[[-1, P]], channel_multiplier=1)
            pool.affine_select(out=before[:, :], in_=before[:, :], compare_op=ALU.is_gt, fill=0.0,
                               base=0, pattern=[[1, P]], channel_multiplier=-1)
            pool.affine_select(out=ties0[:, :, :], in_=ties0[:, :, :], compare_op=ALU.is_gt, fill=0.0,
                               base=0, pattern=[[-1, E0], [1, E0]], channel_multiplier=0)
            pool.affine_select(out=ties1[:, :, :], in_=ties1[:, :, :], compare_op=ALU.is_gt, fill=0.0,
                               base=0, pattern=[[1, E1], [-1, E1]], channel_multiplier=0)
            pool.drain()
            pool.memset(neghalf[:, :], -0.5).then_inc(consts, 1)
            pool.wait_ge(loaded_n, 16 * N_N)
            for c in range(HC):
                ins = pool.tensor_tensor(
                    mem_scaled[c // 4][:, c % 4, :].rearrange("p (h m) -> p h m", h=H),
                    mem_vT[:, c, :].unsqueeze(1).to_broadcast([P, H, NM]),
                    post_col[:, c, :].unsqueeze(2).to_broadcast([P, H, NM]), ALU.mult)
            ins.then_inc(mem_scaled_ready, 1)

            def split(dst, src):
                pool.tensor_copy(dst[0], src)
                pool.drain()
                return pool.tensor_tensor(dst[1], src, dst[0], ALU.subtract)

            pool.wait_ge(fold_copied.sem, fold_copied.at(0, 1))
            for k in range(2):
                split([m_hl[:, i, k, :] for i in range(2)], mt_all[:, 0, k, :]).then_inc(mt_ready[k].sem, 1)
            pool.wait_ge(loaded_b, 16 * N_B)
            split([w_hl[:, i, :, :] for i in range(2)], w13_all[:, 0, :, :]).then_inc(w13_ready.sem, 4)
            pool.wait_ge(su_act, G_COPIED)
            split([k_hl[:, i, 0, 0:NM] for i in range(2)], g_all[:, 0, 0, :]).then_inc(g_ready[0].sem, 1)

            def root(b, n):
                pool.wait_ge(var_ready.sem, var_ready.at(b, n))
                pool.tensor_tensor(rstd[:, :], veps[:, :], neghalf[:, :], ALU.pow).then_inc(rstd_ready.sem, 1)

            root(0, 1)
            pool.wait_ge(su_done, 1)
            with pool.Fori(0, B) as b:

                def normalise(it, u):
                    t, n = u % NT, it * UNITS + u + 1
                    pool.wait_ge(rden_ready.sem, rden_ready.at(b, n))
                    pool.wait_ge(tr_ready.sem, tr_ready.at(b, n - 2))
                    pool.nop(nofuse=True)
                    pool.tensor_scalar(attn[:, u % 2, 0:P * (t + 1)], kept[:, u % 2, NM:NM + P * (t + 1)],
                                       rden[:, u % 2:u % 2 + 1], 1.0, ALU.mult, ALU.mult
                                       ).then_inc(attn_ready.sem, 1)

                def next_m(it, k):
                    pool.nop(nofuse=True)
                    split([m_hl[:, i, k:k + 1, :] for i in range(2)], mt_all[:, bass.ds(it + 1, 1), k, :]
                          ).then_inc(mt_ready[k].sem, 1)

                def next_w13(it, side, m):
                    pool.wait_ge(*misc_done(b, it, ("h1_", "h3_")[side] + str(m)))
                    pool.nop(nofuse=True)
                    split([w_hl[:, i, side:side + 1, m * P:(m + 1) * P] for i in range(2)],
                          w13_all[:, bass.ds(it + 1, 1), side, m * P:(m + 1) * P]).then_inc(w13_ready.sem, 1)

                def step(it, first=False):
                    if first:
                        pool.wait_ge(key0_ps.sem, key0_ps.at(b, 1))
                    else:
                        pool.wait_ge(*misc_done(b, it - 1, "keys0"))
                    next_m(it, 0)
                    if not first:
                        pool.wait_ge(sc_ready.sem, sc_ready.at(b, it * UNITS))
                    pool.nop(nofuse=True)
                    split([k_hl[:, i, 1:2, 0:NM] for i in range(2)], g_all[:, bass.ds(it, 1), 1, :]
                          ).then_inc(g_ready[1].sem, 1)
                    normalise(it, 0)
                    pool.wait_ge(*misc_done(b, it, "keys1"))
                    next_m(it, 1)
                    normalise(it, 1)
                    next_w13(it, 0, 0)
                    normalise(it, 2)
                    next_w13(it, 1, 0)
                    normalise(it, 3)
                    split([k_hl[:, i, 0:1, 0:NM] for i in range(2)], g_all[:, bass.ds(it + 1, 1), 0, :]
                          ).then_inc(g_ready[0].sem, 1)
                    normalise(it, 4)
                    next_w13(it, 0, 1)
                    normalise(it, 5)
                    next_w13(it, 1, 1)
                    normalise(it, 6)
                    normalise(it, 7)

                step(0, first=True)
                with pool.Fori(1, NIT) as it:
                    step(it)
                root(b, 2)
                root(b, 3)
                for t in range(NT):
                    pool.wait_ge(one_hot_ready.sem, one_hot_ready.at(b, t + 1))
                    ins = pool.tensor_tensor(weighted[:, t, :, :], one_hot[:, t, :, :],
                                             pr[:, t, :].unsqueeze(2).to_broadcast([P, E1, CAP]), ALU.mult)
                ins.then_inc(weighted_ready.sem, 1)
                root(b + 1, 1)

        @block.scalar
        def _(act):
            def copied(dst, src, stage, scale=1.0):
                act.wait_ge(su_pe, stage)
                act.activation(dst, src, ACT.Copy, scale=scale).then_inc(su_act, 1)

            def folds(first, dst):
                with act.Fori(0, 2) as i:
                    for j in range(2):
                        act.wait_ge(chunk_read.sem, (2 * HC) * i + ((first + j + 2) * HC))
                        act.activation(dst[:, bass.ds(4 * i + 2 * j, 2), :, :].rearrange("p a k c -> p (a k c)"),
                                       bank(j), ACT.Copy).then_inc(fold_copied.sem, 1)

            act.wait_ge(consts, 1)
            act.wait_ge(loaded_n, 16 * N_N)
            for half in range(2):
                for j in range(4):
                    rows, at = slice(half * DH, (half + 1) * DH), (2 * j + half) * NM
                    ins = act.activation(mem_k_diag[rows, :, j, at:at + NM], mem_kT[rows, :, j, :], ACT.Copy)
            ins.then_inc(diag_ready, 1)
            folds(0, mt_all)
            copied(mem_qk, bank(2)[:, 0:2 * C], 1)
            copied(g_all[:, 0:NIT, :, :].rearrange("p a k m -> p (a k m)"), bank(3)[:, 0:H * NM], G_COPIED)
            folds(4, n_all)

            def evacuate(b, it, name, dst, bias=None):
                act.wait_ge(*misc_done(b, it, name))
                n = MISCS.index(name) % 2
                if bias is None:
                    ins = act.activation(dst, mb[:, n, :], ACT.Copy)
                else:
                    ins = act.activation(dst, mb[:, n, :], ACT.Identity, bias=bias)
                return ins

            def row_start(b):
                act.wait_ge(xnT_ps.sem, xnT_ps.at(b, 1))
                act.activation(xnT[:, :], tr[:, :], ACT.Copy).then_inc(xnT_ready.sem, 1)
                yield
                act.wait_ge(key0_ps.sem, key0_ps.at(b, 1))
                act.activation(k_hl[:, 0, 0, NM:KEYS], sa[:, :], ACT.Copy).then_inc(key0_high.sem, 1)
                yield
                act.wait_ge(logit_ready.sem, logit_ready.at(b, 1))
                act.activation(pr[:, :, :], lg[:, :, :], ACT.Exp).then_inc(gexp_done.sem, 1)
                yield
                act.wait_ge(gatesT_ps.sem, gatesT_ps.at(b, 1))
                act.activation(gatesT[:, :], tr[0:E0 + 1, :], ACT.Copy).then_inc(gatesT_ready.sem, 1)
                yield
                act.wait_ge(facc_ps.sem, facc_ps.at(b, 1))
                act.activation(facc[:, :, :].rearrange("p t c -> p (t c)"), tr[:, :], ACT.Copy
                               ).then_inc(facc_ready.sem, 1)
                yield

            start = row_start(0)
            next(start)
            copied(r_all[:, :, :].rearrange("p a c -> p (a c)"), bank(2)[:, 0:2 * C], R_COPIED)
            next(start)
            next(start)
            for q, src in enumerate((mb[:, 0, :], mb[:, 1, :], bank(0), bank(1))):
                copied(w2f[:, 2 * q:2 * q + 2, :, :].rearrange("p e m c -> p (e m c)"), src, 4 + q, scale=0.5)
            copied(b2f[0:E0, :], bank(3)[0:E0, 0:C], SU_COPIES)
            next(start)
            next(start)
            with act.Fori(0, B) as b:
                def value_keys(it, k):
                    evacuate(b, it, f"keys{k}", k_hl[:, 0, k, NM:KEYS]).then_inc(key_high.sem, 1)

                def hidden1(it, m):
                    evacuate(b, it, f"h1_{m}", h1[:, m, :], b1c[:, bass.ds(it, 1), m]
                             ).then_inc(misc_free[MISCS.index(f"h1_{m}") % 2].sem, 1)

                def exps(it, u):
                    t, n = u % NT, it * UNITS + u + 1
                    src, w = score_slot(u, t)
                    act.wait_ge(nmax_ready.sem, nmax_ready.at(b, n))
                    act.activation(ex[:, u % 2, 0:w], src, ACT.Exp, bias=nmax[:, u % 2:u % 2 + 1]
                                   ).then_inc(exp_done.sem, 1)

                def values(it, k, first):
                    if not (first and k == 0):
                        act.wait_ge(av_done.sem, av_done.at(b, it * UNITS + (k - 1) * NT))
                    evacuate(b, it, f"values{k}", wv[:, :, k, :]
                             ).then_inc(misc_free[MISCS.index(f"values{k}") % 2].sem, 1)

                def turned(it, u):
                    t, n = u % NT, it * UNITS + u + 1
                    act.wait_ge(rden_ready.sem, rden_ready.at(b, n))
                    act.activation(attn_mem[:, t, bass.ds(2 * it + u // NT, 1), :],
                                   kept[:, u % 2:u % 2 + 1, 0:NM], ACT.Copy, scale=rden[:, u % 2:u % 2 + 1]
                                   ).then_inc(mem_kept.sem, 1)
                    act.wait_ge(tr_ready.sem, tr_ready.at(b, n))
                    act.wait_ge(av_done.sem, av_done.at(b, n - 2))
                    act.activation(attnT[:, u % 2, 0:P * (t + 1)], tr[:, 0:P * (t + 1)], ACT.Copy
                                   ).then_inc(attnT_ready.sem, 1)

                def tanhs(it, m):
                    act.wait_ge(*misc_left(b, it, f"h3_{m}"))
                    act.activation(ht[:, m, :], hu[:, m, :], ACT.Tanh, scale=0.5).then_inc(th_ready.sem, 1)

                def step(it, first=False):
                    if not first:
                        turned(it, -2)
                    value_keys(it, 1)
                    exps(it, 0)
                    values(it, 0, first)
                    if not first:
                        turned(it, -1)
                    exps(it, 1)
                    hidden1(it, 0)
                    turned(it, 0)
                    exps(it, 2)
                    turned(it, 1)
                    exps(it, 3)
                    tanhs(it, 0)
                    values(it, 1, first)
                    turned(it, 2)
                    exps(it, 4)
                    hidden1(it, 1)
                    turned(it, 3)
                    exps(it, 5)
                    tanhs(it, 1)
                    value_keys(it, 0)
                    turned(it, 4)
                    exps(it, 6)
                    turned(it, 5)
                    exps(it, 7)

                step(0, first=True)
                with act.Fori(1, NIT) as it:
                    step(it)
                def mem_turned(g):
                    act.wait_ge(memT_ps.sem, memT_ps.at(b, g + 1))
                    act.activation(memT[:, g, :], bank(g), ACT.Copy).then_inc(memT_ready.sem, 1)

                turned(NIT, -2)
                mem_turned(0)
                turned(NIT, -1)
                act.wait_ge(*misc_left(b, NIT - 1, "out1"))
                act.activation(sg[:, :, :], facc[:, :, :], ACT.Tanh, scale=0.5).then_inc(gate_tanh.sem, 1)
                mem_turned(1)
                act.wait_ge(xnT_ps.sem, xnT_ps.at(b, 2))
                act.activation(xnT[:, :], bank(0), ACT.Copy).then_inc(xnT_ready.sem, 1)
                act.wait_ge(logit_ready.sem, logit_ready.at(b, 2))
                act.activation(pr[:, :, :], lg[:, :, :], ACT.Exp).then_inc(gexp_done.sem, 1)
                act.wait_ge(xnT_ps.sem, xnT_ps.at(b, 3))
                act.activation(hT, bank(2), ACT.Copy).then_inc(xnT_ready.sem, 1)
                act.wait_ge(v_ps.sem, v_ps.at(b, 1))
                act.activation(vT, bank(3), ACT.Identity, bias=v_bias[:, 0:1]).then_inc(vT_ready.sem, 1)
                act.wait_ge(cmax_ready.sem, cmax_ready.at(b, 1))
                act.activation(cw[:, :], tr[:, 0:C], ACT.Exp, bias=cmax[:, 0:1], scale=float(1.0 / np.sqrt(T))
                               ).then_inc(cexp_done.sem, 1)
                act.wait_ge(cwT_ps.sem, cwT_ps.at(b, 1))
                act.activation(cwT[:, :], tr[:, 0:C], ACT.Copy).then_inc(cwT_ready.sem, 1)
                act.wait_ge(aT_ps.sem, aT_ps.at(b, 1))
                act.activation(aT, bank(2), ACT.Copy).then_inc(aT_ready.sem, 1)
                for half in range(2):
                    act.wait_ge(buf_ps.sem, buf_ps.at(b, half + 1))
                    act.activation(bufT[:, 4 * half:4 * half + 4, :].rearrange("p e s -> p (e s)"),
                                   bank(half)[:, 0:4 * CAP], ACT.Copy).then_inc(buf_ready.sem, 1)
                start = row_start(b + 1)
                for e in range(E1):
                    act.wait_ge(hid_ps.sem, hid_ps.at(b, e + 1))
                    for m in range(HM1):
                        ins = act.activation(hid[:, e % 2, m, :], bank(e % 2)[:, m * CAP:(m + 1) * CAP], ACT.Relu,
                                             bias=c1c[:, e, m:m + 1])
                    ins.then_inc(hid_ready.sem, 1)
                    act.wait_ge(back_ps.sem, back_ps.at(b, e + 1))
                    act.activation(backT[e], bank(2 + e % 2)[0:CAP, :], ACT.Copy).then_inc(back_ready.sem, 1)
                    if e in START_AT:
                        next(start)
                for half, z in enumerate((mb[:, 0, 0:2 * C], sa[:, 0:2 * C])):
                    act.wait_ge(comb_ps.sem, comb_ps.at(b, half + 1))
                    act.activation(sg[:, 2 * half:2 * half + 2, :].rearrange("p t c -> p (t c)"), z, ACT.Tanh, scale=0.5
                                   ).then_inc(gate_tanh.sem, 1)

        @block.vector
        def _(dve):
            for s in (chunk_read, fold_copied):
                dve.memset(den[:, 0:1], 0.0).then_inc(s.sem, s.preset)
                dve.drain()
            dve.wait_ge(loaded_m, 16 * N_M)
            dve.tensor_scalar(pre_col, pre_col, float(DH) ** -0.5, None, ALU.mult)
            dve.drain()

            def scale_chunks(first, src, col):
                with dve.Fori(0, 2) as i:
                    for j in range(2):
                        for c in range(HC):
                            dve.wait_ge(chunk_read.sem, (2 * HC) * i + ((first + j) * HC + c + 1))
                            dve.nop(nofuse=True)
                            dve.tensor_tensor(scaled[:, c, :, :], src[:, c, :].unsqueeze(1).to_broadcast([P, 4, C]),
                                              col[:, c, bass.ds(8 * i + 4 * j, 4)].unsqueeze(2).to_broadcast([P, 4, C]),
                                              ALU.mult).then_inc(chunk_ready, 1)

            scale_chunks(0, wqT, pre_col)
            dve.wait_ge(consts, 1)
            dve.wait_ge(loaded_n, 16 * N_N)
            dve.tensor_reduce(same_slot, ident[:, :].rearrange("p (h m) -> p m h", m=NM), AX.X, ALU.add)
            dve.drain()
            for g in range(2):
                ins = dve.scalar_tensor_tensor(out=pre_mix[:, g, :, :], in0=pre_row[:, g, :].unsqueeze(2).to_broadcast([P, H, NM]),
                                               scalar=float(DH) ** -0.5,
                                               in1=same_slot.unsqueeze(1).to_broadcast([P, H, NM]), op0=ALU.mult, op1=ALU.mult)
            ins.then_inc(mix_ready, 1)
            scale_chunks(4, wo_sb, post_col)

            def variance(src):
                for t in range(NT):
                    dve.bn_stats(stats[:, t, :], src[:, t, :])
                dve.drain()
                for t in range(NT):
                    dve.bn_aggr(mv[:, t, :], stats[:, t, :])
                dve.drain()
                dve.tensor_scalar(veps[:, :], mv[:, :, 1], EPS, None, ALU.add).then_inc(var_ready.sem, 1)

            def normed(b, n, src, dst):
                dve.wait_ge(rstd_ready.sem, rstd_ready.at(b, n))
                for t in range(NT):
                    ins = dve.tensor_scalar(dst[:, t, :], src[:, t, :], mv[:, t, 0:1], rstd[:, t:t + 1],
                                            ALU.subtract, ALU.mult)
                ins.then_inc(xn_ready.sem, 1)

            def softmax_top2(b, n, logits, bias, ties):
                dve.wait_ge(logit_ps.sem, logit_ps.at(b, n))
                if bias is None:
                    dve.tensor_copy(lg[:, :, :], logits)
                else:
                    dve.tensor_tensor(lg[:, :, :], logits, bias[:, :].unsqueeze(1).to_broadcast([P, NT, E0]), ALU.add)
                dve.drain()
                dve.tensor_reduce(red[:, :], lg[:, :, :], AX.X, ALU.max)
                dve.drain()
                dve.tensor_tensor(lg[:, :, :], lg[:, :, :], red[:, :].unsqueeze(2).to_broadcast([P, NT, E0]),
                                  ALU.subtract).then_inc(logit_ready.sem, 1)
                dve.wait_ge(gexp_done.sem, gexp_done.at(b, n))
                dve.tensor_reduce(red[:, :], pr[:, :, :], AX.X, ALU.add)
                dve.drain()
                dve.reciprocal(red[:, :], red[:, :])
                dve.drain()
                dve.tensor_tensor(pr[:, :, :], pr[:, :, :], red[:, :].unsqueeze(2).to_broadcast([P, NT, E0]), ALU.mult)
                dve.drain()
                other = pr[:, :, :].unsqueeze(2).to_broadcast([P, NT, E0, E0])
                own = pr[:, :, :].unsqueeze(3).to_broadcast([P, NT, E0, E0])
                dve.tensor_tensor(cmpa[:, :, :, :], other, own, ALU.is_gt)
                dve.tensor_tensor(cmpb[:, :, :, :], other, own, ALU.is_equal)
                dve.drain()
                dve.tensor_tensor(cmpb[:, :, :, :], cmpb[:, :, :, :],
                                  ties[:, :, :].unsqueeze(1).to_broadcast([P, NT, E0, E0]), ALU.mult)
                dve.drain()
                dve.tensor_tensor(cmpa[:, :, :, :], cmpa[:, :, :, :], cmpb[:, :, :, :], ALU.add)
                dve.drain()
                dve.tensor_reduce(rank[:, :, :], cmpa[:, :, :, :], AX.X, ALU.add)
                dve.drain()
                dve.tensor_scalar(rank[:, :, :], rank[:, :, :], 1.5, None, ALU.is_lt)
                dve.drain()

            def gate(g, z):
                return dve.scalar_tensor_tensor(out=g, in0=g, scalar=1.0, in1=z, op0=ALU.add, op1=ALU.mult)

            def gated(g, s, base, dst):
                dve.scalar_tensor_tensor(out=g, in0=g, scalar=0.5, in1=s, op0=ALU.mult, op1=ALU.mult)
                dve.drain()
                return dve.tensor_tensor(dst, g, base, ALU.add)

            def row_variance(b):
                dve.wait_ge(x_loaded.sem, x_loaded.at(b, 16))
                dve.tensor_copy(xb[:, :, :], x_next[:, :, :]).then_inc(x_taken.sem, 1)
                dve.drain()
                variance(xb)

            def row_gates(b):
                dve.wait_ge(xnT_ready.sem, xnT_ready.at(b, 1))
                dve.tensor_copy(x_hl[:, 0, :], xnT[:, :])
                dve.drain()
                dve.tensor_tensor(x_hl[:, 1, :], xnT[:, :], x_hl[:, 0, :], ALU.subtract).then_inc(xhl_ready.sem, 1)
                softmax_top2(b, 1, tr[:, 0:NT * E0].rearrange("p (t e) -> p t e", t=NT), bg_b, ties0)
                dve.tensor_tensor(gates[:, :, 0:E0], pr[:, :, :], rank[:, :, :], ALU.mult).then_inc(gates_ready.sem, 1)
                dve.wait_ge(key0_high.sem, key0_high.at(b, 1))
                dve.tensor_tensor(k_hl[:, 1, 0, NM:KEYS], sa[:, :], k_hl[:, 0, 0, NM:KEYS], ALU.subtract
                                  ).then_inc(key0_ready.sem, 1)

            row_variance(0)
            normed(0, 1, xb, xn)
            row_gates(0)
            dve.wait_ge(su_pe, SU_BIASES)
            dve.wait_ge(su_act, SU_COPIES)
            dve.tensor_tensor(qk_bias[:, :, :].rearrange("p a c -> p (a c)"), bank(2)[:, 0:2 * C],
                              qk_bias[:, :, :].rearrange("p a c -> p (a c)"), ALU.add)
            dve.tensor_tensor(v_bias[:, :], bank(2)[:, 2 * C:2 * C + 1], v_bias[:, :], ALU.add)
            dve.tensor_scalar(qkvT[:, :, :].rearrange("p a c -> p (a c)"), hT[:, 0:3 * C], norm_w_col[:, 0:1], None, ALU.mult)
            dve.tensor_copy(mt_all[:, NIT, :, :], mt_all[:, 0, :, :])
            dve.tensor_copy(g_all[:, NIT, :, :], g_all[:, 0, :, :])
            dve.drain()
            for s in (misc_free[0], misc_free[1], kept_ready, attn_ready, tr_ready, attnT_ready, av_done,
                      mem_kept, gate_read, stored):
                dve.memset(den[:, 0:1], 0.0).then_inc(s.sem, s.preset)
                dve.drain()
            dve.memset(den[:, 1:2], 0.0).then_inc(su_done, 1)

            with dve.Fori(0, B) as b:
                dve.wait_ge(facc_ready.sem, facc_ready.at(b, 1))
                dve.nop(nofuse=True)

                def top(it, u):
                    t, n = u % NT, it * UNITS + u + 1
                    src, w = score_slot(u, t)
                    dve.wait_ge(sc_ready.sem, sc_ready.at(b, n))
                    dve.nop(nofuse=True)
                    dve.max(top8[:, u % 2, :], src).then_inc(top_done.sem, 1)
                    dve.wait_ge(top_done.sem, top_done.at(b, n))
                    dve.tensor_scalar(nmax[:, u % 2:u % 2 + 1], top8[:, u % 2, 0:1], -1.0, None, ALU.mult
                                      ).then_inc(nmax_ready.sem, 1)

                def keep(it, u):
                    t, n = u % NT, it * UNITS + u + 1
                    src, w = score_slot(u, t)
                    dve.wait_ge(exp_done.sem, exp_done.at(b, n))
                    dve.wait_ge(attn_ready.sem, attn_ready.at(b, n - 2))
                    dve.wait_ge(mem_kept.sem, mem_kept.at(b, n - 2))
                    dve.scalar_tensor_tensor(out=kept[:, u % 2, 0:w], in0=src, scalar=top8[:, u % 2, 7:8],
                                             in1=ex[:, u % 2, 0:w], op0=ALU.is_ge, op1=ALU.mult,
                                             accum_out=den[:, u % 2:u % 2 + 1]).then_inc(kept_ready.sem, 1)
                    dve.wait_ge(kept_ready.sem, kept_ready.at(b, n))
                    dve.reciprocal(rden[:, u % 2:u % 2 + 1], den[:, u % 2:u % 2 + 1]).then_inc(rden_ready.sem, 1)

                def keys_low(it, k):
                    n = MISCS.index(f"keys{k}") % 2
                    dve.wait_ge(key_high.sem, key_high.at(b, it * 2 + 2 - k))
                    dve.nop(nofuse=True)
                    dve.tensor_tensor(k_hl[:, 1, k, NM:KEYS], mb[:, n, :], k_hl[:, 0, k, NM:KEYS], ALU.subtract
                                      ).then_inc(misc_free[n].sem, 1)

                def hidden3(it, m):
                    dve.wait_ge(*misc_done(b, it, f"h3_{m}"))
                    dve.wait_ge(*misc_left(b, it, f"h1_{m}"))
                    n = MISCS.index(f"h3_{m}") % 2
                    dve.scalar_tensor_tensor(out=hu[:, m, :], in0=mb[:, n, :], scalar=b3c[:, bass.ds(it, 1), m],
                                             in1=h1[:, m, :], op0=ALU.add, op1=ALU.mult
                                             ).then_inc(misc_free[n].sem, 1)

                def silu(it, m):
                    dve.wait_ge(th_ready.sem, th_ready.at(b, it * 2 + m + 1))
                    dve.scalar_tensor_tensor(out=hh[:, m, :], in0=ht[:, m, :], scalar=1.0, in1=hu[:, m, :],
                                             op0=ALU.add, op1=ALU.mult).then_inc(hh_ready.sem, 1)

                def experts_out(it, half):
                    dve.wait_ge(*misc_done(b, it, f"out{half}"))
                    n = MISCS.index(f"out{half}") % 2
                    for j in range(2):
                        t = 2 * half + j
                        ins = dve.scalar_tensor_tensor(
                            out=facc[:, t, :], in0=mb[:, n, j * C:(j + 1) * C], scalar=gates[:, t, bass.ds(it, 1)],
                            in1=facc[:, t, :], op0=ALU.mult, op1=ALU.add)
                    ins.then_inc(misc_free[n].sem, 1)

                def step(it):
                    top(it, 0)
                    keys_low(it, 1)
                    keep(it, 0)
                    top(it, 1)
                    keep(it, 1)
                    top(it, 2)
                    hidden3(it, 0)
                    keep(it, 2)
                    top(it, 3)
                    keep(it, 3)
                    top(it, 4)
                    silu(it, 0)
                    keep(it, 4)
                    top(it, 5)
                    hidden3(it, 1)
                    keep(it, 5)
                    silu(it, 1)
                    top(it, 6)
                    keys_low(it, 0)
                    keep(it, 6)
                    top(it, 7)
                    experts_out(it, 0)
                    experts_out(it, 1)
                    keep(it, 7)

                with dve.Fori(0, NIT) as it:
                    step(it)
                dve.wait_ge(gate_tanh.sem, gate_tanh.at(b, 1))
                gate(sg[:, :, :], facc[:, :, :])
                dve.drain()
                dve.wait_ge(s0_ready.sem, s0_ready.at(b, 1))
                gated(sg[:, :, :], sa[:, :].rearrange("p (t c) -> p t c", t=NT), xb[:, :, :], x1[:, :, :]
                      ).then_inc(x1_ready.sem, 1)
                dve.drain()
                variance(x1)
                normed(b, 2, x1, xn)
                dve.drain()
                variance(xn)
                normed(b, 3, xn, hn)
                softmax_top2(b, 2, bank(1)[:, 0:NT * E1].rearrange("p (t e) -> p t e", t=NT), None, ties1)
                dve.tensor_copy(chosen[:, :, :], rank[:, :, :]).then_inc(chosen_ready.sem, 1)
                dve.tensor_tensor(s1[:, :, :], xn[:, :, :], pb_b[:, :].unsqueeze(1).to_broadcast([P, NT, C]), ALU.add)
                dve.wait_ge(qk_ps.sem, qk_ps.at(b, 1))
                for j in range(2):
                    ins = dve.tensor_tensor(
                        qk[:, 2 * j:2 * j + 2, :, :].rearrange("p t a c -> p t (a c)"),
                        mb[:, j, :].rearrange("p (t n) -> p t n", t=2),
                        qk_bias[:, :, :].rearrange("p a c -> p (a c)").unsqueeze(1).to_broadcast([P, 2, 2 * C]), ALU.add)
                ins.then_inc(qk_ready.sem, 1)
                dve.wait_ge(pos_ps.sem, pos_ps.at(b, 1))
                dve.scalar_tensor_tensor(out=pos[:, :, :], in0=bank(1)[:, 64:64 + NT * E1].rearrange("p (t e) -> p t e", t=NT),
                                         scalar=1.0, in1=rank[:, :, :], op0=ALU.add, op1=ALU.mult)
                dve.drain()
                dve.tensor_scalar(pos[:, :, :], pos[:, :, :], -1.0, None, ALU.add)
                dve.drain()

                def one_hots(t):
                    dve.tensor_tensor(one_hot[:, t, :, :], slot_no[:, :].unsqueeze(1).to_broadcast([P, E1, CAP]),
                                      pos[:, t, :].unsqueeze(2).to_broadcast([P, E1, CAP]), ALU.is_equal
                                      ).then_inc(one_hot_ready.sem, 1)

                one_hots(0)
                dve.wait_ge(cw_ps.sem, cw_ps.at(b, 1))
                dve.tensor_reduce(cmax[:, :], tr[:, 0:C], AX.X, ALU.max)
                dve.drain()
                dve.tensor_scalar(cmax[:, :], cmax[:, :], float(-1.0 / np.sqrt(T)), None, ALU.mult
                                  ).then_inc(cmax_ready.sem, 1)
                one_hots(1)
                dve.wait_ge(cexp_done.sem, cexp_done.at(b, 1))
                dve.tensor_reduce(csum[:, :], cw[:, :], AX.X, ALU.add)
                dve.drain()
                dve.reciprocal(csum[:, :], csum[:, :])
                dve.drain()
                dve.tensor_scalar(cw[:, :], cw[:, :], csum[:, 0:1], None, ALU.mult).then_inc(cw_ready.sem, 1)
                one_hots(2)
                one_hots(3)
                row_variance(b + 1)
                dve.wait_ge(proj_ps.sem, proj_ps.at(b, 1))
                dve.tensor_tensor(s1[:, :, :].rearrange("p t c -> p (t c)"), bank(3),
                                  s1[:, :, :].rearrange("p t c -> p (t c)"), ALU.add).then_inc(s1_ready.sem, 1)
                dve.wait_ge(buf_ps.sem, buf_ps.at(b, 2))
                normed(b + 1, 1, xb, xn)
                dve.wait_ge(weighted_ready.sem, weighted_ready.at(b, 1))
                row_gates(b + 1)
                for half in range(2):
                    dve.wait_ge(y_ps.sem, y_ps.at(b, half + 1))
                    dve.tensor_tensor(y_slots[:, 4 * half:4 * half + 4, :].rearrange("p e c -> p (e c)"),
                                      mb[0:CAP, half, :],
                                      c2_b[:, 4 * half:4 * half + 4, :].rearrange("p e c -> p (e c)"), ALU.add
                                      ).then_inc(y_ready.sem, 1)
                dve.wait_ge(stored.sem, stored.at(b, 0))
                dve.nop(nofuse=True)
                for half, z in enumerate((mb[:, 0, 0:2 * C], sa[:, 0:2 * C])):
                    two = slice(2 * half, 2 * half + 2)
                    dve.wait_ge(gate_tanh.sem, gate_tanh.at(b, 2 + half))
                    gate(sg[:, two, :], z.rearrange("p (t c) -> p t c", t=2)).then_inc(gate_read.sem, 1)
                    dve.drain()
                    ins = gated(sg[:, two, :], s1[:, two, :], x1[:, two, :], y_out[:, two, :])
                ins.then_inc(out_ready.sem, 1)

        @block.tensor
        def _(pe):
            def folds(first, lhsT):
                with pe.Fori(0, 2) as i:
                    for j in range(2):
                        pe.wait_ge(fold_copied.sem, 2 * i + (first + j + 1))
                        for c in range(HC):
                            pe.wait_ge(chunk_ready, (2 * HC) * i + ((first + j) * HC + c + 1))
                            ins = pe.matmul(bank(j), lhsT[:, c, :], scaled[:, c, :, :].rearrange("p k n -> p (k n)"),
                                            start=(c == 0), stop=(c == HC - 1))
                            ins.then_inc(chunk_read.sem, 1)

            folds(0, wkT)
            pe.wait_ge(diag_ready, 1)
            for g in range(2):
                for j in range(4):
                    ins = pe.matmul(bank(2)[:, g * C:(g + 1) * C], mem_k_diag[:, g, j, :], wqT[:, 4 * g + j, :],
                                    start=(j == 0), stop=(j == 3))
            ins.then_inc(su_pe, 1)
            pe.wait_ge(mix_ready, 1)
            pe.wait_ge(su_act, 1)
            for g in range(2):
                ins = pe.matmul(bank(3)[:, 0:H * NM], mem_qk[:, g * C:(g + 1) * C],
                                pre_mix[:, g, :, :].rearrange("p k m -> p (k m)"), start=(g == 0), stop=(g == 1))
            ins.then_inc(su_pe, 1)
            folds(4, wvT)
            def turn(dst_bank, src):
                for t in range(NT):
                    ins = pe.transpose(dst_bank[:, t * P:(t + 1) * P], src[:, t, :], ident[:, :])
                return ins

            def row_start(b):
                pe.wait_ge(xn_ready.sem, xn_ready.at(b, 1))
                turn(tr, xn).then_inc(xnT_ps.sem, 1)
                yield
                pe.wait_ge(xnT_ready.sem, xnT_ready.at(b, 1))
                for t in range(NT):
                    ins = pe.matmul(tr[:, t * E0:(t + 1) * E0], xnT[:, t * P:(t + 1) * P], wg[:, :],
                                    start=True, stop=True)
                ins.then_inc(logit_ps.sem, 1)
                pe.wait_ge(mt_ready[0].sem, mt_ready[0].at(b, 0))
                pe.wait_ge(xhl_ready.sem, xhl_ready.at(b, 1))
                for i, (w, m) in enumerate(PARTS):
                    ins = pe.matmul(sa[:, :], m_hl[:, w, 0, :], x_hl[:, m, :], start=(i == 0), stop=(i == 2))
                ins.then_inc(key0_ps.sem, 1)
                yield
                pe.wait_ge(gates_ready.sem, gates_ready.at(b, 1))
                for t in range(NT):
                    ins = pe.transpose(tr[0:E0 + 1, t * P:(t + 1) * P], gates[:, t, :], ident[:, :])
                ins.then_inc(gatesT_ps.sem, 1)
                yield
                pe.wait_ge(gatesT_ready.sem, gatesT_ready.at(b, 1))
                for t in range(NT):
                    ins = pe.matmul(tr[:, t * C:(t + 1) * C], gatesT[:, t * P:(t + 1) * P], b2f[:, :],
                                    start=True, stop=True)
                ins.then_inc(facc_ps.sem, 1)
                yield

            start = row_start(0)
            next(start)
            pe.wait_ge(mem_scaled_ready, 1)
            for g in range(2):
                for c in range(HC):
                    ins = pe.matmul(bank(2)[:, g * C:(g + 1) * C], mem_scaled[c // 4][:, c % 4, g * P:(g + 1) * P],
                                    wo_sb[:, c, :], start=(c == 0), stop=(c == HC - 1))
            ins.then_inc(su_pe, 1)
            next(start)
            pe.wait_ge(fold_copied.sem, fold_copied.at(0, 8))
            pe.wait_ge(loaded_s, 16 * N_S)
            for q, dst in enumerate((mb[:, 0, :], mb[:, 1, :], bank(0), bank(1))):
                for j in range(4):
                    ins = pe.matmul(dst[:, j * C:(j + 1) * C], w2T[q // 2][:, 2 * (q % 2) + j // 2, j % 2, :], wf,
                                    start=True, stop=True)
                ins.then_inc(su_pe, 1)
            pe.wait_ge(su_act, G_COPIED)
            pe.matmul(bank(3)[0:E0, 0:C], b2T, wf, start=True, stop=True).then_inc(su_pe, 1)
            pe.wait_ge(su_act, R_COPIED)
            pe.matmul(bank(2)[:, 0:2 * C], norm_b_col[:, 0:1].to_broadcast([P, P]), hT[:, 0:2 * C], start=True, stop=True)
            pe.matmul(bank(2)[:, 2 * C:2 * C + 1], hT[:, 2 * C:3 * C], norm_b_col[:, 0:1], start=True, stop=True).then_inc(su_pe, 1)
            next(start)
            pe.wait_ge(su_act, SU_COPIES)
            next(start)
            pe.wait_ge(su_done, 1)
            with pe.Fori(0, B) as b:
                pe.wait_ge(key0_ready.sem, key0_ready.at(b, 1))
                pe.wait_ge(facc_ready.sem, facc_ready.at(b, 1))
                pe.wait_ge(gate_read.sem, gate_read.at(b, -1))
                pe.nop(nofuse=True)

                def misc(it, name, pieces):
                    n = MISCS.index(name)
                    pe.wait_ge(misc_free[n % 2].sem, misc_free[n % 2].at(b, it * (MISC // 2) + n // 2))
                    for at, width, lhsT, rhs, start, stop in pieces:
                        ins = pe.matmul(mb[:, n % 2, at:at + width], lhsT, rhs, start=start, stop=stop)
                    ins.then_inc(misc_ready.sem, 1)

                def value_keys(it, k):
                    misc(it, f"keys{k}", [(0, T, m_hl[:, w, k, :], x_hl[:, m, :], i == 0, i == 2)
                                          for i, (w, m) in enumerate(PARTS)])

                def values(it, k):
                    misc(it, f"values{k}", [(t * C, C, xnT[:, t * P:(t + 1) * P],
                                             n_all[:, bass.ds(it, 1), k, :].rearrange("p o c -> p (o c)"), True, True)
                                            for t in range(NT)])

                def hidden(it, side, m):
                    pe.wait_ge(w13_ready.sem, w13_ready.at(b, 4 * it + 2 * m + side - 3))
                    misc(it, ("h1_", "h3_")[side] + str(m),
                         [(0, T, w_hl[:, w, side, m * P:(m + 1) * P], x_hl[:, r, :], i == 0, i == 2)
                          for i, (w, r) in enumerate(PARTS)])

                def experts_out(it, half):
                    misc(it, f"out{half}",
                         [(j * C, C, hh[:, m, (2 * half + j) * P:(2 * half + j + 1) * P],
                           w2f[:, bass.ds(it, 1), m, :].rearrange("p o c -> p (o c)"), m == 0, m == 1)
                          for j in range(2) for m in range(2)])

                def scores(it, u):
                    t, n = u % NT, it * UNITS + u + 1
                    dst, w = score_slot(u, t)
                    k = u // NT
                    pe.wait_ge(kept_ready.sem, kept_ready.at(b, n - 2))
                    cut = w if w <= 512 else w - 256
                    for lo, hi in ((0, cut), (cut, w)):
                        if lo == hi:
                            continue
                        for i, (a, m) in enumerate(PARTS):
                            pe.matmul(dst[:, lo:hi], x_hl[:, a, t * P:(t + 1) * P], k_hl[:, m, k, lo:hi],
                                      start=(i == 0), stop=(i == 2 and hi < w), skip_group_check=True)
                    pe.matmul(dst[:, w - P:w], ident_h[:, :], causal[:, :], start=False, stop=True,
                              skip_group_check=True).then_inc(sc_ready.sem, 1)

                def turned(it, u):
                    t, n = u % NT, it * UNITS + u + 1
                    pe.wait_ge(attn_ready.sem, attn_ready.at(b, n))
                    pe.wait_ge(attnT_ready.sem, attnT_ready.at(b, n - 1))
                    for j in range(t + 1):
                        ins = pe.transpose(tr[:, j * P:(j + 1) * P], attn[:, u % 2, j * P:(j + 1) * P], ident[:, :])
                    ins.then_inc(tr_ready.sem, 1)

                def attend(it, u):
                    t, n = u % NT, it * UNITS + u + 1
                    pe.wait_ge(attnT_ready.sem, attnT_ready.at(b, n))
                    for j in range(t + 1):
                        ins = pe.matmul(sa[:, t * C:(t + 1) * C], attnT[:, u % 2, j * P:(j + 1) * P],
                                        wv[:, j, u // NT % 2, :], start=False, stop=False, skip_group_check=True)
                    ins.then_inc(av_done.sem, 1)

                def step(it, first=False):
                    pe.wait_ge(g_ready[0].sem, g_ready[0].at(b, it))
                    if not first:
                        pe.wait_ge(*misc_left(b, it - 1, "keys0"))
                    scores(it, 0)
                    if not first:
                        turned(it, -2)
                    pe.wait_ge(mt_ready[1].sem, mt_ready[1].at(b, it))
                    value_keys(it, 1)
                    if not first:
                        attend(it, -3)
                    values(it, 0)
                    scores(it, 1)
                    if first:
                        pe.wait_ge(gate_read.sem, gate_read.at(b, 0))
                        pe.nop(nofuse=True)
                        pe.matmul(sa[:, :], ones_row[:, :], bo_row[:, :, :].to_broadcast([1, NT, C]),
                                  start=True, stop=False, skip_group_check=True)
                    if not first:
                        turned(it, -1)
                    hidden(it, 0, 0)
                    if not first:
                        attend(it, -2)
                    scores(it, 2)
                    turned(it, 0)
                    hidden(it, 1, 0)
                    if not first:
                        attend(it, -1)
                    scores(it, 3)
                    turned(it, 1)
                    values(it, 1)
                    pe.wait_ge(*misc_left(b, it, "values0"))
                    attend(it, 0)
                    pe.wait_ge(g_ready[1].sem, g_ready[1].at(b, it + 1))
                    pe.wait_ge(*misc_left(b, it, "keys1"))
                    scores(it, 4)
                    turned(it, 2)
                    hidden(it, 0, 1)
                    attend(it, 1)
                    hidden(it, 1, 1)
                    scores(it, 5)
                    turned(it, 3)
                    pe.wait_ge(mt_ready[0].sem, mt_ready[0].at(b, it + 1))
                    value_keys(it, 0)
                    attend(it, 2)
                    scores(it, 6)
                    turned(it, 4)
                    attend(it, 3)
                    pe.wait_ge(hh_ready.sem, hh_ready.at(b, it * 2 + 2))
                    experts_out(it, 0)
                    scores(it, 7)
                    turned(it, 5)
                    experts_out(it, 1)
                    pe.wait_ge(*misc_left(b, it, "values1"))
                    attend(it, 4)

                step(0, first=True)
                with pe.Fori(1, NIT) as it:
                    step(it)

                def mem_turned(g):
                    for t in range(NT):
                        ins = pe.transpose(bank(g)[:, t * P:(t + 1) * P],
                                           attn_mem[:, t, 8 * g:8 * g + 8, :].rearrange("p h m -> p (h m)"), ident[:, :])
                    ins.then_inc(memT_ps.sem, 1)

                def mem_attend(g):
                    pe.wait_ge(memT_ready.sem, memT_ready.at(b, g + 1))
                    for t in range(NT):
                        ins = pe.matmul(sa[:, t * C:(t + 1) * C], memT[:, g, t * P:(t + 1) * P], r_all[:, g, :],
                                        start=False, stop=(g == 1), skip_group_check=True)
                    return ins

                attend(NIT, -3)
                turned(NIT, -2)
                pe.wait_ge(mem_kept.sem, mem_kept.at(b, NIT * UNITS // 2))
                mem_turned(0)
                attend(NIT, -2)
                turned(NIT, -1)
                mem_attend(0)
                attend(NIT, -1)
                pe.wait_ge(mem_kept.sem, mem_kept.at(b, NIT * UNITS))
                mem_turned(1)
                mem_attend(1).then_inc(s0_ready.sem, 1)
                pe.wait_ge(xn_ready.sem, xn_ready.at(b, 2))
                turn(bank(0), xn).then_inc(xnT_ps.sem, 1)
                pe.wait_ge(xnT_ready.sem, xnT_ready.at(b, 2))
                for t in range(NT):
                    ins = pe.matmul(bank(1)[:, t * E1:(t + 1) * E1], xnT[:, t * P:(t + 1) * P], wr[:, :],
                                    start=True, stop=True)
                ins.then_inc(logit_ps.sem, 1)
                pe.wait_ge(xn_ready.sem, xn_ready.at(b, 3))
                turn(bank(2), hn).then_inc(xnT_ps.sem, 1)
                pe.wait_ge(xnT_ready.sem, xnT_ready.at(b, 3))
                for t in range(NT):
                    ins = pe.matmul(mb[:, t // 2, (t % 2) * 2 * C:(t % 2 + 1) * 2 * C], hT[:, t * P:(t + 1) * P],
                                    qkvT[:, 0:2, :].rearrange("p a c -> p (a c)"), start=True, stop=True)
                ins.then_inc(qk_ps.sem, 1)
                pe.wait_ge(chosen_ready.sem, chosen_ready.at(b, 1))
                for t in range(NT):
                    for s in range(t + 1):
                        ins = pe.matmul(bank(1)[:, 64 + t * E1:64 + (t + 1) * E1], before[:, :] if s == t else ones_h[:, :],
                                        chosen[:, s, :], start=(s == 0), stop=(s == t))
                ins.then_inc(pos_ps.sem, 1)
                pe.matmul(bank(3), qkvT[:, 2, :], hT, start=True, stop=True).then_inc(v_ps.sem, 1)
                pe.wait_ge(qk_ready.sem, qk_ready.at(b, 1))
                for t in range(NT):
                    ins = pe.matmul(tr[:, 0:C], qk[:, t, 0, :], qk[:, t, 1, :], start=(t == 0), stop=(t == NT - 1))
                ins.then_inc(cw_ps.sem, 1)

                def gather(t):
                    pe.wait_ge(one_hot_ready.sem, one_hot_ready.at(b, t + 1))
                    for half in range(2):
                        ins = pe.matmul(bank(half)[:, 0:4 * CAP], xn[:, t, :],
                                        one_hot[:, t, 4 * half:4 * half + 4, :].rearrange("p e s -> p (e s)"),
                                        start=(t == 0), stop=(t == NT - 1))
                        if t == NT - 1:
                            ins.then_inc(buf_ps.sem, 1)

                gather(0)
                pe.wait_ge(cw_ready.sem, cw_ready.at(b, 1))
                pe.transpose(tr[:, 0:C], cw[:, :], ident[:, :]).then_inc(cwT_ps.sem, 1)
                gather(1)
                pe.wait_ge(cwT_ready.sem, cwT_ready.at(b, 1))
                pe.wait_ge(vT_ready.sem, vT_ready.at(b, 1))
                pe.matmul(bank(2), cwT[:, :], vT, start=True, stop=True).then_inc(aT_ps.sem, 1)
                gather(2)
                gather(3)
                pe.wait_ge(aT_ready.sem, aT_ready.at(b, 1))
                for t in range(NT):
                    ins = pe.matmul(bank(3)[:, t * C:(t + 1) * C], aT[:, t * P:(t + 1) * P], projT[:, :],
                                    start=True, stop=True)
                ins.then_inc(proj_ps.sem, 1)

                def expert_up(e):
                    if e < 2:
                        pe.wait_ge(buf_ready.sem, buf_ready.at(b, 2))
                    else:
                        pe.wait_ge(hid_ready.sem, hid_ready.at(b, e - 1))
                    for m in range(HM1):
                        ins = pe.matmul(bank(e % 2)[:, m * CAP:(m + 1) * CAP], v1_all[:, e, m * P:(m + 1) * P],
                                        bufT[:, e, :], start=True, stop=True)
                    ins.then_inc(hid_ps.sem, 1)

                def back(e):
                    if e == 0:
                        pe.wait_ge(weighted_ready.sem, weighted_ready.at(b, 1))
                        pe.wait_ge(s1_ready.sem, s1_ready.at(b, 1))
                    if e >= 2:
                        pe.wait_ge(back_ready.sem, back_ready.at(b, e - 1))
                    for t in range(NT):
                        ins = pe.transpose(bank(2 + e % 2)[0:CAP, t * P:(t + 1) * P], weighted[:, t, e, :], ident[:, :])
                    ins.then_inc(back_ps.sem, 1)

                def expert_down(e):
                    pe.wait_ge(hid_ready.sem, hid_ready.at(b, e + 1))
                    for m in range(HM1):
                        ins = pe.matmul(mb[0:CAP, e // 4, (e % 4) * C:(e % 4 + 1) * C], hid[:, e % 2, m, :],
                                        v2_all[:, e, m, :], start=(m == 0), stop=(m == HM1 - 1))
                    if e % 4 == 3:
                        ins.then_inc(y_ps.sem, 1)

                start = row_start(b + 1)
                pe.wait_ge(loaded_v, 16 * N_V)
                expert_up(0)
                back(0)
                for e in range(1, E1):
                    expert_up(e)
                    back(e)
                    expert_down(e - 1)
                    if e in PE_START_AT:
                        next(start)
                expert_down(E1 - 1)
                pe.wait_ge(key0_ready.sem, key0_ready.at(b + 1, 1))
                pe.wait_ge(back_ready.sem, back_ready.at(b, E1))
                for half in range(2):
                    pe.wait_ge(y_ready.sem, y_ready.at(b, half + 1))
                    for t in range(NT):
                        for e in range(4 * half, 4 * half + 4):
                            ins = pe.matmul((mb[:, 0, :], sa)[t // 2][:, t % 2 * C:(t % 2 + 1) * C],
                                            backT[e][:, t * P:(t + 1) * P], y_slots[:, e, :],
                                            start=(e == 0 and t % 2 == 0), stop=(e == E1 - 1), skip_group_check=True)
                        if half and t % 2:
                            ins.then_inc(comb_ps.sem, 1)


_INS = ["L0_attn_x", "L0_attn_Wq", "L0_attn_Wk", "L0_attn_Wv", "L0_attn_pre_proj", "L0_attn_post_proj",
        "L0_attn_mem_k", "L0_attn_mem_v", "L0_attn_Wo", "L0_attn_bo", "L0_ffn_W1", "L0_ffn_b1", "L0_ffn_W3",
        "L0_ffn_b3", "L0_ffn_W2", "L0_ffn_b2", "L0_ffn_Wg", "L0_ffn_bg", "L0_ffn_Wf", "L0_ffn_bf",
        "L1_attn_norm_w", "L1_attn_norm_b", "L1_attn_qkv_w", "L1_attn_qkv_b", "L1_attn_proj_w",
        "L1_attn_proj_b", "L1_ffn_Wr", "L1_ffn_W1", "L1_ffn_b1", "L1_ffn_W2", "L1_ffn_b2"]

_BY_CHUNK = ("L0_ffn_b1", "L0_ffn_b3", "L1_ffn_b1")
_ROWS_OF_HEADS = ("L0_attn_Wq", "L0_attn_Wk", "L0_attn_Wv")
_MEMORY = ("L0_attn_mem_k", "L0_attn_mem_v")
_TURNED = ("L0_attn_post_proj", "L0_ffn_b2", "L1_attn_qkv_w", "L1_attn_proj_w")


def kernel(**inputs):
    import concourse.bacc as bacc
    from concourse.bass_utils import run_bass_kernel_spmd

    nc = bacc.Bacc("TRN2", target_bir_lowering=False, num_devices=1)
    arrays, args = {}, []
    for name in _INS:
        a = np.asarray(inputs[name])
        if name in _BY_CHUNK:
            a = a.reshape(a.shape[0], -1, P).transpose(2, 0, 1)
        elif name in _ROWS_OF_HEADS:
            a = a.T.reshape(HC, P, C).transpose(1, 0, 2)
        elif name in _MEMORY:
            a = a.reshape(HC, 2, NM, DH).transpose(1, 3, 0, 2).reshape(P, HC, NM)
        elif name in _TURNED:
            a = a.T
        elif name == "L0_ffn_W2":
            a = a.transpose(2, 0, 1)
        a = np.ascontiguousarray(a)
        arrays[name] = a
        args.append(nc.dram_tensor(name, a.shape, mybir.dt.from_np(a.dtype), kind="ExternalInput").ap())
    args.append(nc.dram_tensor("out", (B, T, C), F32, kind="ExternalOutput").ap())
    build(nc, *args)
    r = run_bass_kernel_spmd(nc, [arrays], core_ids=[0])
    return r.results[0]["out"]
```
